# Optimizing a Trainium2 kernel written in Bass

```python
import numpy as np
import jax
import jax.numpy as jnp

def _softmax(x, axis=-1):
    return jax.nn.softmax(x, axis=axis)

def _gelu(x):
    return jax.nn.gelu(x, approximate=True)

def _silu(x):
    return jax.nn.silu(x)

def _sigmoid(x):
    return jax.nn.sigmoid(x)

def _layernorm(x, axis=-1, eps=1e-05):
    m = jnp.mean(x, axis=axis, keepdims=True)
    v = jnp.var(x, axis=axis, keepdims=True)
    return (x - m) / jnp.sqrt(v + eps)

def _scatter_add(tgt, idx, src, axis=0):
    return tgt.at[idx].add(src)

def _segment_sum(src, seg, n):
    return jax.ops.segment_sum(src, seg, n)
kernel_name = 'mk_adaln_d1_jaxref_r8_81eb31'

def setup_inputs(seed: int=0):
    np.random.seed(seed)
    _w = jnp.asarray

    def _L0_attn_setup():
        import jax, jax.numpy as jnp
        import numpy as np
        NUM_HEADS = 4
        CHUNK = 64
        GATE_NORM = 16.0
        EPS = 1e-05

        def _xavier(key, fan_in, fan_out):
            gain = 2.0 ** (-2.5)
            limit = gain * np.sqrt(6.0 / (fan_in + fan_out))
            return jax.random.uniform(key, (fan_in, fan_out), jnp.float32, -limit, limit)

        def _to_chunks(t, B, H, NC, C):
            d = t.shape[-1]
            return t.reshape(B, H, NC, C, d).transpose(2, 0, 1, 3, 4)

        def _gla_forward(x, Wq, Wk, Wv, Wg, gk_w1, gk_w2, gk_b2, g_norm_w, Wo):
            B, L, D = x.shape
            H = NUM_HEADS
            C = CHUNK
            NC = L // C
            q = x @ Wq
            k = x @ Wk
            v = x @ Wv
            gk = jax.nn.log_sigmoid(x @ gk_w1 @ gk_w2 + gk_b2) / GATE_NORM

            def split_heads(t):
                return t.reshape(B, L, H, -1).transpose(0, 2, 1, 3)
            q, k, v, gk = map(split_heads, (q, k, v, gk))
            dk = q.shape[-1]
            scale = dk ** (-0.5)
            qc = _to_chunks(q, B, H, NC, C)
            kc = _to_chunks(k, B, H, NC, C)
            vc = _to_chunks(v, B, H, NC, C)
            gc = _to_chunks(gk, B, H, NC, C)
            Bcum = jnp.cumsum(gc, axis=3)
            causal = jnp.tril(jnp.ones((C, C), jnp.float32))

            def step(Hst, inp):
                qi, ki, vi, bi = inp
                qg = qi * jnp.exp(bi) * scale
                kg = ki * jnp.exp(-bi)
                o_inter = jnp.einsum('bhcd,bhde->bhce', qg, Hst)
                A = jnp.einsum('bhtd,bhsd->bhts', qg, kg) * causal
                o_intra = jnp.einsum('bhts,bhse->bhte', A, vi)
                b_last = bi[:, :, -1:, :]
                kH = ki * jnp.exp(b_last - bi)
                H_new = jnp.exp(b_last).transpose(0, 1, 3, 2) * Hst + jnp.einsum('bhcd,bhce->bhde', kH, vi)
                return (H_new, o_inter + o_intra)
            dv = v.shape[-1]
            H0 = jnp.zeros((B, H, dk, dv), jnp.float32)
            _, oc = jax.lax.scan(step, H0, (qc, kc, vc, Bcum))
            o = oc.transpose(1, 2, 0, 3, 4).reshape(B, H, L, dv)
            o = o.transpose(0, 2, 1, 3)
            rms = jnp.sqrt(jnp.mean(o * o, axis=-1, keepdims=True) + EPS)
            o_n = o / rms * g_norm_w
            g = (x @ Wg).reshape(B, L, H, dv)
            o = o_n * g * jax.nn.sigmoid(g)
            return o.reshape(B, L, H * dv) @ Wo
        key = jax.random.key(seed)
        ks = jax.random.split(key, 8)
        B, L, D = (4, 256, 128)
        Dk, Dv, R = (128, 256, 16)
        x = jax.random.normal(ks[0], (B, L, D), jnp.float32)
        return {'x': x, 'Wq': _xavier(ks[1], D, Dk), 'Wk': _xavier(ks[2], D, Dk), 'Wv': _xavier(ks[3], D, Dv), 'Wg': _xavier(ks[4], D, Dv), 'gk_w1': _xavier(ks[5], D, R), 'gk_w2': _xavier(ks[6], R, Dk), 'gk_b2': jnp.zeros((Dk,), jnp.float32), 'g_norm_w': jnp.ones((Dv // NUM_HEADS,), jnp.float32), 'Wo': _xavier(ks[7], Dv, D)}
    _L0_attn_in = _L0_attn_setup()

    def _L0_ffn_setup():
        import jax, jax.numpy as jnp
        import numpy as np
        D_MODEL = 128
        N_HEADS = 16
        HEAD_DIM = D_MODEL // N_HEADS
        KV_LATENT = 64
        N_EXPERTS = 4
        D_HIDDEN = 4 * D_MODEL
        B, T = (2, 128)

        def rmsnorm(x, w, eps=1e-06):
            return w * (x * jax.lax.rsqrt(jnp.mean(x * x, axis=-1, keepdims=True) + eps))

        def layernorm(x, g, b, eps=1e-05):
            mu = jnp.mean(x, axis=-1, keepdims=True)
            var = jnp.mean((x - mu) ** 2, axis=-1, keepdims=True)
            return (x - mu) * jax.lax.rsqrt(var + eps) * g + b

        def apply_rope(x):
            t, d = (x.shape[2], x.shape[3])
            half = d // 2
            pos = jnp.arange(t, dtype=x.dtype)[:, None]
            inv_freq = 1.0 / 10000.0 ** (jnp.arange(half, dtype=x.dtype) / half)
            ang = pos * inv_freq[None, :]
            sin, cos = (jnp.sin(ang), jnp.cos(ang))
            x1, x2 = (x[..., :half], x[..., half:])
            return jnp.concatenate([x1 * cos - x2 * sin, x1 * sin + x2 * cos], axis=-1)

        def mla_attention(x, Wq, Wdkv, Wuk, Wuv, Wo, ln_g, ln_b):
            b, t, _ = x.shape
            q = (x @ Wq.T).reshape(b, t, N_HEADS, HEAD_DIM).transpose(0, 2, 1, 3)
            latent = layernorm(x @ Wdkv.T, ln_g, ln_b)
            k = (latent @ Wuk.T).reshape(b, t, N_HEADS, HEAD_DIM).transpose(0, 2, 1, 3)
            v = (latent @ Wuv.T).reshape(b, t, N_HEADS, HEAD_DIM).transpose(0, 2, 1, 3)
            q = apply_rope(q)
            k = apply_rope(k)
            scores = jnp.einsum('bhqd,bhkd->bhqk', q, k) / np.sqrt(HEAD_DIM)
            causal = jnp.tril(jnp.ones((t, t), dtype=bool))
            scores = jnp.where(causal, scores, -jnp.inf)
            attn = jax.nn.softmax(scores, axis=-1)
            out = jnp.einsum('bhqk,bhkd->bhqd', attn, v).transpose(0, 2, 1, 3).reshape(b, t, D_MODEL)
            return out @ Wo.T

        def moe(x, gate_w, gate_b, W1, b1, W2, b2):
            logits = x @ gate_w.T + gate_b
            top = jnp.argmax(logits, axis=-1)
            onehot = jax.nn.one_hot(top, N_EXPERTS, dtype=x.dtype)
            h = jax.nn.relu(jnp.einsum('btd,ehd->bteh', x, W1) + b1)
            y = jnp.einsum('bteh,edh->bted', h, W2) + b2
            return jnp.einsum('bted,bte->btd', y, onehot)
        key = jax.random.key(seed)
        ks = jax.random.split(key, 16)
        s = lambda fan_in: 1.0 / np.sqrt(fan_in)
        return {'x': jax.random.normal(ks[0], (B, T, D_MODEL), jnp.float32), 'norm1_w': jnp.ones((D_MODEL,), jnp.float32), 'norm2_w': jnp.ones((D_MODEL,), jnp.float32), 'Wq': jax.random.normal(ks[1], (D_MODEL, D_MODEL), jnp.float32) * s(D_MODEL), 'Wdkv': jax.random.normal(ks[2], (KV_LATENT, D_MODEL), jnp.float32) * s(D_MODEL), 'Wuk': jax.random.normal(ks[3], (D_MODEL, KV_LATENT), jnp.float32) * s(KV_LATENT), 'Wuv': jax.random.normal(ks[4], (D_MODEL, KV_LATENT), jnp.float32) * s(KV_LATENT), 'Wo': jax.random.normal(ks[5], (D_MODEL, D_MODEL), jnp.float32) * s(D_MODEL), 'ln_g': jnp.ones((KV_LATENT,), jnp.float32), 'ln_b': jnp.zeros((KV_LATENT,), jnp.float32), 'gate_w': jax.random.normal(ks[6], (N_EXPERTS, D_MODEL), jnp.float32) * s(D_MODEL), 'gate_b': jnp.zeros((N_EXPERTS,), jnp.float32), 'W1': jax.random.normal(ks[7], (N_EXPERTS, D_HIDDEN, D_MODEL), jnp.float32) * s(D_MODEL), 'b1': jnp.zeros((N_EXPERTS, D_HIDDEN), jnp.float32), 'W2': jax.random.normal(ks[8], (N_EXPERTS, D_MODEL, D_HIDDEN), jnp.float32) * s(D_HIDDEN), 'b2': jnp.zeros((N_EXPERTS, D_MODEL), jnp.float32)}
    _L0_ffn_in = _L0_ffn_setup()
    _L0_c = _w((lambda *s: np.random.randn(*s).astype(np.float32) * 0.05)(32, 128))
    _L0_wmod = _w((lambda *s: np.random.randn(*s).astype(np.float32) * 0.05)(128, 6 * 128) * 128 ** (-0.5))
    _d = {'L0_attn_x': _L0_attn_in['x'], 'L0_attn_Wq': _L0_attn_in['Wq'], 'L0_attn_Wk': _L0_attn_in['Wk'], 'L0_attn_Wv': _L0_attn_in['Wv'], 'L0_attn_Wg': _L0_attn_in['Wg'], 'L0_attn_gk_w1': _L0_attn_in['gk_w1'], 'L0_attn_gk_w2': _L0_attn_in['gk_w2'], 'L0_attn_gk_b2': _L0_attn_in['gk_b2'], 'L0_attn_g_norm_w': _L0_attn_in['g_norm_w'], 'L0_attn_Wo': _L0_attn_in['Wo'], 'L0_ffn_norm1_w': _L0_ffn_in['norm1_w'], 'L0_ffn_norm2_w': _L0_ffn_in['norm2_w'], 'L0_ffn_Wq': _L0_ffn_in['Wq'], 'L0_ffn_Wdkv': _L0_ffn_in['Wdkv'], 'L0_ffn_Wuk': _L0_ffn_in['Wuk'], 'L0_ffn_Wuv': _L0_ffn_in['Wuv'], 'L0_ffn_Wo': _L0_ffn_in['Wo'], 'L0_ffn_ln_g': _L0_ffn_in['ln_g'], 'L0_ffn_ln_b': _L0_ffn_in['ln_b'], 'L0_ffn_gate_w': _L0_ffn_in['gate_w'], 'L0_ffn_gate_b': _L0_ffn_in['gate_b'], 'L0_ffn_W1': _L0_ffn_in['W1'], 'L0_ffn_b1': _L0_ffn_in['b1'], 'L0_ffn_W2': _L0_ffn_in['W2'], 'L0_ffn_b2': _L0_ffn_in['b2'], 'L0_c': _L0_c, 'L0_wmod': _L0_wmod}
    _x0 = _d['L0_attn_x']
    _d['L0_attn_x'] = jax.random.normal(jax.random.fold_in(jax.random.key(seed), 1), (32, 256, 128), dtype=_x0.dtype)
    del _x0
    return _d

def reference(L0_attn_x, L0_attn_Wq, L0_attn_Wk, L0_attn_Wv, L0_attn_Wg, L0_attn_gk_w1, L0_attn_gk_w2, L0_attn_gk_b2, L0_attn_g_norm_w, L0_attn_Wo, L0_ffn_norm1_w, L0_ffn_norm2_w, L0_ffn_Wq, L0_ffn_Wdkv, L0_ffn_Wuk, L0_ffn_Wuv, L0_ffn_Wo, L0_ffn_ln_g, L0_ffn_ln_b, L0_ffn_gate_w, L0_ffn_gate_b, L0_ffn_W1, L0_ffn_b1, L0_ffn_W2, L0_ffn_b2, L0_c, L0_wmod):

    def _L0_attn_ref(x, Wq, Wk, Wv, Wg, gk_w1, gk_w2, gk_b2, g_norm_w, Wo):
        import jax, jax.numpy as jnp
        import numpy as np
        NUM_HEADS = 4
        CHUNK = 64
        GATE_NORM = 16.0
        EPS = 1e-05

        def _xavier(key, fan_in, fan_out):
            gain = 2.0 ** (-2.5)
            limit = gain * np.sqrt(6.0 / (fan_in + fan_out))
            return jax.random.uniform(key, (fan_in, fan_out), jnp.float32, -limit, limit)

        def _to_chunks(t, B, H, NC, C):
            d = t.shape[-1]
            return t.reshape(B, H, NC, C, d).transpose(2, 0, 1, 3, 4)

        def _gla_forward(x, Wq, Wk, Wv, Wg, gk_w1, gk_w2, gk_b2, g_norm_w, Wo):
            B, L, D = x.shape
            H = NUM_HEADS
            C = CHUNK
            NC = L // C
            q = x @ Wq
            k = x @ Wk
            v = x @ Wv
            gk = jax.nn.log_sigmoid(x @ gk_w1 @ gk_w2 + gk_b2) / GATE_NORM

            def split_heads(t):
                return t.reshape(B, L, H, -1).transpose(0, 2, 1, 3)
            q, k, v, gk = map(split_heads, (q, k, v, gk))
            dk = q.shape[-1]
            scale = dk ** (-0.5)
            qc = _to_chunks(q, B, H, NC, C)
            kc = _to_chunks(k, B, H, NC, C)
            vc = _to_chunks(v, B, H, NC, C)
            gc = _to_chunks(gk, B, H, NC, C)
            Bcum = jnp.cumsum(gc, axis=3)
            causal = jnp.tril(jnp.ones((C, C), jnp.float32))

            def step(Hst, inp):
                qi, ki, vi, bi = inp
                qg = qi * jnp.exp(bi) * scale
                kg = ki * jnp.exp(-bi)
                o_inter = jnp.einsum('bhcd,bhde->bhce', qg, Hst)
                A = jnp.einsum('bhtd,bhsd->bhts', qg, kg) * causal
                o_intra = jnp.einsum('bhts,bhse->bhte', A, vi)
                b_last = bi[:, :, -1:, :]
                kH = ki * jnp.exp(b_last - bi)
                H_new = jnp.exp(b_last).transpose(0, 1, 3, 2) * Hst + jnp.einsum('bhcd,bhce->bhde', kH, vi)
                return (H_new, o_inter + o_intra)
            dv = v.shape[-1]
            H0 = jnp.zeros((B, H, dk, dv), jnp.float32)
            _, oc = jax.lax.scan(step, H0, (qc, kc, vc, Bcum))
            o = oc.transpose(1, 2, 0, 3, 4).reshape(B, H, L, dv)
            o = o.transpose(0, 2, 1, 3)
            rms = jnp.sqrt(jnp.mean(o * o, axis=-1, keepdims=True) + EPS)
            o_n = o / rms * g_norm_w
            g = (x @ Wg).reshape(B, L, H, dv)
            o = o_n * g * jax.nn.sigmoid(g)
            return o.reshape(B, L, H * dv) @ Wo
        return _gla_forward(x, Wq, Wk, Wv, Wg, gk_w1, gk_w2, gk_b2, g_norm_w, Wo)

    def _L0_ffn_ref(x, norm1_w, norm2_w, Wq, Wdkv, Wuk, Wuv, Wo, ln_g, ln_b, gate_w, gate_b, W1, b1, W2, b2):
        import jax, jax.numpy as jnp
        import numpy as np
        D_MODEL = 128
        N_HEADS = 16
        HEAD_DIM = D_MODEL // N_HEADS
        KV_LATENT = 64
        N_EXPERTS = 4
        D_HIDDEN = 4 * D_MODEL
        B, T = (2, 128)

        def rmsnorm(x, w, eps=1e-06):
            return w * (x * jax.lax.rsqrt(jnp.mean(x * x, axis=-1, keepdims=True) + eps))

        def layernorm(x, g, b, eps=1e-05):
            mu = jnp.mean(x, axis=-1, keepdims=True)
            var = jnp.mean((x - mu) ** 2, axis=-1, keepdims=True)
            return (x - mu) * jax.lax.rsqrt(var + eps) * g + b

        def apply_rope(x):
            t, d = (x.shape[2], x.shape[3])
            half = d // 2
            pos = jnp.arange(t, dtype=x.dtype)[:, None]
            inv_freq = 1.0 / 10000.0 ** (jnp.arange(half, dtype=x.dtype) / half)
            ang = pos * inv_freq[None, :]
            sin, cos = (jnp.sin(ang), jnp.cos(ang))
            x1, x2 = (x[..., :half], x[..., half:])
            return jnp.concatenate([x1 * cos - x2 * sin, x1 * sin + x2 * cos], axis=-1)

        def mla_attention(x, Wq, Wdkv, Wuk, Wuv, Wo, ln_g, ln_b):
            b, t, _ = x.shape
            q = (x @ Wq.T).reshape(b, t, N_HEADS, HEAD_DIM).transpose(0, 2, 1, 3)
            latent = layernorm(x @ Wdkv.T, ln_g, ln_b)
            k = (latent @ Wuk.T).reshape(b, t, N_HEADS, HEAD_DIM).transpose(0, 2, 1, 3)
            v = (latent @ Wuv.T).reshape(b, t, N_HEADS, HEAD_DIM).transpose(0, 2, 1, 3)
            q = apply_rope(q)
            k = apply_rope(k)
            scores = jnp.einsum('bhqd,bhkd->bhqk', q, k) / np.sqrt(HEAD_DIM)
            causal = jnp.tril(jnp.ones((t, t), dtype=bool))
            scores = jnp.where(causal, scores, -jnp.inf)
            attn = jax.nn.softmax(scores, axis=-1)
            out = jnp.einsum('bhqk,bhkd->bhqd', attn, v).transpose(0, 2, 1, 3).reshape(b, t, D_MODEL)
            return out @ Wo.T

        def moe(x, gate_w, gate_b, W1, b1, W2, b2):
            logits = x @ gate_w.T + gate_b
            top = jnp.argmax(logits, axis=-1)
            onehot = jax.nn.one_hot(top, N_EXPERTS, dtype=x.dtype)
            h = jax.nn.relu(jnp.einsum('btd,ehd->bteh', x, W1) + b1)
            y = jnp.einsum('bteh,edh->bted', h, W2) + b2
            return jnp.einsum('bted,bte->btd', y, onehot)
        x = x + mla_attention(rmsnorm(x, norm1_w), Wq, Wdkv, Wuk, Wuv, Wo, ln_g, ln_b)
        x = x + moe(rmsnorm(x, norm2_w), gate_w, gate_b, W1, b1, W2, b2)
        return x
    x = L0_attn_x
    mod = (_silu(L0_c) @ L0_wmod).reshape(L0_c.shape[0], 6, 1, -1)
    sa, ca, ga, sb, cb, gb = (mod[:, 0], mod[:, 1], mod[:, 2], mod[:, 3], mod[:, 4], mod[:, 5])
    ga = (2 * (ga >= 0) - 1) * jnp.maximum(jnp.abs(ga), 0.25)
    gb = (2 * (gb >= 0) - 1) * jnp.maximum(jnp.abs(gb), 0.25)
    h = _layernorm(x, axis=-1) * (1 + ca) + sa
    x = x + ga * _L0_attn_ref(h, L0_attn_Wq, L0_attn_Wk, L0_attn_Wv, L0_attn_Wg, L0_attn_gk_w1, L0_attn_gk_w2, L0_attn_gk_b2, L0_attn_g_norm_w, L0_attn_Wo)
    h = _layernorm(x, axis=-1) * (1 + cb) + sb
    x = x + gb * _L0_ffn_ref(h, L0_ffn_norm1_w, L0_ffn_norm2_w, L0_ffn_Wq, L0_ffn_Wdkv, L0_ffn_Wuk, L0_ffn_Wuv, L0_ffn_Wo, L0_ffn_ln_g, L0_ffn_ln_b, L0_ffn_gate_w, L0_ffn_gate_b, L0_ffn_W1, L0_ffn_b1, L0_ffn_W2, L0_ffn_b2)
    return x

_drawn_inputs = setup_inputs


def setup_inputs(seed=0):
    import zlib

    import numpy as np

    out = dict(_drawn_inputs(seed))
    spreads = {'L0_attn_gk_b2': (0.0, 0.8),
     'L0_attn_g_norm_w': (1.0, 0.6),
     'L0_ffn_norm1_w': (1.0, 0.2),
     'L0_ffn_norm2_w': (1.0, 0.2),
     'L0_ffn_ln_g': (1.0, 0.2),
     'L0_ffn_ln_b': (0.0, 0.1),
     'L0_ffn_gate_b': (0.0, 0.1),
     'L0_ffn_b1': (0.0, 0.487),
     'L0_ffn_b2': (0.0, 0.351)}
    factors = {'L0_attn_Wq': 6.52,
     'L0_attn_Wk': 6.079,
     'L0_attn_Wv': 6.638,
     'L0_attn_Wg': 5.908,
     'L0_attn_gk_w1': 8.0,
     'L0_attn_gk_w2': 8.0,
     'L0_attn_Wo': 5.605}
    for name, (base, spread) in spreads.items():
        noise = np.random.default_rng([zlib.crc32(name.encode()), seed]).standard_normal(out[name].shape)
        drawn = base * np.exp(spread * noise) if base else spread * noise
        out[name] = jnp.asarray(drawn.astype(out[name].dtype))
    for name, factor in factors.items():
        out[name] = (out[name] * factor).astype(out[name].dtype)
    return out
```

```python
from contextlib import ExitStack

import numpy as np

import concourse.bass as bass
from concourse import mybir

F32 = mybir.dt.float32
BF16 = mybir.dt.bfloat16
ALU = mybir.AluOpType
ACT = mybir.ActivationFunctionType
AX = mybir.AxisListType

P = 128
D = 128
B = 32
T = 256
TB = T // P
EPS = 1e-5
EPS_RMS = 1e-6

GH, GK, GV, CH = 4, 32, 64, 64
DV = GH * GV
UB = 2
UT = UB * TB
UN = UB * T
UNITS = B // UB
NCH = T // CH
GATE_NORM = 16.0

MH, MD = 16, 8
LAT = 64
KROWS = 6 * MD
MROWS = 3

NE, HID = 4, 512
HT = HID // P


def shape_constants():
    half = MD // 2
    pos = np.arange(T, dtype=np.float32)
    freq = (np.float32(1.0) / np.float32(10000.0) ** (np.arange(half, dtype=np.float32) / np.float32(half))).astype(np.float32)
    ang = (pos[None, :] * freq[:, None]).astype(np.float32)
    cos, sin = np.cos(ang).astype(np.float32), np.sin(ang).astype(np.float32)
    rope_cos = np.repeat(np.concatenate([cos, cos]), MH, axis=0)
    rope_sin = np.repeat(np.concatenate([-sin, sin]), MH, axis=0)
    ident = np.eye(P, dtype=np.float32)
    s, t = np.arange(P)[:, None], np.arange(P)[None, :]
    chunk_causal = ((s <= t) & (s // CH == t // CH)).astype(np.float32)
    above = np.where(t > s, -1e30, 0.0).astype(np.float32)
    scan_keep = np.tile((np.arange(UN) % CH != 0).astype(np.float32), (P, 1))
    head_of_row = (np.arange(P)[:, None] // GK == np.arange(GH)[None, :]).astype(np.float32)
    off = np.eye(NE, dtype=np.float32) * np.float32(1e30)
    first_of_four = np.tile((np.arange(TB * NE) % NE != 0).astype(np.float32), (P, 1))
    return {"rope_cos": rope_cos, "rope_sin": rope_sin, "ident": ident, "chunk_causal": chunk_causal,
            "above": above, "scan_keep": scan_keep, "head_of_row": head_of_row, "first_of_four": first_of_four,
            "off": off}


def linear_attention(nc, a, x_res, ident, mhalf, rowmod_dram, consts_in, n_const):
    with ExitStack() as ctx:
        def sb(name, shape, dt=F32):
            return ctx.enter_context(nc.sbuf_tensor(name, shape, dt))

        def sem(name):
            return ctx.enter_context(nc.semaphore(name))

        chunk_causal = sb("chunk_causal_sb", [P, P])
        scan_keep = sb("scan_keep_sb", [P, UN])
        head_of_row = sb("head_of_row_sb", [P, GH])
        wq = sb("wq", [D, P])
        wk = sb("wk", [D, P])
        wvg = sb("wvg", [D, 2 * DV])
        w1t = sb("w1t", [16, D])
        w2 = sb("w2", [16, P])
        w12 = sb("w12", [D, P])
        gk_b = sb("gk_b", [P, 1])
        wo = sb("wo", [P, 2, D])
        gnorm = sb("gnorm", [P, 1])
        cT = sb("cT", [D, B])
        cth = sb("cth", [D, B])
        csil = sb("csil", [D, B])
        wmod = sb("wmod", [D, 6 * D])
        shiftT = sb("shiftT", [D, B])
        scaleT = sb("scaleT", [D, B])
        rowmod = sb("rowmod", [B, 4, D])
        sgn = sb("sgn", [B, 2, D])

        ln1_st = sb("ln1_st", [P, UT, 6])
        ln1_mv = sb("ln1_mv", [P, UT, 2])
        ln1_ve = sb("ln1_ve", [P, UT])
        ln1_rs = sb("ln1_rs", [P, UT])
        xn = sb("xn", [P, UT, D])
        hT = sb("hT", [D, UN])
        g_a = sb("g_a", [P, UN])
        g_e = sb("g_e", [P, UN])
        g_l = sb("g_l", [P, UN])
        g_m = sb("g_m", [P, UN])
        g_g = sb("g_g", [P, UN])
        g_cum = sb("g_cum", [P, UN])
        eb = sb("eb", [P, UN])
        enb = sb("enb", [P, UN])
        qg = sb("qg", [P, UN])
        kg = sb("kg", [P, UN])
        kH = sb("kH", [P, UN])
        kHt = sb("kHt", [P, UT, P])
        v_sb = sb("v_sb", [P, UT, DV])
        tg = sb("tg", [P, UT, DV])
        sg = sb("sg", [P, UT, DV])
        att = sb("att", [P, GH, UN])
        state = sb("state", [P, UB, NCH - 1, GV])
        state_bd = sb("state_bd", [P, UB * (NCH - 1), GH, GV])
        sq = sb("sq", [P, UT * GH, GV])
        og = sb("og", [P, UT * GH, GV])
        og2 = sb("og2", [P, UT * GH, GV])
        ss = sb("ss", [P, UT * GH])
        ss_e = sb("ss_e", [P, UT * GH])
        rrms = sb("rrms", [P, UT * GH])
        oT = sb("oT", [P, UT, 2, P])
        ga_bc = sb("ga_bc", [P, UB, D])
        yg = sb("yg", [P, UB, TB, D])

        PS = ctx.enter_context(nc.psum_tensor("PS", [P, 8, 512], F32))

        x_head_in = sem("x_head_in")
        x_rest_in = sem("x_rest_in")
        tanh_c = sem("tanh_c")
        silu_c = sem("silu_c")
        setup_mm = sem("setup_mm")
        setup_v = sem("setup_v")
        setup_v2 = sem("setup_v2")
        mhalf_set = sem("mhalf_set")
        rowmod_out = sem("rowmod_out")
        own_step = sem("own_step")
        ga_in = sem("ga_in")
        S = {n: sem(n) for n in (
            "ln1_stats", "ln1_mean", "ln1_eps", "ln1_rstd", "xn_ready", "xnT_ready", "hT_ready", "z_ready",
            "g_abs", "g_exp", "g_ln", "g_min", "g_ready", "cum_ready", "eb_ready", "enb_ready",
            "q_ready", "k_ready", "vg_ready", "v_ready", "tanh_ready", "sg_ready", "qg_ready", "kg_ready",
            "kH_ready", "kHT_ready", "kHt_ready", "A_ready", "att_ready", "U_ready", "H_step", "H_ready", "bd_ready",
            "o_ready", "sq_ready", "og_ready", "ss_ready", "ss_eps", "rrms_ready", "og2_ready", "oTp_ready",
            "oT_ready", "y_ready", "yg_ready", "x1_ready")}
        PER = {"ln1_stats": UT, "ln1_mean": UT, "xn_ready": UT, "hT_ready": UB, "vg_ready": UT, "A_ready": GH,
               "att_ready": GH, "H_step": 3}

        def wait(eng, name, n, k=None):
            per = PER.get(name, 1)
            k = per if k is None else k
            if isinstance(n, int) and n * per + k <= 0:
                return
            eng.wait_ge(S[name], n * per + k)

        def apart(eng):
            eng.sem_inc(own_step, 1)

        block = ctx.enter_context(nc.Block())

        CONST_LOADS = [
            (ident, "ident"), (chunk_causal, "chunk_causal"), (scan_keep, "scan_keep"), (head_of_row, "head_of_row"),
            (wq, "wq"), (wk, "wk"), (wvg, "wvg"), (w1t, "w1t"), (w2, "w2"), (gk_b, "gk_b"), (gnorm, "gnorm"),
            (cT, "cT"), (wmod, "wmod")]
        N_CONST = 16 * (len(CONST_LOADS) + 1)

        x_tiles = a["x"].rearrange("b (t p) d -> p (b t) d", p=P)

        @block.sync
        def _(sp):
            for dst, name in CONST_LOADS:
                sp.dma_start(dst[:, :], a[name]).then_inc(consts_in, 16)
            sp.dma_start(wo[:, :, :], a["wo"].rearrange("(e p) n -> p e n", p=P)).then_inc(consts_in, 16)
            sp.dma_start(x_res[:, 0:2 * UT, :], x_tiles[:, 0:2 * UT, :]).then_inc(x_head_in, 16)
            sp.dma_start(x_res[:, 2 * UT:, :], x_tiles[:, 2 * UT:, :]).then_inc(x_rest_in, 16)
            sp.wait_ge(setup_v2, 4)
            sp.dma_start(rowmod_dram, rowmod[:, :, :]).then_inc(rowmod_out, 16)
            sp.wait_ge(rowmod_out, 16)

            def load_ga(u):
                wait(sp, "yg_ready", u - 1)
                sp.dma_start(ga_bc[:, :, :], rowmod_dram[bass.ts(u, UB), 0:1, :].rearrange("b o d -> o b d")
                             .broadcast_to([P, UB, D])).then_inc(ga_in, 16)
            load_ga(0)
            with sp.Fori(1, UNITS) as u:
                load_ga(u)

        @block.gpsimd
        def _(pool):
            pool.memset(mhalf[:, :], -0.5).then_inc(mhalf_set, 1)
            pool.wait_ge(mhalf_set, 1)

            def ln1_rstd(u):
                wait(pool, "ln1_mean", u)
                apart(pool)
                pool.tensor_scalar(ln1_ve[:, :], ln1_mv[:, :, 1], EPS, None, ALU.add).then_inc(S["ln1_eps"], 1)
                wait(pool, "ln1_eps", u)
                wait(pool, "xn_ready", u - 1)
                pool.tensor_tensor(ln1_rs[:, :], ln1_ve[:, :], mhalf[:, 0:UT], ALU.pow).then_inc(S["ln1_rstd"], 1)

            def body(u, last=False):
                if not last:
                    ln1_rstd(u + 1)
                wait(pool, "ss_ready", u)
                apart(pool)
                pool.tensor_scalar(ss_e[:, :], ss[:, :], 1.0 / GV, EPS, ALU.mult, ALU.add).then_inc(S["ss_eps"], 1)
                wait(pool, "ss_eps", u)
                wait(pool, "og2_ready", u - 1)
                pool.tensor_tensor(rrms[:, :], ss_e[:, :], mhalf[:, :], ALU.pow).then_inc(S["rrms_ready"], 1)
                wait(pool, "yg_ready", u)
                xs = x_res[:, bass.ts(u, UT), :].rearrange("p (b t) d -> p b t d", b=UB)
                pool.tensor_tensor(xs, xs, yg[:, :, :, :], ALU.add).then_inc(S["x1_ready"], 1)

            ln1_rstd(0)
            body(0)
            with pool.Fori(1, UNITS - 1) as u:
                body(u)
            body(UNITS - 1, last=True)

        @block.scalar
        def _(act):
            act.wait_ge(consts_in, N_CONST)
            act.activation(cth[:, :], cT[:, :], ACT.Tanh, scale=0.5).then_inc(tanh_c, 1)

            def modulate(u):
                wait(act, "xnT_ready", u)
                wait(act, "vg_ready", u - 1)
                for i in range(UB):
                    b = u * UB + i
                    act.activation(hT[:, i * T:(i + 1) * T], PS[:, 0, i * T:(i + 1) * T], ACT.Identity,
                                   scale=scaleT[:, bass.ds(b, 1)], bias=shiftT[:, bass.ds(b, 1)]).then_inc(S["hT_ready"], 1)

            def gate_logs(u):
                wait(act, "z_ready", u)
                wait(act, "g_ready", u - 1)
                act.activation(g_a[:, :], PS[:, 1, :], ACT.Abs, bias=gk_b[:, 0:1]).then_inc(S["g_abs"], 1)
                wait(act, "g_abs", u)
                act.activation(g_e[:, :], g_a[:, :], ACT.Exp, scale=-1.0).then_inc(S["g_exp"], 1)
                wait(act, "g_exp", u)
                act.activation(g_l[:, :], g_e[:, :], ACT.Ln, bias=1.0).then_inc(S["g_ln"], 1)

            def decays(u):
                wait(act, "cum_ready", u)
                wait(act, "bd_ready", u - 1)
                wait(act, "kH_ready", u - 1)
                act.activation(eb[:, :], g_cum[:, :], ACT.Exp, scale=1.0 / GATE_NORM).then_inc(S["eb_ready"], 1)
                act.activation(enb[:, :], g_cum[:, :], ACT.Exp, scale=-1.0 / GATE_NORM).then_inc(S["enb_ready"], 1)

            def body(u, last=False):
                decays(u)
                wait(act, "vg_ready", u)
                wait(act, "o_ready", u - 1)
                act.activation(v_sb[:, :, :], PS[:, 4:8, 0:DV], ACT.Copy).then_inc(S["v_ready"], 1)
                wait(act, "sg_ready", u - 1)
                act.activation(tg[:, :, :], PS[:, 4:8, DV:2 * DV], ACT.Tanh, scale=0.5).then_inc(S["tanh_ready"], 1)
                if not last:
                    modulate(u + 1)
                wait(act, "kHT_ready", u)
                act.activation(kHt[:, :, :], PS[:, 2, :].rearrange("p (j c) -> p j c", j=UT), ACT.Copy)\
                   .then_inc(S["kHt_ready"], 1)
                if not last:
                    gate_logs(u + 1)
                wait(act, "o_ready", u)
                wait(act, "ss_ready", u - 1)
                act.activation(sq[:, :, :], PS[:, 4:6, :].rearrange("p k (h v) -> p (k h) v", v=GV), ACT.Square)\
                   .then_inc(S["sq_ready"], 1)
                wait(act, "oTp_ready", u)
                wait(act, "y_ready", u - 1)
                act.activation(oT[:, :, :, :].rearrange("p j e t -> p (j e t)"),
                               PS[:, 6:8, :].rearrange("p k n -> p (k n)"), ACT.Copy).then_inc(S["oT_ready"], 1)

            act.wait_ge(setup_v, 2)
            modulate(0)
            gate_logs(0)
            body(0)
            with act.Fori(1, UNITS - 1) as u:
                body(u)
            body(UNITS - 1, last=True)

        @block.vector
        def _(dve):
            dve.wait_ge(tanh_c, 1)
            dve.scalar_tensor_tensor(out=cth[:, :], in0=cth[:, :], scalar=1.0, in1=cT[:, :], op0=ALU.add, op1=ALU.mult)\
               .then_inc(silu_c, 1)
            dve.wait_ge(silu_c, 1)
            dve.tensor_scalar(csil[:, :], cth[:, :], 0.5, None, ALU.mult).then_inc(silu_c, 1)
            dve.wait_ge(setup_mm, 3)
            dve.tensor_copy(shiftT[:, :], PS[:, 0, 0:B]).then_inc(setup_v, 1)
            dve.tensor_scalar(scaleT[:, :], PS[:, 0, B:2 * B], 1.0, None, ALU.add).then_inc(setup_v, 1)
            dve.tensor_copy(w12[:, :], PS[:, 2, 0:P]).then_inc(setup_v, 1)
            rows = PS[0:B, 1, :].rearrange("b (k d) -> b k d", k=4)
            dve.tensor_copy(rowmod[:, 1, :], rows[:, 1, :]).then_inc(setup_v2, 1)
            dve.tensor_scalar(rowmod[:, 2, :], rows[:, 2, :], 1.0, None, ALU.add).then_inc(setup_v2, 1)
            for i, k in enumerate((0, 3)):
                dve.tensor_scalar(sgn[:, i, :], rows[:, k, :], 0.0, 2.0, ALU.is_ge, ALU.mult).then_inc(setup_v, 1)
                dve.tensor_scalar(rowmod[:, k, :], rows[:, k, :], -1.0, 0.25, ALU.mult, ALU.max).then_inc(setup_v, 1)
                dve.wait_ge(setup_v, 3 + 3 * i + 2)
                dve.tensor_tensor(rowmod[:, k, :], rows[:, k, :], rowmod[:, k, :], ALU.max).then_inc(setup_v, 1)
                dve.wait_ge(setup_v, 3 + 3 * i + 3)
                dve.scalar_tensor_tensor(out=rowmod[:, k, :], in0=sgn[:, i, :], scalar=-1.0, in1=rowmod[:, k, :],
                                         op0=ALU.add, op1=ALU.mult).then_inc(setup_v2, 1)
            dve.tensor_scalar(wo[:, :, :], wo[:, :, :], gnorm[:, 0:1], 0.5, ALU.mult, ALU.mult).then_inc(setup_v, 1)

            def ln1_stats(u):
                wait(dve, "xn_ready", u - 1)
                for j in range(UT):
                    dve.bn_stats(ln1_st[:, j, :], x_res[:, bass.ds(u * UT + j, 1), :].rearrange("p o d -> p (o d)"))\
                       .then_inc(S["ln1_stats"], 1)
                for j in range(UT):
                    wait(dve, "ln1_stats", u, j + 1)
                    apart(dve)
                    dve.bn_aggr(ln1_mv[:, j, :], ln1_st[:, j, :]).then_inc(S["ln1_mean"], 1)

            def ln1_apply(u):
                wait(dve, "ln1_rstd", u)
                wait(dve, "xnT_ready", u - 1)
                for j in range(UT):
                    dve.tensor_scalar(xn[:, j, :], x_res[:, bass.ds(u * UT + j, 1), :].rearrange("p o d -> p (o d)"),
                                      ln1_mv[:, j, 0:1], ln1_rs[:, j:j + 1], ALU.subtract, ALU.mult)\
                       .then_inc(S["xn_ready"], 1)

            def gate_min(u):
                wait(dve, "g_abs", u)
                dve.tensor_scalar(g_m[:, :], PS[:, 1, :], gk_b[:, 0:1], 0.0, ALU.add, ALU.min).then_inc(S["g_min"], 1)

            def gate_cumsum(u):
                wait(dve, "g_ln", u)
                wait(dve, "g_min", u)
                wait(dve, "cum_ready", u - 1)
                dve.tensor_tensor(g_g[:, :], g_m[:, :], g_l[:, :], ALU.subtract).then_inc(S["g_ready"], 1)
                wait(dve, "g_ready", u)
                wait(dve, "enb_ready", u - 1)
                wait(dve, "eb_ready", u - 1)
                dve.tensor_tensor_scan(g_cum[:, :], scan_keep[:, :], g_g[:, :], 0.0, ALU.mult, ALU.add)\
                   .then_inc(S["cum_ready"], 1)

            def body(u, last=False):
                if not last:
                    ln1_stats(u + 1)
                wait(dve, "q_ready", u)
                wait(dve, "eb_ready", u)
                wait(dve, "o_ready", u - 1)
                dve.scalar_tensor_tensor(out=qg[:, :], in0=PS[:, 2, :], scalar=float(GK) ** -0.5, in1=eb[:, :],
                                         op0=ALU.mult, op1=ALU.mult).then_inc(S["qg_ready"], 1)
                wait(dve, "k_ready", u)
                wait(dve, "enb_ready", u)
                dve.tensor_tensor(kg[:, :], PS[:, 3, :], enb[:, :], ALU.mult).then_inc(S["kg_ready"], 1)
                wait(dve, "kg_ready", u)
                wait(dve, "kHT_ready", u - 1)
                ebl = eb[:, CH - 1:UN:CH].unsqueeze(2).broadcast_to([P, UN // CH, CH])
                dve.tensor_tensor(kH[:, :].rearrange("p (c s) -> p c s", s=CH),
                                  kg[:, :].rearrange("p (c s) -> p c s", s=CH), ebl, ALU.mult).then_inc(S["kH_ready"], 1)
                if not last:
                    ln1_apply(u + 1)
                wait(dve, "tanh_ready", u)
                wait(dve, "og_ready", u - 1)
                dve.scalar_tensor_tensor(out=sg[:, :, :], in0=tg[:, :, :], scalar=1.0, in1=PS[:, 4:8, DV:2 * DV],
                                         op0=ALU.add, op1=ALU.mult).then_inc(S["sg_ready"], 1)
                for h in range(GH):
                    wait(dve, "A_ready", u, h + 1)
                    dve.tensor_tensor(att[:, h, :].rearrange("p (j t) -> p j t", j=UT),
                                      PS[:, 4 + h, :].rearrange("p (j t) -> p j t", j=UT),
                                      chunk_causal[:, :].unsqueeze(1).broadcast_to([P, UT, P]), ALU.mult)\
                       .then_inc(S["att_ready"], 1)
                wait(dve, "U_ready", u)
                even = PS[:, 0, 0:UB * 2 * GV].rearrange("p (b c v) -> p b c v", b=UB, c=2)
                odd = PS[:, 3, 0:UB * GV].rearrange("p (b v) -> p b v", b=UB)
                wait(dve, "bd_ready", u - 1)
                dve.tensor_copy(state[:, :, 0, :], even[:, :, 0, :]).then_inc(S["H_step"], 1)
                for c in (1, 2):
                    wait(dve, "H_step", u, 1 if c == 1 else 2)
                    for i in range(UB):
                        at = i * T + c * CH + CH - 1
                        ins = dve.scalar_tensor_tensor(out=state[:, i, c, :], in0=state[:, i, c - 1, :],
                                                       scalar=eb[:, at:at + 1],
                                                       in1=odd[:, i, :] if c == 1 else even[:, i, 1, :],
                                                       op0=ALU.mult, op1=ALU.add)
                        if i == UB - 1:
                            ins.then_inc(S["H_step"], 1)
                wait(dve, "H_step", u)
                dve.tensor_tensor(state_bd[:, :, :, :],
                                  state[:, :, :, :].rearrange("p b c v -> p (b c) v").unsqueeze(2)
                                  .broadcast_to([P, UB * (NCH - 1), GH, GV]),
                                  head_of_row[:, :].unsqueeze(1).unsqueeze(3)
                                  .broadcast_to([P, UB * (NCH - 1), GH, GV]), ALU.mult).then_inc(S["bd_ready"], 1)
                if not last:
                    gate_min(u + 1)
                    gate_cumsum(u + 1)
                wait(dve, "sq_ready", u)
                wait(dve, "og2_ready", u - 1)
                dve.tensor_tensor(og[:, :, :], PS[:, 4:6, :].rearrange("p k (h v) -> p (k h) v", v=GV),
                                  sg[:, :, :].rearrange("p j (h v) -> p (j h) v", v=GV), ALU.mult).then_inc(S["og_ready"], 1)
                wait(dve, "rrms_ready", u - 1)
                dve.tensor_reduce(ss[:, :], sq[:, :, :], AX.X, ALU.add).then_inc(S["ss_ready"], 1)
                wait(dve, "rrms_ready", u)
                wait(dve, "og_ready", u)
                wait(dve, "oTp_ready", u - 1)
                dve.tensor_tensor(og2[:, :, :], og[:, :, :], rrms[:, :].unsqueeze(2).broadcast_to([P, UT * GH, GV]),
                                  ALU.mult).then_inc(S["og2_ready"], 1)
                wait(dve, "y_ready", u)
                wait(dve, "x1_ready", u - 1)
                dve.wait_ge(ga_in, (u + 1) * 16)
                dve.tensor_tensor(yg[:, :, :, :], PS[:, 1, :].rearrange("p (b t d) -> p b t d", b=UB, t=TB),
                                  ga_bc[:, :, :].unsqueeze(2).broadcast_to([P, UB, TB, D]), ALU.mult)\
                   .then_inc(S["yg_ready"], 1)

            dve.wait_ge(x_head_in, 16)
            ln1_stats(0)
            ln1_apply(0)
            gate_min(0)
            gate_cumsum(0)
            body(0)
            dve.wait_ge(x_rest_in, 16)
            with dve.Fori(1, UNITS - 1) as u:
                body(u)
            body(UNITS - 1, last=True)

        @block.tensor
        def _(pe):
            pe.wait_ge(consts_in, N_CONST)
            pe.wait_ge(silu_c, 2)
            for k in range(2):
                pe.matmul(PS[:, 0, k * B:(k + 1) * B], wmod[:, k * D:(k + 1) * D], csil[:, :], start=(k == 0),
                          stop=True, skip_group_check=True)
            mm = pe.matmul(PS[0:B, 1, :], csil[:, :], wmod[:, 2 * D:6 * D], start=True, stop=True)
            mm.then_inc(setup_mm, 2)
            pe.matmul(PS[:, 2, 0:P], w1t[:, :], w2[:, :], start=True, stop=True).then_inc(setup_mm, 1)

            def normed_T(u):
                wait(pe, "xn_ready", u)
                wait(pe, "H_step", u - 2)
                wait(pe, "hT_ready", u - 1)
                for j in range(UT):
                    mm = pe.transpose(PS[:, 0, j * P:(j + 1) * P], xn[:, j, :], ident[:, :])
                mm.then_inc(S["xnT_ready"], 1)

            def gate_z(u):
                wait(pe, "hT_ready", u)
                wait(pe, "yg_ready", u - 2)
                wait(pe, "g_min", u - 1)
                pe.matmul(PS[:, 1, :], w12[:, :], hT[:, :], start=True, stop=True).then_inc(S["z_ready"], 1)

            def body(u, last=False):
                wait(pe, "kHt_ready", u - 1)
                pe.matmul(PS[:, 2, :], wq[:, :], hT[:, :], start=True, stop=True).then_inc(S["q_ready"], 1)
                wait(pe, "H_step", u - 1)
                pe.matmul(PS[:, 3, :], wk[:, :], hT[:, :], start=True, stop=True).then_inc(S["k_ready"], 1)
                wait(pe, "og_ready", u - 1)
                wait(pe, "oT_ready", u - 1)
                for j in range(UT):
                    pe.matmul(PS[:, 4 + j, :], hT[:, j * P:(j + 1) * P], wvg[:, :], start=True, stop=True)\
                      .then_inc(S["vg_ready"], 1)
                if not last:
                    normed_T(u + 1)
                    gate_z(u + 1)
                wait(pe, "kH_ready", u)
                wait(pe, "qg_ready", u)
                for j in range(UT):
                    mm = pe.transpose(PS[:, 2, j * P:(j + 1) * P], kH[:, j * P:(j + 1) * P], ident[:, :])
                mm.then_inc(S["kHT_ready"], 1)
                wait(pe, "v_ready", u)
                wait(pe, "sg_ready", u)
                for j in range(UT):
                    for h in range(GH):
                        rows = slice(h * GK, (h + 1) * GK)
                        mm = pe.matmul(PS[:, 4 + h, j * P:(j + 1) * P], kg[rows, j * P:(j + 1) * P],
                                       qg[rows, j * P:(j + 1) * P], start=True, stop=True)
                        if j == UT - 1:
                            mm.then_inc(S["A_ready"], 1)
                wait(pe, "kHt_ready", u)
                apart(pe)
                for i in range(UB):
                    for c in range(NCH - 1):
                        j, half = i * TB + c // 2, c % 2
                        col = (i * 2 + c // 2) * GV if half == 0 else i * GV
                        rows = slice(half * CH, (half + 1) * CH)
                        for h in range(GH):
                            mm = pe.matmul(PS[h * GK:(h + 1) * GK, 3 * half, col:col + GV],
                                           kHt[rows, j, h * GK:(h + 1) * GK], v_sb[rows, j, h * GV:(h + 1) * GV],
                                           start=True, stop=True, skip_group_check=True)
                mm.then_inc(S["U_ready"], 1)
                wait(pe, "att_ready", u)
                for j in range(UT):
                    for h in range(GH):
                        pe.matmul(PS[:, 4 + j // 2, (j % 2) * DV + h * GV:(j % 2) * DV + (h + 1) * GV],
                                  att[:, h, j * P:(j + 1) * P], v_sb[:, j, h * GV:(h + 1) * GV],
                                  start=(j % 2 == 0 and h == 0), stop=False, skip_group_check=True)
                wait(pe, "bd_ready", u)
                for i in range(UB):
                    for c in range(1, NCH):
                        j, half = i * TB + c // 2, c % 2
                        mm = pe.matmul(PS[half * CH:(half + 1) * CH, 4 + j // 2, (j % 2) * DV:(j % 2 + 1) * DV],
                                       qg[:, i * T + c * CH:i * T + (c + 1) * CH], state_bd[:, i * (NCH - 1) + c - 1, :, :],
                                       start=False, stop=True, skip_group_check=True)
                mm.then_inc(S["o_ready"], 1)
                wait(pe, "og2_ready", u)
                for j in range(UT):
                    for e in range(2):
                        k = j * 2 + e
                        mm = pe.transpose(PS[:, 6 + k // 4, (k % 4) * P:(k % 4 + 1) * P],
                                          og2[:, j * GH + e * 2:j * GH + e * 2 + 2, :].rearrange("p h v -> p (h v)"),
                                          ident[:, :])
                mm.then_inc(S["oTp_ready"], 1)
                wait(pe, "oT_ready", u)
                if not last:
                    wait(pe, "g_min", u + 1)
                for j in range(UT):
                    for e in range(2):
                        mm = pe.matmul(PS[:, 1, j * D:(j + 1) * D], oT[:, j, e, :], wo[:, e, :],
                                       start=(e == 0), stop=(e == 1))
                mm.then_inc(S["y_ready"], 1)

            pe.wait_ge(setup_v, 10)
            normed_T(0)
            gate_z(0)
            body(0)
            with pe.Fori(1, UNITS - 1) as u:
                body(u)
            body(UNITS - 1, last=True)


class Step:

    def __init__(self, k, c):
        self.k, self.c = k, c
        self.n = 2 * k + c

    def __add__(self, d):
        return Step(self.k, self.c + d)

    @property
    def par(self):
        return self.c % 2

    @property
    def half(self):
        return self.k + self.c // 2


FIRST, LOOP0, LOOP1, LAST = -3, 3, 29, B + 1


def turns(eng, body):
    for i in range(FIRST, LOOP0):
        body(Step(0, i), lambda lag, i=i: 0 <= i + lag < B)
    with eng.Fori(0, (LOOP1 - LOOP0) // 2) as k:
        for r in range(2):
            body(Step(k, LOOP0 + r), lambda lag: True)
    for i in range(LOOP1, LAST + 1):
        body(Step(0, i), lambda lag, i=i: 0 <= i + lag < B)


def feed_forward(nc, a, out, x_res, ident, mhalf, rowmod_dram, consts_in, n_const):
    NORM, PROJ, MAXI, PROB, TAIL, EXPS = 3, 2, 1, 0, -1, -2
    with ExitStack() as ctx:
        def sb(name, shape, dt=F32):
            return ctx.enter_context(nc.sbuf_tensor(name, shape, dt))

        def sem(name):
            return ctx.enter_context(nc.semaphore(name))

        r_res = sb("r_res", [P, B * TB, D])
        rope_cos = sb("rope_cos_sb", [P, T])
        rope_sin = sb("rope_sin_sb", [P, T])
        above_f = sb("above_f", [P, P])
        above = sb("above_sb", [P, P], BF16)
        ident_b = sb("ident_b", [P, P], BF16)
        cum_keep = sb("cum_keep", [P, TB * NE])
        wq2 = sb("wq2", [D, P + P // 2])
        wuk2 = sb("wuk2", [LAT, P + P // 2])
        wdkv = sb("wdkv", [D, LAT])
        wuv = sb("wuv", [LAT, P])
        wo2 = sb("wo2", [P, D])
        n1w = sb("n1w", [D, 1])
        n2w = sb("n2w", [D, 1])
        lng = sb("lng", [LAT, 1])
        lnb = sb("lnb", [LAT, 1])
        gw = sb("gw", [D, NE])
        gb4 = sb("gb4", [P, TB, NE])
        w1 = sb("w1", [D, NE * HID])
        w2 = sb("w2e", [P, NE * HT, D])
        b1 = sb("b1", [P, NE * HT])
        b2 = sb("b2", [NE, D])
        off_f = sb("off_f", [NE, NE])
        off = sb("off_sb", [NE, NE, P], BF16)

        ln_st = sb("ln_st", [P, TB, 6])
        ln_mv = sb("ln_mv", [P, TB, 2])
        ln_ve = sb("ln_ve", [P, TB])
        ln_rs = sb("ln_rs", [P, TB])
        xn = sb("xn2", [P, TB, D])
        xc = sb("xc2", [P, TB, D])
        mod_bc = sb("mod_bc", [P, 2, D])
        gb_bc = sb("gb_bc", [P, D])
        sqj = sb("sqj", [P, TB, D])
        s1 = sb("s1", [P, TB])
        s1e = sb("s1e", [P, TB])
        s1r = sb("s1r", [P, TB])
        a1 = sb("a1", [P, TB, D])
        a1T = sb("a1T", [D, T])
        la_st = sb("la_st", [P, TB, 6])
        la_mv = sb("la_mv", [P, TB, 2])
        la_ve = sb("la_ve", [P, TB])
        la_rs = sb("la_rs", [P, TB])
        la = sb("la", [P, TB, LAT])
        laT = sb("laT", [LAT, T])
        rt1 = sb("rt1", [P, 2, T])
        rt2 = sb("rt2", [P, 2, T])
        rt = sb("rt", [P, 2, T])
        rr = sb("rr", [P, 2, T])
        parts = sb("parts", [P, 3, 2, T], BF16)
        v1 = [sb(f"v1_{n}", [P, TB, MH, 32]) for n in range(2)]
        qs = [sb(f"qs{n}", [64, MH, T], BF16) for n in range(2)]
        ks = [sb(f"ks{n}", [64, MH, T], BF16) for n in range(2)]
        nm = sb("nm", [P, TB, MH])
        nr = sb("nr", [P, TB, MH])
        nparts = sb("nparts", [P, TB, 3, MH], BF16)
        nT = sb("nT", [3 * MH, T], BF16)
        pexp = sb("pexp", [P, 2, 1536])
        o_sb = sb("o_sb", [P, 4, T])
        rec = sb("rec", [P, TB * MH])
        on = sb("on", [P, TB, MH * MD])
        onT = sb("onT", [P, T])
        sqk = sb("sqk", [P, TB, D])
        s2 = sb("s2", [P, TB])
        s2e = sb("s2e", [P, TB])
        s2r = sb("s2r", [P, TB])
        a2 = sb("a2", [P, TB, D])
        a2T = sb("a2T", [D, T])
        lg = sb("lg", [P, TB, NE])
        lmax = sb("lmax", [P, TB])
        hit = sb("hit", [P, TB, NE])
        hits = sb("hits", [P, TB, NE])
        pick = sb("pick", [P, TB, NE])
        pickT = sb("pickT", [NE, T])
        missT = sb("missT", [NE, T], BF16)
        hs = sb("hs", [P, 2, 2, T])
        yr = sb("yr", [P, TB, D])
        yg = sb("yg2", [P, TB, D])
        res = sb("res", [P, TB, D])

        PS = ctx.enter_context(nc.psum_tensor("PS2", [P, 8, 512], F32))
        PB, XB, OB, ZB, YB, MB = (0, 1), (2, 5), 3, 5, 6, 7

        parts_dram = nc.dram_tensor("parts_dram", (B, 2, 3 * MD, MH, T), BF16, kind="Internal").ap()
        negmax_dram = nc.dram_tensor("negmax_dram", (B, 3, MH, T), BF16, kind="Internal").ap()

        w_in = sem("w_in")
        w_set = sem("w_set")
        pool_set = sem("pool_set")
        act_set = sem("act_set")
        mod_in = sem("mod_in")
        gb_in = sem("gb_in")
        parts_out = [sem("parts_out0"), sem("parts_out1")]
        stack_in = [sem("stack_in0"), sem("stack_in1")]
        negmax_out = sem("negmax_out")
        negmax_in = sem("negmax_in")
        res_out = sem("res_out")
        own = sem("own2")
        PER = {"f_stats": TB, "f_mean": TB, "f_xn": TB, "f_sq": TB, "a1_ready": TB, "la_stats": TB, "la_mean": TB,
               "la_ready": TB, "max_mm": 12, "max_ready": 12, "prob_mm": 12, "prob_ready": 12, "diag_ready": 8,
               "pv_done": 4, "t_sq": TB, "a2_ready": TB, "z_ready": 8, "h_ready": 8, "h_used": 8}
        NAMES = ("f_stats f_mean f_eps f_rstd f_xn f_scaled h_ready2 f_sq f_eps2 f_rstd2 a1_ready a1Tp a1T_ready lat_mm "
                 "la_stats la_mean la_eps la_rstd la_ready laTp laT_ready q_mm k_mm rt1_ready rt2_ready rt_ready p0_ready rr1_ready "
                 "p1_ready parts_ready v_mm v_ready max_mm max_ready n_0 n_r1 n_1 n_ready nTp nT_ready prob_mm prob_ready "
                 "diag_ready pv_done o_ready OT_mm rec_ready on_ready onTp onT_ready wo_mm r_ready t_sq t_eps t_rstd "
                 "a2_ready a2Tp a2T_ready lg_mm lg_ready lmax_ready hit_ready hits_ready pick_ready pickTp pickT_ready missT_ready "
                 "z_ready h_ready h_used y_mm yr_ready yg_ready res_ready").split()
        S = {n: sem("ff_" + n) for n in NAMES}

        def wait(eng, name, s, k=None):
            per = PER.get(name, 1)
            k = per if k is None else k
            if isinstance(s.n, int) and s.n * per + k <= 0:
                return
            eng.wait_ge(S[name], s.n * per + k)

        def apart(eng):
            eng.sem_inc(own, 1)

        block = ctx.enter_context(nc.Block())
        LOADS = [(rope_cos, "rope_cos"), (rope_sin, "rope_sin"), (above_f, "above"), (wq2, "wq2"), (wuk2, "wuk2"),
                 (cum_keep, "first_of_four"), (wdkv, "wdkv"), (wuv, "wuv"), (wo2, "wo2"), (n1w, "n1w"), (n2w, "n2w"),
                 (lng, "lng"), (lnb, "lnb"), (gw, "gw"), (w1, "w1"), (b1, "b1"), (b2, "b2"), (off_f, "off")]
        N_W = 16 * (len(LOADS) + 2)

        @block.sync
        def _(sp):
            for dst, name in LOADS:
                sp.dma_start(dst[:, :], a[name]).then_inc(w_in, 16)
            sp.dma_start(gb4[:, :, :], a["gate_b"].unsqueeze(0).broadcast_to([P, TB, NE])).then_inc(w_in, 16)
            sp.dma_start(w2[:, :, :], a["w2e"].rearrange("(h p) n -> p h n", p=P)).then_inc(w_in, 16)
            sp.wait_ge(pool_set, 2)

            def body(i, on_):
                if on_(MAXI):
                    s = i + MAXI
                    sp.wait_ge(parts_out[s.par], 32 * (s.half + 1))
                    wait(sp, "pv_done", s + -2)
                    wait(sp, "prob_mm", s + -2)
                    sin = stack_in[s.par]
                    src = parts_dram[bass.ds(s.n, 1)].rearrange("o a r h t -> (o a) r (h t)")
                    q, k = src[0], src[1]
                    qd, kd = (x[:, :, :].rearrange("r h t -> r (h t)") for x in (qs[s.par], ks[s.par]))
                    sp.dma_start(qd[0:24, :], q[0:24, :]).then_inc(sin, 16)
                    sp.dma_start(qd[24:40, :], q[0:16, :]).then_inc(sin, 16)
                    sp.dma_start(qd[40:48, :], q[0:8, :]).then_inc(sin, 16)
                    for row, part in ((0, 0), (8, 0), (16, 0), (24, 1), (32, 1), (40, 2)):
                        sp.dma_start(kd[row:row + 8, :], k[part * 8:part * 8 + 8, :]).then_inc(sin, 16)
                if on_(PROB):
                    s = i + PROB
                    wait(sp, "nT_ready", s)
                    dst = negmax_dram[bass.ds(s.n, 1)]
                    sp.dma_start(dst.rearrange("o a h t -> (o a h) t"), nT[:, :]).then_inc(negmax_out, 16)
                    sp.wait_ge(negmax_out, 16 * (s.n + 1))
                    sp.dma_start(qs[s.par][KROWS:KROWS + 3, :, :].rearrange("r h t -> r (h t)"),
                                 dst.rearrange("o a h t -> (o a) (h t)")).then_inc(negmax_in, 16)
                if on_(EXPS):
                    s = i + EXPS
                    wait(sp, "yg_ready", s + -1)
                    sp.dma_start(gb_bc[:, :], rowmod_dram[bass.ds(s.n, 1), 3, :].broadcast_to([P, D])).then_inc(gb_in, 16)
                if on_(NORM):
                    s = i + NORM
                    wait(sp, "h_ready2", s + -1)
                    sp.dma_start(mod_bc[:, :, :], rowmod_dram[bass.ds(s.n, 1), 1:3, :].broadcast_to([P, 2, D]))\
                      .then_inc(mod_in, 16)
                if on_(PROJ):
                    s = i + PROJ
                    wait(sp, "parts_ready", s)
                    for x in range(2):
                        sp.dma_start(parts_dram[bass.ds(s.n, 1), x].rearrange("o (a d) h t -> (o d h) a t", a=3),
                                     parts[:, :, x, :]).then_inc(parts_out[s.par], 16)
                if on_(EXPS):
                    s = i + EXPS
                    wait(sp, "res_ready", s)
                    sp.dma_start(out[bass.ds(s.n, 1)].rearrange("o (t p) d -> p (o t) d", p=P), res[:, :, :])\
                      .then_inc(res_out, 16)
            turns(sp, body)
            sp.wait_ge(res_out, 16 * B)

        @block.gpsimd
        def _(pool):
            fills = [(ks[n][32:64, :, :], 1.0) for n in range(2)]
            fills += [(v1[n][:, :, :, :], 0.0) for n in range(2)] + [(v1[n][:, :, :, MD:MD + 1], 1.0) for n in range(2)]
            for n, (where, value) in enumerate(fills):
                if n > 0:
                    pool.wait_ge(pool_set, n)
                pool.memset(where, value).then_inc(pool_set, 1)

            def rstd(s, src, ve, rs, eps, scale, got, stepped, done, used):
                wait(pool, got, s)
                apart(pool)
                pool.tensor_scalar(ve[:, :], src, scale, eps, ALU.mult, ALU.add).then_inc(S[stepped], 1)
                wait(pool, used, s + -1)
                wait(pool, stepped, s)
                pool.tensor_tensor(rs[:, :], ve[:, :], mhalf[:, 0:TB], ALU.pow).then_inc(S[done], 1)

            def body(i, on_):
                if on_(PROJ):
                    s = i + PROJ
                    rstd(s, la_mv[:, :, 1], la_ve, la_rs, EPS, 1.0, "la_mean", "la_eps", "la_rstd", "la_ready")
                if on_(TAIL):
                    s = i + TAIL
                    rstd(s, s2[:, :], s2e, s2r, EPS_RMS, 1.0 / D, "t_sq", "t_eps", "t_rstd", "a2_ready")
                if on_(PROJ):
                    s = i + PROJ
                    wait(pool, "rt1_ready", s, None)
                    wait(pool, "rt2_ready", s)
                    wait(pool, "rr1_ready", s + -1)
                    wait(pool, "p0_ready", s + -1)
                    pool.tensor_tensor(rt[:, :, :], rt1[:, :, :], rt2[:, :, :], ALU.add).then_inc(S["rt_ready"], 1)
                if on_(NORM):
                    s = i + NORM
                    rstd(s, ln_mv[:, :, 1], ln_ve, ln_rs, EPS, 1.0, "f_mean", "f_eps", "f_rstd", "f_xn")
                    pool.wait_ge(mod_in, 16 * (s.n + 1))
                    wait(pool, "f_xn", s)
                    pool.tensor_tensor(xc[:, :, :], xn[:, :, :], mod_bc[:, 1:2, :].broadcast_to([P, TB, D]), ALU.mult)\
                        .then_inc(S["f_scaled"], 1)
                    wait(pool, "f_scaled", s)
                    pool.tensor_tensor(r_res[:, bass.ts(s.n, TB), :], xc[:, :, :],
                                       mod_bc[:, 0:1, :].broadcast_to([P, TB, D]), ALU.add).then_inc(S["h_ready2"], 1)
                    rstd(s, s1[:, :], s1e, s1r, EPS_RMS, 1.0 / D, "f_sq", "f_eps2", "f_rstd2", "a1_ready")
                if on_(EXPS):
                    s = i + EXPS
                    wait(pool, "yr_ready", s)
                    pool.wait_ge(gb_in, 16 * (s.n + 1))
                    wait(pool, "res_ready", s + -1)
                    pool.tensor_tensor(yg[:, :, :], yr[:, :, :], gb_bc[:, :].unsqueeze(1).broadcast_to([P, TB, D]), ALU.mult)\
                        .then_inc(S["yg_ready"], 1)
                    wait(pool, "yg_ready", s)
                    if not isinstance(s.n, int) or s.n > 0:
                        pool.wait_ge(res_out, 16 * s.n)
                    pool.tensor_tensor(res[:, :, :], yg[:, :, :], x_res[:, bass.ts(s.n, TB), :], ALU.add)\
                        .then_inc(S["res_ready"], 1)
                if on_(PROB):
                    s = i + PROB
                    for g in range(4):
                        buf = pexp[:, g % 2, :]
                        wait(pool, "prob_ready", s, 3 * g + 2)
                        apart(pool)
                        first = buf[:, 0:1024].rearrange("p (h q) -> p h q", h=4)[:, :, 0:P]
                        pool.affine_select(out=first, in_=first, compare_op=ALU.is_ge, fill=0.0, base=0,
                                           pattern=[[0, 4], [1, P]], channel_multiplier=-1).then_inc(S["diag_ready"], 1)
                        wait(pool, "prob_ready", s, 3 * g + 3)
                        apart(pool)
                        second = buf[:, 1024:1536].rearrange("p (h q) -> p h q", h=4)
                        pool.affine_select(out=second, in_=second, compare_op=ALU.is_ge, fill=0.0, base=0,
                                           pattern=[[0, 4], [1, P]], channel_multiplier=-1).then_inc(S["diag_ready"], 1)
            turns(pool, body)

        @block.scalar
        def _(act):
            act.wait_ge(w_in, N_W)
            act.activation(above[:, :], above_f[:, :], ACT.Copy).then_inc(act_set, 1)
            act.activation(ident_b[:, :], ident[:, :], ACT.Copy).then_inc(act_set, 1)
            act.activation(off[:, :, :], off_f[:, :].unsqueeze(2).broadcast_to([NE, NE, P]), ACT.Copy).then_inc(act_set, 1)
            act.wait_ge(pool_set, 6)
            act.wait_ge(w_set, 4)

            def experts(i, on_, lo, hi):
                if on_(EXPS):
                    s = i + EXPS
                    for p in range(lo, hi):
                        wait(act, "z_ready", s, p + 1)
                        wait(act, "h_used", s, p + 1 - 2)
                        for m in range(2):
                            ins = act.activation(hs[:, p % 2, m, :], PS[:, ZB, m * T:(m + 1) * T], ACT.Relu,
                                                 bias=b1[:, 2 * p + m:2 * p + m + 1])
                        ins.then_inc(S["h_ready"], 1)

            def body(i, on_):
                if on_(PROB):
                    s = i + PROB
                    wait(act, "nTp", s)
                    if isinstance(s.n, int) and s.n <= 0:
                        pass
                    else:
                        act.wait_ge(negmax_out, 16 * s.n)
                    act.activation(nT[:, :], PS[0:3 * MH, MB, 0:T // 2].bitcast(BF16), ACT.Copy).then_inc(S["nT_ready"], 1)
                if on_(PROJ):
                    s = i + PROJ
                    wait(act, "a1Tp", s)
                    wait(act, "q_mm", s + -1)
                    act.activation(a1T[:, :], PS[:, MB, 0:T], ACT.Copy).then_inc(S["a1T_ready"], 1)
                experts(i, on_, 0, 3)
                if on_(TAIL):
                    s = i + TAIL
                    wait(act, "onTp", s)
                    wait(act, "wo_mm", s + -1)
                    act.activation(onT[:, :], PS[:, MB, 0:T], ACT.Copy).then_inc(S["onT_ready"], 1)
                experts(i, on_, 3, 4)
                if on_(PROJ):
                    s = i + PROJ
                    wait(act, "laTp", s)
                    wait(act, "v_mm", s + -1)
                    act.activation(laT[:, :], PS[0:LAT, MB, 0:T], ACT.Identity, scale=lng[:, 0:1], bias=lnb[:, 0:1])\
                       .then_inc(S["laT_ready"], 1)
                if on_(TAIL):
                    s = i + TAIL
                    wait(act, "r_ready", s)
                    wait(act, "t_eps", s + -1)
                    for t in range(TB):
                        act.activation(sqk[:, t, :], r_res[:, bass.ds(s.n * TB + t, 1), :].rearrange("p o d -> p (o d)"),
                                       ACT.Square, accum_out=s2[:, t:t + 1]).then_inc(S["t_sq"], 1)
                experts(i, on_, 4, 6)
                if on_(PROJ):
                    s = i + PROJ
                    wait(act, "rt_ready", s)
                    if not isinstance(s.n, int) or s.n >= 1:
                        act.wait_ge(parts_out[(s + -1).par], 32 * ((s + -1).half + 1))
                    act.activation(parts[:, 0, :, :], rt[:, :, :], ACT.Copy).then_inc(S["p0_ready"], 1)
                    wait(act, "rr1_ready", s)
                    act.activation(parts[:, 1, :, :], rr[:, :, :], ACT.Copy).then_inc(S["p1_ready"], 1)
                if on_(NORM):
                    s = i + NORM
                    wait(act, "h_ready2", s)
                    wait(act, "f_eps2", s + -1)
                    for t in range(TB):
                        act.activation(sqj[:, t, :], r_res[:, bass.ds(s.n * TB + t, 1), :].rearrange("p o d -> p (o d)"),
                                       ACT.Square, accum_out=s1[:, t:t + 1]).then_inc(S["f_sq"], 1)
                experts(i, on_, 6, 8)
                if on_(TAIL):
                    s = i + TAIL
                    wait(act, "a2Tp", s)
                    wait(act, "z_ready", s + -1)
                    act.activation(a2T[:, :], PS[:, MB, 0:T], ACT.Copy).then_inc(S["a2T_ready"], 1)
                if on_(PROB):
                    s = i + PROB
                    for g in range(12):
                        hg, x = g // 3, g % 3
                        wait(act, "prob_mm", s, g + 1)
                        wait(act, "pv_done", s, hg + 1 - 2)
                        act.activation(pexp[:, hg % 2, x * 512:(x + 1) * 512], PS[:, PB[g % 2], :], ACT.Exp,
                                       scale=float(MD) ** -0.5).then_inc(S["prob_ready"], 1)
                    wait(act, "pv_done", s)
                    wait(act, "OT_mm", s + -1)
                    act.activation(o_sb[:, :, :], PS[:, OB:OB + 2, :].rearrange("p k (g q) -> p (k g) q", g=2), ACT.Copy)\
                       .then_inc(S["o_ready"], 1)
                if on_(TAIL):
                    s = i + TAIL
                    wait(act, "pickTp", s)
                    wait(act, "y_mm", s + -1)
                    act.activation(pickT[:, :], PS[0:NE, MB, 0:T], ACT.Copy).then_inc(S["pickT_ready"], 1)
                    act.activation(missT[:, :], PS[0:NE, MB, 0:T], ACT.Copy, scale=1.0, bias=-1.0)\
                       .then_inc(S["missT_ready"], 1)
                if on_(PROJ):
                    s = i + PROJ
                    wait(act, "v_mm", s)
                    wait(act, "pv_done", s + -2)
                    act.activation(v1[s.par][:, :, :, 0:MD], PS[:, MB, 0:T].rearrange("p (t h d) -> p t h d", t=TB, h=MH),
                                   ACT.Copy).then_inc(S["v_ready"], 1)
            turns(act, body)

        @block.vector
        def _(dve):
            dve.wait_ge(w_in, N_W)
            dve.tensor_scalar(wq2[:, :], wq2[:, :], n1w[:, 0:1], None, ALU.mult).then_inc(w_set, 1)
            dve.tensor_scalar(wdkv[:, :], wdkv[:, :], n1w[:, 0:1], None, ALU.mult).then_inc(w_set, 1)
            dve.tensor_scalar(gw[:, :], gw[:, :], n2w[:, 0:1], None, ALU.mult).then_inc(w_set, 1)
            dve.tensor_scalar(w1[:, :], w1[:, :], n2w[:, 0:1], None, ALU.mult).then_inc(w_set, 1)

            def norm_stats(s, tile_of, st, mv, stats, mean, used):
                wait(dve, used, s + -1)
                for t in range(TB):
                    dve.bn_stats(st[:, t, :], tile_of(t)).then_inc(S[stats], 1)
                for t in range(TB):
                    wait(dve, stats, s, t + 1)
                    apart(dve)
                    dve.bn_aggr(mv[:, t, :], st[:, t, :]).then_inc(S[mean], 1)

            def body(i, on_):
                if on_(TAIL):
                    s = i + TAIL
                    ot = PS[:, OB:OB + 2, :].rearrange("p t (h c) -> p (t h) c", c=32)
                    wait(dve, "OT_mm", s)
                    wait(dve, "on_ready", s + -1)
                    dve.reciprocal(rec[:, :], ot[:, :, MD]).then_inc(S["rec_ready"], 1)
                    wait(dve, "rec_ready", s)
                    wait(dve, "onTp", s + -1)
                    dve.tensor_tensor(on[:, :, :].rearrange("p t (h d) -> p (t h) d", d=MD), ot[:, :, 0:MD],
                                      rec[:, :].unsqueeze(2).broadcast_to([P, TB * MH, MD]), ALU.mult)\
                       .then_inc(S["on_ready"], 1)
                if on_(PROJ):
                    s = i + PROJ
                    wait(dve, "lat_mm", s)
                    lat = PS[:, MB, 0:TB * LAT].rearrange("p (t c) -> p t c", t=TB)
                    norm_stats(s, lambda t: lat[:, t, :], la_st, la_mv, "la_stats", "la_mean", "la_ready")
                    wait(dve, "la_rstd", s)
                    wait(dve, "laTp", s + -1)
                    for t in range(TB):
                        dve.tensor_scalar(la[:, t, :], lat[:, t, :], la_mv[:, t, 0:1], la_rs[:, t:t + 1], ALU.subtract,
                                          ALU.mult).then_inc(S["la_ready"], 1)
                if on_(TAIL):
                    s = i + TAIL
                    wait(dve, "wo_mm", s)
                    h = r_res[:, bass.ts(s.n, TB), :]
                    dve.tensor_tensor(h, h, PS[:, MB, 0:T].rearrange("p (t d) -> p t d", t=TB), ALU.add)\
                       .then_inc(S["r_ready"], 1)
                if on_(PROJ):
                    s = i + PROJ
                    wait(dve, "k_mm", s)
                    wait(dve, "rt_ready", s + -1)
                    dve.tensor_tensor(rt1[:, :, :], PS[:, OB, :].rearrange("p (x t) -> p x t", x=2),
                                      rope_cos[:, :].unsqueeze(1).broadcast_to([P, 2, T]), ALU.mult).then_inc(S["rt1_ready"], 1)
                    dve.tensor_tensor(rt2[:, :, :], PS[:, OB + 1, :].rearrange("p (x t) -> p x t", x=2),
                                      rope_sin[:, :].unsqueeze(1).broadcast_to([P, 2, T]), ALU.mult).then_inc(S["rt2_ready"], 1)
                if on_(TAIL):
                    s = i + TAIL
                    wait(dve, "t_rstd", s)
                    wait(dve, "a2Tp", s + -1)
                    for t in range(TB):
                        dve.tensor_scalar(a2[:, t, :], r_res[:, bass.ds(s.n * TB + t, 1), :].rearrange("p o d -> p (o d)"),
                                          s2r[:, t:t + 1], None, ALU.mult).then_inc(S["a2_ready"], 1)
                if on_(NORM):
                    s = i + NORM
                    norm_stats(s, lambda t: x_res[:, bass.ds(s.n * TB + t, 1), :].rearrange("p o d -> p (o d)"),
                               ln_st, ln_mv, "f_stats", "f_mean", "f_xn")
                if on_(PROJ):
                    s = i + PROJ
                    wait(dve, "p0_ready", s)
                    wait(dve, "p1_ready", s + -1)
                    dve.tensor_tensor(rr[:, :, :], rt[:, :, :], parts[:, 0, :, :], ALU.subtract).then_inc(S["rr1_ready"], 1)
                    wait(dve, "p1_ready", s)
                    if not isinstance(s.n, int) or s.n >= 1:
                        dve.wait_ge(parts_out[(s + -1).par], 32 * ((s + -1).half + 1))
                    dve.tensor_tensor(parts[:, 2, :, :], rr[:, :, :], parts[:, 1, :, :], ALU.subtract)\
                       .then_inc(S["parts_ready"], 1)
                if on_(NORM):
                    s = i + NORM
                    wait(dve, "f_rstd", s)
                    wait(dve, "f_scaled", s + -1)
                    for t in range(TB):
                        dve.tensor_scalar(xn[:, t, :], x_res[:, bass.ds(s.n * TB + t, 1), :].rearrange("p o d -> p (o d)"),
                                          ln_mv[:, t, 0:1], ln_rs[:, t:t + 1], ALU.subtract, ALU.mult).then_inc(S["f_xn"], 1)
                if on_(EXPS):
                    s = i + EXPS
                    wait(dve, "y_mm", s)
                    wait(dve, "yg_ready", s + -1)
                    dve.tensor_tensor(yr[:, :, :], PS[:, YB, 0:T].rearrange("p (t d) -> p t d", t=TB),
                                      r_res[:, bass.ts(s.n, TB), :], ALU.add).then_inc(S["yr_ready"], 1)
                if on_(TAIL):
                    s = i + TAIL
                    wait(dve, "lg_mm", s)
                    dve.tensor_tensor(lg[:, :, :], PS[:, MB, 0:TB * NE].rearrange("p (t e) -> p t e", t=TB), gb4[:, :, :],
                                      ALU.add).then_inc(S["lg_ready"], 1)
                    wait(dve, "lg_ready", s)
                    dve.tensor_reduce(lmax[:, :], lg[:, :, :], AX.X, ALU.max).then_inc(S["lmax_ready"], 1)
                    wait(dve, "lmax_ready", s)
                    dve.tensor_tensor(hit[:, :, :], lg[:, :, :], lmax[:, :].unsqueeze(2).broadcast_to([P, TB, NE]),
                                      ALU.is_ge).then_inc(S["hit_ready"], 1)
                    wait(dve, "hit_ready", s)
                    apart(dve)
                    dve.tensor_tensor_scan(hits[:, :, :].rearrange("p t e -> p (t e)"), cum_keep[:, :],
                                           hit[:, :, :].rearrange("p t e -> p (t e)"), 0.0, ALU.mult, ALU.add)\
                       .then_inc(S["hits_ready"], 1)
                    wait(dve, "hits_ready", s)
                    wait(dve, "pickTp", s + -1)
                    dve.scalar_tensor_tensor(out=pick[:, :, :], in0=hits[:, :, :], scalar=1.0, in1=hit[:, :, :],
                                             op0=ALU.is_equal, op1=ALU.mult).then_inc(S["pick_ready"], 1)
                if on_(NORM):
                    s = i + NORM
                    wait(dve, "f_rstd2", s)
                    wait(dve, "a1Tp", s + -1)
                    for t in range(TB):
                        dve.tensor_scalar(a1[:, t, :], r_res[:, bass.ds(s.n * TB + t, 1), :].rearrange("p o d -> p (o d)"),
                                          s1r[:, t:t + 1], None, ALU.mult).then_inc(S["a1_ready"], 1)
                if on_(MAXI):
                    s = i + MAXI
                    wait(dve, "n_ready", s + -1)
                    for g in range(12):
                        wait(dve, "max_mm", s, g + 1)
                        if g < 4:
                            dve.tensor_reduce(nm[:, 0, 4 * g:4 * g + 4], PS[:, XB[g % 2], :].rearrange("p (h k) -> p h k", h=4),
                                              AX.X, ALU.max, negate=True).then_inc(S["max_ready"], 1)
                        else:
                            dve.tensor_reduce(nm[:, 1, 2 * g - 8:2 * g - 6],
                                              PS[:, XB[g % 2], :].rearrange("p (h k) -> p h k", h=2),
                                              AX.X, ALU.max, negate=True).then_inc(S["max_ready"], 1)
                    wait(dve, "max_ready", s)
                    wait(dve, "nTp", s + -1)
                    dve.tensor_copy(nparts[:, :, 0, :], nm[:, :, :]).then_inc(S["n_0"], 1)
                    wait(dve, "n_0", s)
                    dve.tensor_tensor(nr[:, :, :], nm[:, :, :], nparts[:, :, 0, :], ALU.subtract).then_inc(S["n_r1"], 1)
                    wait(dve, "n_r1", s)
                    dve.tensor_copy(nparts[:, :, 1, :], nr[:, :, :]).then_inc(S["n_1"], 1)
                    wait(dve, "n_1", s)
                    dve.tensor_tensor(nparts[:, :, 2, :], nr[:, :, :], nparts[:, :, 1, :], ALU.subtract)\
                       .then_inc(S["n_ready"], 1)
            turns(dve, body)

        @block.tensor
        def _(pe):
            pe.wait_ge(w_in, N_W)
            pe.wait_ge(w_set, 4)
            pe.wait_ge(act_set, 3)

            def values_back(s, p):
                wait(pe, "h_ready", s, p + 1)
                for m in range(2):
                    for t in range(TB):
                        mm = pe.matmul(PS[:, YB, t * D:(t + 1) * D], hs[:, p % 2, m, t * P:(t + 1) * P],
                                       w2[:, 2 * p + m, :], start=(p == 0 and m == 0 and t == 0), stop=False,
                                       skip_group_check=True)
                mm.then_inc(S["h_used"], 1)

            def experts(i, on_, lo, hi):
                if not on_(EXPS):
                    return
                s = i + EXPS
                for p in range(lo, hi):
                    if p == 0:
                        wait(pe, "missT_ready", s)
                        wait(pe, "yr_ready", s + -1)
                        wait(pe, "h_ready", s + -1)
                        if on_(PROB):
                            wait(pe, "max_ready", s + (PROB - EXPS))
                    else:
                        wait(pe, "h_ready", s, p)
                    e = 2 * p // HT
                    for m in range(2):
                        pe.matmul(PS[:, ZB, m * T:(m + 1) * T], w1[:, (2 * p + m) * P:(2 * p + m + 1) * P], a2T[:, :],
                                  start=(m == 0), stop=False, skip_group_check=True)
                    pe.matmul(PS[:, ZB, :].rearrange("p (m t) -> p m t", m=2), off[:, e, :],
                              missT[:, :].unsqueeze(1).broadcast_to([NE, 2, T]), start=False, stop=True,
                              skip_group_check=True).then_inc(S["z_ready"], 1)
                    if p > 0:
                        values_back(s, p - 1)
                if hi == 8:
                    values_back(s, 7)
                    for t in range(TB):
                        mm = pe.matmul(PS[:, YB, t * D:(t + 1) * D], pickT[:, t * P:(t + 1) * P], b2[:, :],
                                       start=False, stop=True, skip_group_check=True)
                    mm.then_inc(S["y_mm"], 1)

            def chain_T(s, src, tiles, width, name):
                for t in range(tiles):
                    mm = pe.transpose(PS[0:width, MB, t * P:(t + 1) * P], src(t), ident[:, :])
                mm.then_inc(S[name], 1)

            def scores_for_exp(s, hg):
                q, k = qs[s.par], ks[s.par]
                R = KROWS + MROWS
                for x in range(3):
                    g = 3 * hg + x
                    wait(pe, "prob_ready", s, g + 1 - 2)
                    bank = PS[:, PB[g % 2], :]
                    if x < 2:
                        for c in range(2):
                            mm = pe.matmul(bank[:, c * T:(c + 1) * T], k[0:R, 4 * hg + 2 * x + c, 0:P],
                                           q[0:R, 4 * hg + 2 * x + c, :], start=True, stop=True)
                    else:
                        for c in range(4):
                            mm = pe.matmul(bank[:, c * P:(c + 1) * P], k[0:R, 4 * hg + c, P:2 * P],
                                           q[0:R, 4 * hg + c, P:2 * P], start=True, stop=True)
                    mm.then_inc(S["prob_mm"], 1)

            def values(s, hg):
                wait(pe, "diag_ready", s, 2 * hg + 2)
                wait(pe, "prob_ready", s, 3 * hg + 3)
                for kt in range(TB):
                    for c in range(4):
                        if kt == 0:
                            o, pr = slice((hg % 2) * T, (hg % 2 + 1) * T), slice(c * T, (c + 1) * T)
                        else:
                            o, pr = slice((hg % 2) * T + P, (hg % 2 + 1) * T), slice(4 * T + c * P, 4 * T + (c + 1) * P)
                        mm = pe.matmul(PS[32 * c:32 * c + 32, OB + hg // 2, o], v1[s.par][:, kt, 4 * hg + c, :],
                                       pexp[:, hg % 2, pr], start=(kt == 0), stop=(kt == 1), skip_group_check=True)
                mm.then_inc(S["pv_done"], 1)

            def scores_for_max(s, lo, hi, on_):
                q, k = qs[s.par], ks[s.par]
                for g in range(lo, hi):
                    wait(pe, "max_ready", s, g + 1 - 2)
                    if g == 1 and on_(EXPS):
                        wait(pe, "h_ready", s + (EXPS - MAXI))
                    bank = PS[:, XB[g % 2], :]
                    if g < 4:
                        pe.matmul(bank.rearrange("p (h k) -> p h k", h=4), ident_b[:, :],
                                  above[:, :].unsqueeze(1).broadcast_to([P, 4, P]), start=True, stop=False,
                                  skip_group_check=True)
                        for c in range(4):
                            mm = pe.matmul(bank[:, c * P:(c + 1) * P], q[0:KROWS, 4 * g + c, 0:P],
                                           k[0:KROWS, 4 * g + c, 0:P], start=False, stop=True, skip_group_check=True)
                    else:
                        pe.matmul(bank.rearrange("p (h k) -> p h k", h=2)[:, :, P:2 * P], ident_b[:, :],
                                  above[:, :].unsqueeze(1).broadcast_to([P, 2, P]), start=True, stop=False,
                                  skip_group_check=True)
                        for c in range(2):
                            h = 2 * (g - 4) + c
                            mm = pe.matmul(bank[:, c * T:(c + 1) * T], q[0:KROWS, h, P:2 * P],
                                           k[0:KROWS, h, :], start=False, stop=True, skip_group_check=True)
                    mm.then_inc(S["max_mm"], 1)

            def body(i, on_):
                if on_(PROB):
                    s = i + PROB
                    wait(pe, "n_ready", s)
                    wait(pe, "v_ready", s + 1) if on_(PROB + 1) else wait(pe, "missT_ready", s + -2)
                    apart(pe)
                    for t in range(TB):
                        mm = pe.transpose(PS[0:3 * MH, MB, t * P // 2:(t + 1) * P // 2].bitcast(BF16),
                                          nparts[:, t, :, :].rearrange("p a h -> p (a h)"), ident_b[:, :])
                    mm.then_inc(S["nTp"], 1)
                if on_(TAIL):
                    s = i + TAIL
                    wait(pe, "o_ready", s)
                    for t in range(TB):
                        for g in range(4):
                            mm = pe.transpose(PS[:, OB + t, g * P:(g + 1) * P], o_sb[:, g, t * P:(t + 1) * P], ident[:, :])
                    mm.then_inc(S["OT_mm"], 1)
                if on_(PROJ):
                    s = i + PROJ
                    wait(pe, "a1_ready", s)
                    wait(pe, "nT_ready", s + -2) if on_(PROB) else wait(pe, "v_ready", s + -1)
                    chain_T(s, lambda t: a1[:, t, :], TB, D, "a1Tp")
                experts(i, on_, 0, 2)
                if on_(PROJ):
                    s = i + PROJ
                    wait(pe, "a1T_ready", s)
                    for t in range(TB):
                        mm = pe.matmul(PS[:, MB, t * LAT:(t + 1) * LAT], a1T[:, t * P:(t + 1) * P], wdkv[:, :],
                                       start=True, stop=True)
                    mm.then_inc(S["lat_mm"], 1)
                    wait(pe, "on_ready", s + -3)
                    wait(pe, "rt2_ready", s + -1)
                    pe.matmul(PS[:, OB, 0:T], wq2[:, 0:P], a1T[:, :], start=True, stop=True)
                    pe.matmul(PS[:, OB + 1, 0:T], wq2[:, P // 2:P // 2 + P], a1T[:, :], start=True, stop=True)\
                      .then_inc(S["q_mm"], 1)
                experts(i, on_, 2, 3)
                if on_(TAIL):
                    s = i + TAIL
                    wait(pe, "on_ready", s)
                    if on_(PROJ):
                        wait(pe, "la_ready", s + 3)
                    elif on_(PROB):
                        wait(pe, "nT_ready", s + 1)
                    else:
                        wait(pe, "missT_ready", s + -1)
                    chain_T(s, lambda t: on[:, t, :], TB, P, "onTp")
                experts(i, on_, 3, 4)
                if on_(PROJ):
                    s = i + PROJ
                    wait(pe, "la_ready", s)
                    wait(pe, "onT_ready", s + -3)
                    apart(pe)
                    chain_T(s, lambda t: la[:, t, :], TB, LAT, "laTp")
                if on_(TAIL):
                    s = i + TAIL
                    wait(pe, "onT_ready", s)
                    if on_(PROJ):
                        wait(pe, "laT_ready", s + 3)
                    for t in range(TB):
                        mm = pe.matmul(PS[:, MB, t * D:(t + 1) * D], onT[:, t * P:(t + 1) * P], wo2[:, :],
                                       start=True, stop=True)
                    mm.then_inc(S["wo_mm"], 1)
                experts(i, on_, 4, 6)
                if on_(PROJ):
                    s = i + PROJ
                    wait(pe, "laT_ready", s)
                    pe.matmul(PS[:, OB, T:2 * T], wuk2[:, 0:P], laT[:, :], start=True, stop=True)
                    pe.matmul(PS[:, OB + 1, T:2 * T], wuk2[:, P // 2:P // 2 + P], laT[:, :], start=True, stop=True)\
                      .then_inc(S["k_mm"], 1)
                experts(i, on_, 6, 8)
                if on_(TAIL):
                    s = i + TAIL
                    wait(pe, "a2_ready", s)
                    chain_T(s, lambda t: a2[:, t, :], TB, D, "a2Tp")
                    wait(pe, "a2T_ready", s)
                    for t in range(TB):
                        mm = pe.matmul(PS[:, MB, t * NE:(t + 1) * NE], a2T[:, t * P:(t + 1) * P], gw[:, :],
                                       start=True, stop=True)
                    mm.then_inc(S["lg_mm"], 1)
                if on_(PROB):
                    s = i + PROB
                    pe.wait_ge(stack_in[s.par], 144 * (s.half + 1))
                    pe.wait_ge(negmax_in, 16 * (s.n + 1))
                    wait(pe, "rt2_ready", s + 2) if on_(PROJ) else wait(pe, "on_ready", s + -1)
                    wait(pe, "v_ready", s)
                if on_(MAXI):
                    s = i + MAXI
                    pe.wait_ge(stack_in[s.par], 144 * (s.half + 1))
                for hg in range(4):
                    if on_(PROB):
                        scores_for_exp(i + PROB, hg)
                        if hg >= 1:
                            values(i + PROB, hg - 1)
                    if on_(MAXI):
                        scores_for_max(i + MAXI, 3 * hg, 3 * hg + 3, on_)
                if on_(PROB):
                    values(i + PROB, 3)
                if on_(TAIL):
                    s = i + TAIL
                    wait(pe, "pick_ready", s)
                    chain_T(s, lambda t: pick[:, t, :], TB, NE, "pickTp")
                if on_(PROJ):
                    s = i + PROJ
                    wait(pe, "missT_ready", s + -3)
                    for t in range(TB):
                        mm = pe.matmul(PS[:, MB, t * P:(t + 1) * P], laT[:, t * P:(t + 1) * P], wuv[:, :],
                                       start=True, stop=True)
                    mm.then_inc(S["v_mm"], 1)
            turns(pe, body)


def build(nc, a, out):
    with ExitStack() as ctx:
        x_res = ctx.enter_context(nc.sbuf_tensor("x_res", [P, B * TB, D], F32))
        ident = ctx.enter_context(nc.sbuf_tensor("ident_sb", [P, P], F32))
        mhalf = ctx.enter_context(nc.sbuf_tensor("mhalf", [P, 16], F32))
        rowmod_dram = nc.dram_tensor("rowmod_dram", (B, 4, D), F32, kind="Internal").ap()
        consts_in = ctx.enter_context(nc.semaphore("consts_in"))
        linear_attention(nc, a, x_res, ident, mhalf, rowmod_dram, consts_in, None)
        feed_forward(nc, a, out, x_res, ident, mhalf, rowmod_dram, consts_in, None)


def kernel(**inputs):
    import numpy as _np
    import concourse.bacc as _bacc
    from concourse.bass_utils import run_bass_kernel_spmd as _run

    g = {k: _np.asarray(v) for k, v in inputs.items()}
    arrays = {
        "x": g["L0_attn_x"], "wq": g["L0_attn_Wq"], "wk": g["L0_attn_Wk"],
        "wvg": _np.concatenate([g["L0_attn_Wv"], g["L0_attn_Wg"]], axis=1),
        "w1t": g["L0_attn_gk_w1"].T, "w2": g["L0_attn_gk_w2"], "gk_b": g["L0_attn_gk_b2"].reshape(-1, 1),
        "gnorm": _np.concatenate([g["L0_attn_g_norm_w"]] * 2).reshape(-1, 1), "wo": g["L0_attn_Wo"],
        "cT": g["L0_c"].T, "wmod": g["L0_wmod"],
    }
    def by_feature(w):
        w = w.reshape(-1, MH, MD).transpose(0, 2, 1).reshape(-1, P)
        return _np.concatenate([w, w[:, :P // 2]], axis=1)

    arrays.update({
        "wq2": by_feature(g["L0_ffn_Wq"].T), "wuk2": by_feature(g["L0_ffn_Wuk"].T), "wdkv": g["L0_ffn_Wdkv"].T,
        "wuv": g["L0_ffn_Wuv"].T, "wo2": g["L0_ffn_Wo"].T, "n1w": g["L0_ffn_norm1_w"].reshape(-1, 1),
        "n2w": g["L0_ffn_norm2_w"].reshape(-1, 1), "lng": g["L0_ffn_ln_g"].reshape(-1, 1),
        "lnb": g["L0_ffn_ln_b"].reshape(-1, 1), "gw": g["L0_ffn_gate_w"].T, "gate_b": g["L0_ffn_gate_b"].reshape(1, -1),
        "w1": g["L0_ffn_W1"].transpose(2, 0, 1).reshape(D, NE * HID), "b1": g["L0_ffn_b1"].reshape(NE * HT, P).T,
        "w2e": g["L0_ffn_W2"].transpose(0, 2, 1).reshape(NE * HID, D), "b2": g["L0_ffn_b2"],
    })
    arrays.update(shape_constants())
    arrays = {f"in_{k}": _np.ascontiguousarray(v) for k, v in arrays.items()}
    nc = _bacc.Bacc("TRN2", target_bir_lowering=False, num_devices=1)
    aps = {k[3:]: nc.dram_tensor(k, v.shape, mybir.dt.from_np(v.dtype), kind="ExternalInput").ap()
           for k, v in arrays.items()}
    out = nc.dram_tensor("out", g["L0_attn_x"].shape, F32, kind="ExternalOutput").ap()
    build(nc, aps, out)
    r = _run(nc, [arrays], core_ids=[0])
    return r.results[0]["out"]
```

```python
from contextlib import ExitStack

import numpy as np

import concourse.bass as bass
from concourse import mybir

F32 = mybir.dt.float32
BF16 = mybir.dt.bfloat16
ALU = mybir.AluOpType
ACT = mybir.ActivationFunctionType
AX = mybir.AxisListType

P = 128
D = 128
B = 32
T = 256
TB = T // P
EPS = 1e-5
EPS_RMS = 1e-6

GH, GK, GV, CH = 4, 32, 64, 64
DV = GH * GV
UB = 2
UT = UB * TB
UN = UB * T
UNITS = B // UB
NCH = T // CH
GATE_NORM = 16.0

MH, MD = 16, 8
LAT = 64
KROWS = 6 * MD
MROWS = 3

NE, HID = 4, 512
HT = HID // P


def shape_constants():
    half = MD // 2
    pos = np.arange(T, dtype=np.float32)
    freq = (np.float32(1.0) / np.float32(10000.0) ** (np.arange(half, dtype=np.float32) / np.float32(half))).astype(np.float32)
    ang = (pos[None, :] * freq[:, None]).astype(np.float32)
    cos, sin = np.cos(ang).astype(np.float32), np.sin(ang).astype(np.float32)
    rope_cos = np.repeat(np.concatenate([cos, cos]), MH, axis=0)
    rope_sin = np.repeat(np.concatenate([-sin, sin]), MH, axis=0)
    ident = np.eye(P, dtype=np.float32)
    s, t = np.arange(P)[:, None], np.arange(P)[None, :]
    chunk_causal = ((s <= t) & (s // CH == t // CH)).astype(np.float32)
    above = np.where(t > s, -1e30, 0.0).astype(np.float32)
    scan_keep = np.tile((np.arange(UN) % CH != 0).astype(np.float32), (P, 1))
    head_of_row = (np.arange(P)[:, None] // GK == np.arange(GH)[None, :]).astype(np.float32)
    off = np.eye(NE, dtype=np.float32) * np.float32(1e30)
    first_of_four = np.tile((np.arange(TB * NE) % NE != 0).astype(np.float32), (P, 1))
    return {"rope_cos": rope_cos, "rope_sin": rope_sin, "ident": ident, "chunk_causal": chunk_causal,
            "above": above, "scan_keep": scan_keep, "head_of_row": head_of_row, "first_of_four": first_of_four,
            "off": off}


def linear_attention(nc, a, x_res, ident, mhalf, rowmod_dram, consts_in, n_const):
    with ExitStack() as ctx:
        def sb(name, shape, dt=F32):
            return ctx.enter_context(nc.sbuf_tensor(name, shape, dt))

        def sem(name):
            return ctx.enter_context(nc.semaphore(name))

        chunk_causal = sb("chunk_causal_sb", [P, P])
        scan_keep = sb("scan_keep_sb", [P, UN])
        head_of_row = sb("head_of_row_sb", [P, GH])
        wq = sb("wq", [D, P])
        wk = sb("wk", [D, P])
        wvg = sb("wvg", [D, 2 * DV])
        w1t = sb("w1t", [16, D])
        w2 = sb("w2", [16, P])
        w12 = sb("w12", [D, P])
        gk_b = sb("gk_b", [P, 1])
        wo = sb("wo", [P, 2, D])
        gnorm = sb("gnorm", [P, 1])
        cT = sb("cT", [D, B])
        cth = sb("cth", [D, B])
        csil = sb("csil", [D, B])
        wmod = sb("wmod", [D, 6 * D])
        shiftT = sb("shiftT", [D, B])
        scaleT = sb("scaleT", [D, B])
        rowmod = sb("rowmod", [B, 4, D])
        sgn = sb("sgn", [B, 2, D])

        ln1_st = sb("ln1_st", [P, UT, 6])
        ln1_mv = sb("ln1_mv", [P, UT, 2])
        ln1_ve = sb("ln1_ve", [P, UT])
        ln1_rs = sb("ln1_rs", [P, UT])
        xn = sb("xn", [P, UT, D])
        hT = sb("hT", [D, UN])
        g_a = sb("g_a", [P, UN])
        g_e = sb("g_e", [P, UN])
        g_l = sb("g_l", [P, UN])
        g_m = sb("g_m", [P, UN])
        g_g = sb("g_g", [P, UN])
        g_cum = sb("g_cum", [P, UN])
        eb = sb("eb", [P, UN])
        enb = sb("enb", [P, UN])
        qg = sb("qg", [P, UN])
        kg = sb("kg", [P, UN])
        kH = sb("kH", [P, UN])
        kHt = sb("kHt", [P, UT, P])
        v_sb = sb("v_sb", [P, UT, DV])
        tg = sb("tg", [P, UT, DV])
        sg = sb("sg", [P, UT, DV])
        att = sb("att", [P, GH, UN])
        state = sb("state", [P, UB, NCH - 1, GV])
        state_bd = sb("state_bd", [P, UB * (NCH - 1), GH, GV])
        sq = sb("sq", [P, UT * GH, GV])
        og = sb("og", [P, UT * GH, GV])
        og2 = sb("og2", [P, UT * GH, GV])
        ss = sb("ss", [P, UT * GH])
        ss_e = sb("ss_e", [P, UT * GH])
        rrms = sb("rrms", [P, UT * GH])
        oT = sb("oT", [P, UT, 2, P])
        ga_bc = sb("ga_bc", [P, UB, D])
        yg = sb("yg", [P, UB, TB, D])

        PS = ctx.enter_context(nc.psum_tensor("PS", [P, 8, 512], F32))

        x_head_in = sem("x_head_in")
        x_rest_in = sem("x_rest_in")
        tanh_c = sem("tanh_c")
        silu_c = sem("silu_c")
        setup_mm = sem("setup_mm")
        setup_v = sem("setup_v")
        setup_v2 = sem("setup_v2")
        mhalf_set = sem("mhalf_set")
        rowmod_out = sem("rowmod_out")
        own_step = sem("own_step")
        ga_in = sem("ga_in")
        S = {n: sem(n) for n in (
            "ln1_stats", "ln1_mean", "ln1_eps", "ln1_rstd", "xn_ready", "xnT_ready", "hT_ready", "z_ready",
            "g_abs", "g_exp", "g_ln", "g_min", "g_ready", "cum_ready", "eb_ready", "enb_ready",
            "q_ready", "k_ready", "vg_ready", "v_ready", "tanh_ready", "sg_ready", "qg_ready", "kg_ready",
            "kH_ready", "kHT_ready", "kHt_ready", "A_ready", "att_ready", "U_ready", "H_step", "H_ready", "bd_ready",
            "o_ready", "sq_ready", "og_ready", "ss_ready", "ss_eps", "rrms_ready", "og2_ready", "oTp_ready",
            "oT_ready", "y_ready", "yg_ready", "x1_ready")}
        PER = {"ln1_stats": UT, "ln1_mean": UT, "xn_ready": UT, "hT_ready": UB, "vg_ready": UT, "A_ready": GH,
               "att_ready": GH, "H_step": 3}

        def wait(eng, name, n, k=None):
            per = PER.get(name, 1)
            k = per if k is None else k
            if isinstance(n, int) and n * per + k <= 0:
                return
            eng.wait_ge(S[name], n * per + k)

        def apart(eng):
            eng.sem_inc(own_step, 1)

        block = ctx.enter_context(nc.Block())

        CONST_LOADS = [
            (ident, "ident"), (chunk_causal, "chunk_causal"), (scan_keep, "scan_keep"), (head_of_row, "head_of_row"),
            (wq, "wq"), (wk, "wk"), (wvg, "wvg"), (w1t, "w1t"), (w2, "w2"), (gk_b, "gk_b"), (gnorm, "gnorm"),
            (cT, "cT"), (wmod, "wmod")]
        N_CONST = 16 * (len(CONST_LOADS) + 1)

        x_tiles = a["x"].rearrange("b (t p) d -> p (b t) d", p=P)

        @block.sync
        def _(sp):
            for dst, name in CONST_LOADS:
                sp.dma_start(dst[:, :], a[name]).then_inc(consts_in, 16)
            sp.dma_start(wo[:, :, :], a["wo"].rearrange("(e p) n -> p e n", p=P)).then_inc(consts_in, 16)
            sp.dma_start(x_res[:, 0:2 * UT, :], x_tiles[:, 0:2 * UT, :]).then_inc(x_head_in, 16)
            sp.dma_start(x_res[:, 2 * UT:, :], x_tiles[:, 2 * UT:, :]).then_inc(x_rest_in, 16)
            sp.wait_ge(setup_v2, 4)
            sp.dma_start(rowmod_dram, rowmod[:, :, :]).then_inc(rowmod_out, 16)
            sp.wait_ge(rowmod_out, 16)

            def load_ga(u):
                wait(sp, "yg_ready", u - 1)
                sp.dma_start(ga_bc[:, :, :], rowmod_dram[bass.ts(u, UB), 0:1, :].rearrange("b o d -> o b d")
                             .broadcast_to([P, UB, D])).then_inc(ga_in, 16)
            load_ga(0)
            with sp.Fori(1, UNITS) as u:
                load_ga(u)

        @block.gpsimd
        def _(pool):
            pool.memset(mhalf[:, :], -0.5).then_inc(mhalf_set, 1)
            pool.wait_ge(mhalf_set, 1)

            def ln1_rstd(u):
                wait(pool, "ln1_mean", u)
                apart(pool)
                pool.tensor_scalar(ln1_ve[:, :], ln1_mv[:, :, 1], EPS, None, ALU.add).then_inc(S["ln1_eps"], 1)
                wait(pool, "ln1_eps", u)
                wait(pool, "xn_ready", u - 1)
                pool.tensor_tensor(ln1_rs[:, :], ln1_ve[:, :], mhalf[:, 0:UT], ALU.pow).then_inc(S["ln1_rstd"], 1)

            def body(u, last=False):
                if not last:
                    ln1_rstd(u + 1)
                wait(pool, "ss_ready", u)
                apart(pool)
                pool.tensor_scalar(ss_e[:, :], ss[:, :], 1.0 / GV, EPS, ALU.mult, ALU.add).then_inc(S["ss_eps"], 1)
                wait(pool, "ss_eps", u)
                wait(pool, "og2_ready", u - 1)
                pool.tensor_tensor(rrms[:, :], ss_e[:, :], mhalf[:, :], ALU.pow).then_inc(S["rrms_ready"], 1)
                wait(pool, "yg_ready", u)
                xs = x_res[:, bass.ts(u, UT), :].rearrange("p (b t) d -> p b t d", b=UB)
                pool.tensor_tensor(xs, xs, yg[:, :, :, :], ALU.add).then_inc(S["x1_ready"], 1)

            ln1_rstd(0)
            body(0)
            with pool.Fori(1, UNITS - 1) as u:
                body(u)
            body(UNITS - 1, last=True)

        @block.scalar
        def _(act):
            act.wait_ge(consts_in, N_CONST)
            act.activation(cth[:, :], cT[:, :], ACT.Tanh, scale=0.5).then_inc(tanh_c, 1)

            def modulate(u):
                wait(act, "xnT_ready", u)
                wait(act, "vg_ready", u - 1)
                for i in range(UB):
                    b = u * UB + i
                    act.activation(hT[:, i * T:(i + 1) * T], PS[:, 0, i * T:(i + 1) * T], ACT.Identity,
                                   scale=scaleT[:, bass.ds(b, 1)], bias=shiftT[:, bass.ds(b, 1)]).then_inc(S["hT_ready"], 1)

            def gate_logs(u):
                wait(act, "z_ready", u)
                wait(act, "g_ready", u - 1)
                act.activation(g_a[:, :], PS[:, 1, :], ACT.Abs, bias=gk_b[:, 0:1]).then_inc(S["g_abs"], 1)
                wait(act, "g_abs", u)
                act.activation(g_e[:, :], g_a[:, :], ACT.Exp, scale=-1.0).then_inc(S["g_exp"], 1)
                wait(act, "g_exp", u)
                act.activation(g_l[:, :], g_e[:, :], ACT.Ln, bias=1.0).then_inc(S["g_ln"], 1)

            def decays(u):
                wait(act, "cum_ready", u)
                wait(act, "bd_ready", u - 1)
                wait(act, "kH_ready", u - 1)
                act.activation(eb[:, :], g_cum[:, :], ACT.Exp, scale=1.0 / GATE_NORM).then_inc(S["eb_ready"], 1)
                act.activation(enb[:, :], g_cum[:, :], ACT.Exp, scale=-1.0 / GATE_NORM).then_inc(S["enb_ready"], 1)

            def body(u, last=False):
                decays(u)
                wait(act, "vg_ready", u)
                wait(act, "o_ready", u - 1)
                act.activation(v_sb[:, :, :], PS[:, 4:8, 0:DV], ACT.Copy).then_inc(S["v_ready"], 1)
                wait(act, "sg_ready", u - 1)
                act.activation(tg[:, :, :], PS[:, 4:8, DV:2 * DV], ACT.Tanh, scale=0.5).then_inc(S["tanh_ready"], 1)
                if not last:
                    modulate(u + 1)
                wait(act, "kHT_ready", u)
                act.activation(kHt[:, :, :], PS[:, 2, :].rearrange("p (j c) -> p j c", j=UT), ACT.Copy)\
                   .then_inc(S["kHt_ready"], 1)
                if not last:
                    gate_logs(u + 1)
                wait(act, "o_ready", u)
                wait(act, "ss_ready", u - 1)
                act.activation(sq[:, :, :], PS[:, 4:6, :].rearrange("p k (h v) -> p (k h) v", v=GV), ACT.Square)\
                   .then_inc(S["sq_ready"], 1)
                wait(act, "oTp_ready", u)
                wait(act, "y_ready", u - 1)
                act.activation(oT[:, :, :, :].rearrange("p j e t -> p (j e t)"),
                               PS[:, 6:8, :].rearrange("p k n -> p (k n)"), ACT.Copy).then_inc(S["oT_ready"], 1)

            act.wait_ge(setup_v, 2)
            modulate(0)
            gate_logs(0)
            body(0)
            with act.Fori(1, UNITS - 1) as u:
                body(u)
            body(UNITS - 1, last=True)

        @block.vector
        def _(dve):
            dve.wait_ge(tanh_c, 1)
            dve.scalar_tensor_tensor(out=cth[:, :], in0=cth[:, :], scalar=1.0, in1=cT[:, :], op0=ALU.add, op1=ALU.mult)\
               .then_inc(silu_c, 1)
            dve.wait_ge(silu_c, 1)
            dve.tensor_scalar(csil[:, :], cth[:, :], 0.5, None, ALU.mult).then_inc(silu_c, 1)
            dve.wait_ge(setup_mm, 3)
            dve.tensor_copy(shiftT[:, :], PS[:, 0, 0:B]).then_inc(setup_v, 1)
            dve.tensor_scalar(scaleT[:, :], PS[:, 0, B:2 * B], 1.0, None, ALU.add).then_inc(setup_v, 1)
            dve.tensor_copy(w12[:, :], PS[:, 2, 0:P]).then_inc(setup_v, 1)
            rows = PS[0:B, 1, :].rearrange("b (k d) -> b k d", k=4)
            dve.tensor_copy(rowmod[:, 1, :], rows[:, 1, :]).then_inc(setup_v2, 1)
            dve.tensor_scalar(rowmod[:, 2, :], rows[:, 2, :], 1.0, None, ALU.add).then_inc(setup_v2, 1)
            for i, k in enumerate((0, 3)):
                dve.tensor_scalar(sgn[:, i, :], rows[:, k, :], 0.0, 2.0, ALU.is_ge, ALU.mult).then_inc(setup_v, 1)
                dve.tensor_scalar(rowmod[:, k, :], rows[:, k, :], -1.0, 0.25, ALU.mult, ALU.max).then_inc(setup_v, 1)
                dve.wait_ge(setup_v, 3 + 3 * i + 2)
                dve.tensor_tensor(rowmod[:, k, :], rows[:, k, :], rowmod[:, k, :], ALU.max).then_inc(setup_v, 1)
                dve.wait_ge(setup_v, 3 + 3 * i + 3)
                dve.scalar_tensor_tensor(out=rowmod[:, k, :], in0=sgn[:, i, :], scalar=-1.0, in1=rowmod[:, k, :],
                                         op0=ALU.add, op1=ALU.mult).then_inc(setup_v2, 1)
            dve.tensor_scalar(wo[:, :, :], wo[:, :, :], gnorm[:, 0:1], 0.5, ALU.mult, ALU.mult).then_inc(setup_v, 1)

            def ln1_stats(u):
                wait(dve, "xn_ready", u - 1)
                for j in range(UT):
                    dve.bn_stats(ln1_st[:, j, :], x_res[:, bass.ds(u * UT + j, 1), :].rearrange("p o d -> p (o d)"))\
                       .then_inc(S["ln1_stats"], 1)
                for j in range(UT):
                    wait(dve, "ln1_stats", u, j + 1)
                    apart(dve)
                    dve.bn_aggr(ln1_mv[:, j, :], ln1_st[:, j, :]).then_inc(S["ln1_mean"], 1)

            def ln1_apply(u):
                wait(dve, "ln1_rstd", u)
                wait(dve, "xnT_ready", u - 1)
                for j in range(UT):
                    dve.tensor_scalar(xn[:, j, :], x_res[:, bass.ds(u * UT + j, 1), :].rearrange("p o d -> p (o d)"),
                                      ln1_mv[:, j, 0:1], ln1_rs[:, j:j + 1], ALU.subtract, ALU.mult)\
                       .then_inc(S["xn_ready"], 1)

            def gate_min(u):
                wait(dve, "g_abs", u)
                dve.tensor_scalar(g_m[:, :], PS[:, 1, :], gk_b[:, 0:1], 0.0, ALU.add, ALU.min).then_inc(S["g_min"], 1)

            def gate_cumsum(u):
                wait(dve, "g_ln", u)
                wait(dve, "g_min", u)
                wait(dve, "cum_ready", u - 1)
                dve.tensor_tensor(g_g[:, :], g_m[:, :], g_l[:, :], ALU.subtract).then_inc(S["g_ready"], 1)
                wait(dve, "g_ready", u)
                wait(dve, "enb_ready", u - 1)
                wait(dve, "eb_ready", u - 1)
                dve.tensor_tensor_scan(g_cum[:, :], scan_keep[:, :], g_g[:, :], 0.0, ALU.mult, ALU.add)\
                   .then_inc(S["cum_ready"], 1)

            def body(u, last=False):
                if not last:
                    ln1_stats(u + 1)
                wait(dve, "q_ready", u)
                wait(dve, "eb_ready", u)
                wait(dve, "o_ready", u - 1)
                dve.scalar_tensor_tensor(out=qg[:, :], in0=PS[:, 2, :], scalar=float(GK) ** -0.5, in1=eb[:, :],
                                         op0=ALU.mult, op1=ALU.mult).then_inc(S["qg_ready"], 1)
                wait(dve, "k_ready", u)
                wait(dve, "enb_ready", u)
                dve.tensor_tensor(kg[:, :], PS[:, 3, :], enb[:, :], ALU.mult).then_inc(S["kg_ready"], 1)
                wait(dve, "kg_ready", u)
                wait(dve, "kHT_ready", u - 1)
                ebl = eb[:, CH - 1:UN:CH].unsqueeze(2).broadcast_to([P, UN // CH, CH])
                dve.tensor_tensor(kH[:, :].rearrange("p (c s) -> p c s", s=CH),
                                  kg[:, :].rearrange("p (c s) -> p c s", s=CH), ebl, ALU.mult).then_inc(S["kH_ready"], 1)
                if not last:
                    ln1_apply(u + 1)
                wait(dve, "tanh_ready", u)
                wait(dve, "og_ready", u - 1)
                dve.scalar_tensor_tensor(out=sg[:, :, :], in0=tg[:, :, :], scalar=1.0, in1=PS[:, 4:8, DV:2 * DV],
                                         op0=ALU.add, op1=ALU.mult).then_inc(S["sg_ready"], 1)
                for h in range(GH):
                    wait(dve, "A_ready", u, h + 1)
                    dve.tensor_tensor(att[:, h, :].rearrange("p (j t) -> p j t", j=UT),
                                      PS[:, 4 + h, :].rearrange("p (j t) -> p j t", j=UT),
                                      chunk_causal[:, :].unsqueeze(1).broadcast_to([P, UT, P]), ALU.mult)\
                       .then_inc(S["att_ready"], 1)
                wait(dve, "U_ready", u)
                even = PS[:, 0, 0:UB * 2 * GV].rearrange("p (b c v) -> p b c v", b=UB, c=2)
                odd = PS[:, 3, 0:UB * GV].rearrange("p (b v) -> p b v", b=UB)
                wait(dve, "bd_ready", u - 1)
                dve.tensor_copy(state[:, :, 0, :], even[:, :, 0, :]).then_inc(S["H_step"], 1)
                for c in (1, 2):
                    wait(dve, "H_step", u, 1 if c == 1 else 2)
                    for i in range(UB):
                        at = i * T + c * CH + CH - 1
                        ins = dve.scalar_tensor_tensor(out=state[:, i, c, :], in0=state[:, i, c - 1, :],
                                                       scalar=eb[:, at:at + 1],
                                                       in1=odd[:, i, :] if c == 1 else even[:, i, 1, :],
                                                       op0=ALU.mult, op1=ALU.add)
                        if i == UB - 1:
                            ins.then_inc(S["H_step"], 1)
                wait(dve, "H_step", u)
                dve.tensor_tensor(state_bd[:, :, :, :],
                                  state[:, :, :, :].rearrange("p b c v -> p (b c) v").unsqueeze(2)
                                  .broadcast_to([P, UB * (NCH - 1), GH, GV]),
                                  head_of_row[:, :].unsqueeze(1).unsqueeze(3)
                                  .broadcast_to([P, UB * (NCH - 1), GH, GV]), ALU.mult).then_inc(S["bd_ready"], 1)
                if not last:
                    gate_min(u + 1)
                    gate_cumsum(u + 1)
                wait(dve, "sq_ready", u)
                wait(dve, "og2_ready", u - 1)
                dve.tensor_tensor(og[:, :, :], PS[:, 4:6, :].rearrange("p k (h v) -> p (k h) v", v=GV),
                                  sg[:, :, :].rearrange("p j (h v) -> p (j h) v", v=GV), ALU.mult).then_inc(S["og_ready"], 1)
                wait(dve, "rrms_ready", u - 1)
                dve.tensor_reduce(ss[:, :], sq[:, :, :], AX.X, ALU.add).then_inc(S["ss_ready"], 1)
                wait(dve, "rrms_ready", u)
                wait(dve, "og_ready", u)
                wait(dve, "oTp_ready", u - 1)
                dve.tensor_tensor(og2[:, :, :], og[:, :, :], rrms[:, :].unsqueeze(2).broadcast_to([P, UT * GH, GV]),
                                  ALU.mult).then_inc(S["og2_ready"], 1)
                wait(dve, "y_ready", u)
                wait(dve, "x1_ready", u - 1)
                dve.wait_ge(ga_in, (u + 1) * 16)
                dve.tensor_tensor(yg[:, :, :, :], PS[:, 1, :].rearrange("p (b t d) -> p b t d", b=UB, t=TB),
                                  ga_bc[:, :, :].unsqueeze(2).broadcast_to([P, UB, TB, D]), ALU.mult)\
                   .then_inc(S["yg_ready"], 1)

            dve.wait_ge(x_head_in, 16)
            ln1_stats(0)
            ln1_apply(0)
            gate_min(0)
            gate_cumsum(0)
            body(0)
            dve.wait_ge(x_rest_in, 16)
            with dve.Fori(1, UNITS - 1) as u:
                body(u)
            body(UNITS - 1, last=True)

        @block.tensor
        def _(pe):
            pe.wait_ge(consts_in, N_CONST)
            pe.wait_ge(silu_c, 2)
            for k in range(2):
                pe.matmul(PS[:, 0, k * B:(k + 1) * B], wmod[:, k * D:(k + 1) * D], csil[:, :], start=(k == 0),
                          stop=True, skip_group_check=True)
            mm = pe.matmul(PS[0:B, 1, :], csil[:, :], wmod[:, 2 * D:6 * D], start=True, stop=True)
            mm.then_inc(setup_mm, 2)
            pe.matmul(PS[:, 2, 0:P], w1t[:, :], w2[:, :], start=True, stop=True).then_inc(setup_mm, 1)

            def normed_T(u):
                wait(pe, "xn_ready", u)
                wait(pe, "H_step", u - 2)
                wait(pe, "hT_ready", u - 1)
                for j in range(UT):
                    mm = pe.transpose(PS[:, 0, j * P:(j + 1) * P], xn[:, j, :], ident[:, :])
                mm.then_inc(S["xnT_ready"], 1)

            def gate_z(u):
                wait(pe, "hT_ready", u)
                wait(pe, "yg_ready", u - 2)
                wait(pe, "g_min", u - 1)
                pe.matmul(PS[:, 1, :], w12[:, :], hT[:, :], start=True, stop=True).then_inc(S["z_ready"], 1)

            def body(u, last=False):
                wait(pe, "kHt_ready", u - 1)
                pe.matmul(PS[:, 2, :], wq[:, :], hT[:, :], start=True, stop=True).then_inc(S["q_ready"], 1)
                wait(pe, "H_step", u - 1)
                pe.matmul(PS[:, 3, :], wk[:, :], hT[:, :], start=True, stop=True).then_inc(S["k_ready"], 1)
                wait(pe, "og_ready", u - 1)
                wait(pe, "oT_ready", u - 1)
                for j in range(UT):
                    pe.matmul(PS[:, 4 + j, :], hT[:, j * P:(j + 1) * P], wvg[:, :], start=True, stop=True)\
                      .then_inc(S["vg_ready"], 1)
                if not last:
                    normed_T(u + 1)
                    gate_z(u + 1)
                wait(pe, "kH_ready", u)
                wait(pe, "qg_ready", u)
                for j in range(UT):
                    mm = pe.transpose(PS[:, 2, j * P:(j + 1) * P], kH[:, j * P:(j + 1) * P], ident[:, :])
                mm.then_inc(S["kHT_ready"], 1)
                wait(pe, "v_ready", u)
                wait(pe, "sg_ready", u)
                for j in range(UT):
                    for h in range(GH):
                        rows = slice(h * GK, (h + 1) * GK)
                        mm = pe.matmul(PS[:, 4 + h, j * P:(j + 1) * P], kg[rows, j * P:(j + 1) * P],
                                       qg[rows, j * P:(j + 1) * P], start=True, stop=True)
                        if j == UT - 1:
                            mm.then_inc(S["A_ready"], 1)
                wait(pe, "kHt_ready", u)
                apart(pe)
                for i in range(UB):
                    for c in range(NCH - 1):
                        j, half = i * TB + c // 2, c % 2
                        col = (i * 2 + c // 2) * GV if half == 0 else i * GV
                        rows = slice(half * CH, (half + 1) * CH)
                        for h in range(GH):
                            mm = pe.matmul(PS[h * GK:(h + 1) * GK, 3 * half, col:col + GV],
                                           kHt[rows, j, h * GK:(h + 1) * GK], v_sb[rows, j, h * GV:(h + 1) * GV],
                                           start=True, stop=True, skip_group_check=True)
                mm.then_inc(S["U_ready"], 1)
                wait(pe, "att_ready", u)
                for j in range(UT):
                    for h in range(GH):
                        pe.matmul(PS[:, 4 + j // 2, (j % 2) * DV + h * GV:(j % 2) * DV + (h + 1) * GV],
                                  att[:, h, j * P:(j + 1) * P], v_sb[:, j, h * GV:(h + 1) * GV],
                                  start=(j % 2 == 0 and h == 0), stop=False, skip_group_check=True)
                wait(pe, "bd_ready", u)
                for i in range(UB):
                    for c in range(1, NCH):
                        j, half = i * TB + c // 2, c % 2
                        mm = pe.matmul(PS[half * CH:(half + 1) * CH, 4 + j // 2, (j % 2) * DV:(j % 2 + 1) * DV],
                                       qg[:, i * T + c * CH:i * T + (c + 1) * CH], state_bd[:, i * (NCH - 1) + c - 1, :, :],
                                       start=False, stop=True, skip_group_check=True)
                mm.then_inc(S["o_ready"], 1)
                wait(pe, "og2_ready", u)
                for j in range(UT):
                    for e in range(2):
                        k = j * 2 + e
                        mm = pe.transpose(PS[:, 6 + k // 4, (k % 4) * P:(k % 4 + 1) * P],
                                          og2[:, j * GH + e * 2:j * GH + e * 2 + 2, :].rearrange("p h v -> p (h v)"),
                                          ident[:, :])
                mm.then_inc(S["oTp_ready"], 1)
                wait(pe, "oT_ready", u)
                if not last:
                    wait(pe, "g_min", u + 1)
                for j in range(UT):
                    for e in range(2):
                        mm = pe.matmul(PS[:, 1, j * D:(j + 1) * D], oT[:, j, e, :], wo[:, e, :],
                                       start=(e == 0), stop=(e == 1))
                mm.then_inc(S["y_ready"], 1)

            pe.wait_ge(setup_v, 10)
            normed_T(0)
            gate_z(0)
            body(0)
            with pe.Fori(1, UNITS - 1) as u:
                body(u)
            body(UNITS - 1, last=True)


class Step:

    def __init__(self, k, c):
        self.k, self.c = k, c
        self.n = 2 * k + c

    def __add__(self, d):
        return Step(self.k, self.c + d)

    @property
    def par(self):
        return self.c % 2

    @property
    def half(self):
        return self.k + self.c // 2


FIRST, LOOP0, LOOP1, LAST = -3, 3, 29, B + 2


def turns(eng, body):
    for i in range(FIRST, LOOP0):
        body(Step(0, i), lambda lag, i=i: 0 <= i + lag < B)
    with eng.Fori(0, (LOOP1 - LOOP0) // 2) as k:
        for r in range(2):
            body(Step(k, LOOP0 + r), lambda lag: True)
    for i in range(LOOP1, LAST + 1):
        body(Step(0, i), lambda lag, i=i: 0 <= i + lag < B)


def feed_forward(nc, a, out, x_res, ident, mhalf, rowmod_dram, consts_in, n_const):
    NORM, PROJ, MAXI, PROB, TAIL, EXPS, OUT = 3, 2, 1, 0, -1, -2, -3
    SLOTS = 8
    with ExitStack() as ctx:
        def sb(name, shape, dt=F32):
            return ctx.enter_context(nc.sbuf_tensor(name, shape, dt))

        def sem(name):
            return ctx.enter_context(nc.semaphore(name))

        r_res = sb("r_res", [P, B * TB, D])
        rope_cos = sb("rope_cos_sb", [P, T])
        rope_sin = sb("rope_sin_sb", [P, T])
        above_f = sb("above_f", [P, P])
        above = sb("above_sb", [P, P], BF16)
        ident_b = sb("ident_b", [P, P], BF16)
        cum_keep = sb("cum_keep", [P, TB * NE])
        wq2 = sb("wq2", [D, P + P // 2])
        wuk2 = sb("wuk2", [LAT, P + P // 2])
        wdkv = sb("wdkv", [D, LAT])
        wuv = sb("wuv", [LAT, P])
        wo2 = sb("wo2", [P, D])
        n1w = sb("n1w", [D, 1])
        n2w = sb("n2w", [D, 1])
        lng = sb("lng", [LAT, 1])
        lnb = sb("lnb", [LAT, 1])
        gw = sb("gw", [D, NE])
        gb4 = sb("gb4", [P, TB, NE])
        w1 = sb("w1", [D, NE * HID])
        w2 = sb("w2e", [P, NE * HT, D])
        b1 = sb("b1", [P, NE * HT])
        b2 = sb("b2", [NE, D])
        off_f = sb("off_f", [NE, NE])
        off = sb("off_sb", [NE, NE, P], BF16)

        ln_st = sb("ln_st", [P, TB, 6])
        ln_mv = sb("ln_mv", [P, TB, 2])
        ln_ve = sb("ln_ve", [P, TB])
        ln_rs = sb("ln_rs", [P, TB])
        xn = sb("xn2", [P, TB, D])
        xc = sb("xc2", [P, TB, D])
        mod_bc = sb("mod_bc", [P, 2, D])
        gb_bc = sb("gb_bc", [P, D])
        sqj = sb("sqj", [P, TB, D])
        s1 = sb("s1", [P, TB])
        s1e = sb("s1e", [P, TB])
        s1r = sb("s1r", [P, TB])
        a1 = sb("a1", [P, TB, D])
        a1T = sb("a1T", [D, T])
        la_st = sb("la_st", [P, TB, 6])
        la_mv = sb("la_mv", [P, TB, 2])
        la_ve = sb("la_ve", [P, TB])
        la_rs = sb("la_rs", [P, TB])
        la = sb("la", [P, TB, LAT])
        laT = sb("laT", [LAT, T])
        rt1 = sb("rt1", [P, 2, T])
        rt2 = sb("rt2", [P, 2, T])
        rt = sb("rt", [P, 2, T])
        rr = sb("rr", [P, 2, T])
        parts = sb("parts", [P, 3, 2, T], BF16)
        v1 = [sb(f"v1_{n}", [P, TB, MH, 32]) for n in range(2)]
        qs = [sb(f"qs{n}", [64, MH, T], BF16) for n in range(2)]
        ks = [sb(f"ks{n}", [64, MH, T], BF16) for n in range(2)]
        nm = sb("nm", [P, TB, MH])
        nr = sb("nr", [P, TB, MH])
        nparts = sb("nparts", [P, TB, 3, MH], BF16)
        nT = sb("nT", [3 * MH, T], BF16)
        pexp = sb("pexp", [P, 2, 1536])
        o_sb = sb("o_sb", [P, 4, T])
        rec = sb("rec", [P, TB, MH])
        on = sb("on", [P, TB, MH * MD])
        onT = sb("onT", [P, T])
        sqk = sb("sqk", [P, TB, D])
        s2 = sb("s2", [P, TB])
        s2e = sb("s2e", [P, TB])
        s2r = sb("s2r", [P, TB])
        a2 = sb("a2", [P, TB, D])
        a2T = [sb(f"a2T_{n}", [D, T]) for n in range(2)]
        lg = sb("lg", [P, TB, NE])
        lmax = sb("lmax", [P, TB])
        hit = sb("hit", [P, TB, NE])
        hits = sb("hits", [P, TB, NE])
        pick = sb("pick", [P, TB, NE])
        pickT = [sb(f"pickT_{n}", [NE, T]) for n in range(2)]
        missT = [sb(f"missT_{n}", [NE, T], BF16) for n in range(2)]
        hs = sb("hs", [P, 2, 2, T])
        yr = sb("yr", [P, TB, D])
        yg = sb("yg2", [P, TB, D])
        res = sb("res", [P, TB, D])

        PS = ctx.enter_context(nc.psum_tensor("PS2", [P, 8, 512], F32))
        PB, XB, OB, WB, ZB, YB, MB = (0, 1), 2, 3, 4, 5, 6, 7

        parts_dram = nc.dram_tensor("parts_dram", (B, 2, 3 * MD, MH, T), BF16, kind="Internal").ap()
        negmax_dram = nc.dram_tensor("negmax_dram", (B, 3, MH, T), BF16, kind="Internal").ap()

        w_in = sem("w_in")
        w_set = sem("w_set")
        pool_set = sem("pool_set")
        act_set = sem("act_set")
        mod_in = sem("mod_in")
        gb_in = sem("gb_in")
        parts_out = [sem("parts_out0"), sem("parts_out1")]
        stack_in = [sem("stack_in0"), sem("stack_in1")]
        negmax_out = sem("negmax_out")
        negmax_in = sem("negmax_in")
        res_out = sem("res_out")
        own = sem("own2")
        PER = {"f_stats": TB, "f_mean": TB, "f_xn": TB, "f_sq": TB, "a1_ready": TB, "la_stats": TB, "la_mean": TB,
               "la_ready": TB, "max_mm": 12, "max_ready": 12, "prob_mm": 12, "prob_ready": 12, "diag_ready": 8,
               "pv_done": 4, "o_ready": 4, "OT_mm": TB, "rec_ready": TB, "on_ready": TB, "rt1_ready": 2, "rt2_ready": 2,
               "rt_ready": 2, "p0_ready": 2, "rr1_ready": 2, "p1_ready": 2, "parts_ready": 2, "t_sq": TB, "a2_ready": TB, "z_ready": 8, "h_ready": 8, "h_used": 8}
        NAMES = ("f_stats f_mean f_eps f_rstd f_xn f_scaled h_ready2 f_sq f_eps2 f_rstd2 a1_ready a1Tp a1T_ready lat_mm "
                 "la_stats la_mean la_eps la_rstd la_ready laTp laT_ready q_mm k_mm rt1_ready rt2_ready rt_ready p0_ready rr1_ready "
                 "p1_ready parts_ready v_mm v_ready max_mm max_ready n_0 n_r1 n_1 n_ready nTp nT_ready prob_mm prob_ready "
                 "diag_ready pv_done o_ready OT_mm rec_ready on_ready onTp onT_ready wo_mm r_ready t_sq t_eps t_rstd "
                 "a2_ready a2Tp a2T_ready lg_mm lg_ready lmax_ready hit_ready hits_ready pick_ready pickTp pickT_ready missT_ready "
                 "z_ready h_ready h_used y_mm yr_ready yg_ready res_ready").split()
        S = {n: sem("ff_" + n) for n in NAMES}

        def wait(eng, name, s, k=None):
            per = PER.get(name, 1)
            k = per if k is None else k
            if isinstance(s.n, int) and s.n * per + k <= 0:
                return
            eng.wait_ge(S[name], s.n * per + k)

        def apart(eng):
            eng.sem_inc(own, 1)

        block = ctx.enter_context(nc.Block())
        LOADS = [(rope_cos, "rope_cos"), (rope_sin, "rope_sin"), (above_f, "above"), (wq2, "wq2"), (wuk2, "wuk2"),
                 (cum_keep, "first_of_four"), (wdkv, "wdkv"), (wuv, "wuv"), (wo2, "wo2"), (n1w, "n1w"), (n2w, "n2w"),
                 (lng, "lng"), (lnb, "lnb"), (gw, "gw"), (w1, "w1"), (b1, "b1"), (b2, "b2"), (off_f, "off")]
        N_W = 16 * (len(LOADS) + 2)

        @block.sync
        def _(sp):
            for dst, name in LOADS:
                sp.dma_start(dst[:, :], a[name]).then_inc(w_in, 16)
            sp.dma_start(gb4[:, :, :], a["gate_b"].unsqueeze(0).broadcast_to([P, TB, NE])).then_inc(w_in, 16)
            sp.dma_start(w2[:, :, :], a["w2e"].rearrange("(h p) n -> p h n", p=P)).then_inc(w_in, 16)
            sp.wait_ge(pool_set, 2)

            def body(i, on_):
                if on_(OUT):
                    s = i + OUT
                    wait(sp, "yg_ready", s + -1)
                    sp.dma_start(gb_bc[:, :], rowmod_dram[bass.ds(s.n, 1), 3, :].broadcast_to([P, D])).then_inc(gb_in, 16)
                if on_(NORM):
                    s = i + NORM
                    wait(sp, "h_ready2", s + -1)
                    sp.dma_start(mod_bc[:, :, :], rowmod_dram[bass.ds(s.n, 1), 1:3, :].broadcast_to([P, 2, D]))\
                      .then_inc(mod_in, 16)
                if on_(OUT):
                    s = i + OUT
                    wait(sp, "res_ready", s)
                    sp.dma_start(out[bass.ds(s.n, 1)].rearrange("o (t p) d -> p (o t) d", p=P), res[:, :, :])\
                      .then_inc(res_out, 16)
                if on_(PROJ):
                    s = i + PROJ
                    for x in range(2):
                        wait(sp, "parts_ready", s, x + 1)
                        sp.dma_start(parts_dram[bass.ds(s.n, 1), x].rearrange("o (a d) h t -> (o d h) a t", a=3),
                                     parts[:, :, x, :]).then_inc(parts_out[s.par], 16)
                if on_(MAXI):
                    s = i + MAXI
                    wait(sp, "nT_ready", s)
                    dst = negmax_dram[bass.ds(s.n, 1)]
                    sp.dma_start(dst.rearrange("o a h t -> (o a h) t"), nT[:, :]).then_inc(negmax_out, 16)
                if on_(PROJ):
                    s = i + PROJ
                    sp.wait_ge(parts_out[s.par], 32 * (s.half + 1))
                    wait(sp, "prob_mm", s + -2)
                    sin = stack_in[s.par]
                    src = parts_dram[bass.ds(s.n, 1)].rearrange("o a r h t -> (o a) r (h t)")
                    q, k = src[0], src[1]
                    qd, kd = (x[:, :, :].rearrange("r h t -> r (h t)") for x in (qs[s.par], ks[s.par]))
                    sp.dma_start(qd[0:24, :], q[0:24, :]).then_inc(sin, 16)
                    sp.dma_start(qd[24:40, :], q[0:16, :]).then_inc(sin, 16)
                    sp.dma_start(qd[40:48, :], q[0:8, :]).then_inc(sin, 16)
                    for row, part in ((0, 0), (8, 0), (16, 0), (24, 1), (32, 1), (40, 2)):
                        sp.dma_start(kd[row:row + 8, :], k[part * 8:part * 8 + 8, :]).then_inc(sin, 16)
                if on_(MAXI):
                    s = i + MAXI
                    sp.wait_ge(negmax_out, 16 * (s.n + 1))
                    wait(sp, "prob_mm", s + -2)
                    sp.dma_start(qs[s.par][KROWS:KROWS + 3, :, :].rearrange("r h t -> r (h t)"),
                                 negmax_dram[bass.ds(s.n, 1)].rearrange("o a h t -> (o a) (h t)")).then_inc(negmax_in, 16)
            turns(sp, body)
            sp.wait_ge(res_out, 16 * B)

        @block.gpsimd
        def _(pool):
            fills = [(ks[n][32:64, :, :], 1.0) for n in range(2)]
            fills += [(v1[n][:, :, :, :], 0.0) for n in range(2)] + [(v1[n][:, :, :, MD:MD + 1], 1.0) for n in range(2)]
            for n, (where, value) in enumerate(fills):
                if n > 0:
                    pool.wait_ge(pool_set, n)
                pool.memset(where, value).then_inc(pool_set, 1)

            def rstd(s, src, ve, rs, eps, scale, got, stepped, done, used):
                wait(pool, got, s)
                apart(pool)
                pool.tensor_scalar(ve[:, :], src, scale, eps, ALU.mult, ALU.add).then_inc(S[stepped], 1)
                wait(pool, used, s + -1)
                wait(pool, stepped, s)
                pool.tensor_tensor(rs[:, :], ve[:, :], mhalf[:, 0:TB], ALU.pow).then_inc(S[done], 1)

            def keys_after_queries(s, hg, x):
                wait(pool, "prob_ready", s, 3 * hg + 2 + x)
                apart(pool)
                buf = pexp[:, hg % 2, 1024 * x:1024 + 512 * x].rearrange("p (h q) -> p h q", h=4)[:, :, 0:P]
                pool.affine_select(out=buf, in_=buf, compare_op=ALU.is_ge, fill=0.0, base=0,
                                   pattern=[[0, 4], [1, P]], channel_multiplier=-1).then_inc(S["diag_ready"], 1)

            def rotated(s, x):
                wait(pool, "rt1_ready", s, x + 1)
                wait(pool, "rt2_ready", s, x + 1)
                wait(pool, "rr1_ready", s + -1, x + 1)
                wait(pool, "p0_ready", s + -1, x + 1)
                pool.tensor_tensor(rt[:, x, :], rt1[:, x, :], rt2[:, x, :], ALU.add).then_inc(S["rt_ready"], 1)

            def body(i, on_):
                for j in range(SLOTS):
                    if on_(PROB):
                        keys_after_queries(i + PROB, j // 2, j % 2)
                    if j == 0 and on_(NORM):
                        s = i + NORM
                        rstd(s, ln_mv[:, :, 1], ln_ve, ln_rs, EPS, 1.0, "f_mean", "f_eps", "f_rstd", "f_xn")
                    if j == 1 and on_(OUT):
                        s = i + OUT
                        wait(pool, "yr_ready", s)
                        pool.wait_ge(gb_in, 16 * (s.n + 1))
                        wait(pool, "res_ready", s + -1)
                        pool.tensor_tensor(yg[:, :, :], yr[:, :, :], gb_bc[:, :].unsqueeze(1).broadcast_to([P, TB, D]),
                                           ALU.mult).then_inc(S["yg_ready"], 1)
                        wait(pool, "yg_ready", s)
                        if not isinstance(s.n, int) or s.n > 0:
                            pool.wait_ge(res_out, 16 * s.n)
                        pool.tensor_tensor(res[:, :, :], yg[:, :, :], x_res[:, bass.ts(s.n, TB), :], ALU.add)\
                            .then_inc(S["res_ready"], 1)
                    if j == 2 and on_(PROJ):
                        s = i + PROJ
                        rstd(s, la_mv[:, :, 1], la_ve, la_rs, EPS, 1.0, "la_mean", "la_eps", "la_rstd", "la_ready")
                    if j == 2 and on_(NORM):
                        s = i + NORM
                        pool.wait_ge(mod_in, 16 * (s.n + 1))
                        wait(pool, "f_xn", s)
                        pool.tensor_tensor(xc[:, :, :], xn[:, :, :], mod_bc[:, 1:2, :].broadcast_to([P, TB, D]), ALU.mult)\
                            .then_inc(S["f_scaled"], 1)
                        wait(pool, "f_scaled", s)
                        pool.tensor_tensor(r_res[:, bass.ts(s.n, TB), :], xc[:, :, :],
                                           mod_bc[:, 0:1, :].broadcast_to([P, TB, D]), ALU.add).then_inc(S["h_ready2"], 1)
                    if j == 3 and on_(PROJ):
                        rotated(i + PROJ, 0)
                    if j == 4 and on_(PROJ):
                        rotated(i + PROJ, 1)
                    if j == 5 and on_(TAIL):
                        s = i + TAIL
                        rstd(s, s2[:, :], s2e, s2r, EPS_RMS, 1.0 / D, "t_sq", "t_eps", "t_rstd", "a2_ready")
                    if j == 5 and on_(NORM):
                        s = i + NORM
                        rstd(s, s1[:, :], s1e, s1r, EPS_RMS, 1.0 / D, "f_sq", "f_eps2", "f_rstd2", "a1_ready")
            turns(pool, body)

        @block.scalar
        def _(act):
            act.wait_ge(w_in, N_W)
            act.activation(above[:, :], above_f[:, :], ACT.Copy).then_inc(act_set, 1)
            act.activation(ident_b[:, :], ident[:, :], ACT.Copy).then_inc(act_set, 1)
            act.activation(off[:, :, :], off_f[:, :].unsqueeze(2).broadcast_to([NE, NE, P]), ACT.Copy).then_inc(act_set, 1)
            act.wait_ge(pool_set, 6)
            act.wait_ge(w_set, 4)

            def hidden(s, p):
                wait(act, "z_ready", s, p + 1)
                wait(act, "h_used", s, p + 1 - 2)
                for m in range(2):
                    ins = act.activation(hs[:, p % 2, m, :], PS[:, ZB, m * T:(m + 1) * T], ACT.Relu,
                                         bias=b1[:, 2 * p + m:2 * p + m + 1])
                ins.then_inc(S["h_ready"], 1)

            def exponentials(s, g):
                hg, x = g // 3, g % 3
                wait(act, "prob_mm", s, g + 1)
                wait(act, "pv_done", s, hg + 1 - 2)
                act.activation(pexp[:, hg % 2, x * 512:(x + 1) * 512], PS[:, PB[g % 2], :], ACT.Exp,
                               scale=float(MD) ** -0.5).then_inc(S["prob_ready"], 1)

            def values_out(s, hg):
                wait(act, "pv_done", s, hg + 1)
                wait(act, "OT_mm", s + -1)
                act.activation(o_sb[:, hg, :], PS[:, OB, (hg % 2) * T:(hg % 2 + 1) * T], ACT.Copy)\
                   .then_inc(S["o_ready"], 1)

            def part(s, x, a, src, source_ready, done):
                wait(act, source_ready, s, x + 1)
                if not isinstance(s.n, int) or s.n >= 1:
                    act.wait_ge(parts_out[(s + -1).par], 32 * ((s + -1).half + 1))
                act.activation(parts[:, a, x, :], src[:, x, :], ACT.Copy).then_inc(S[done], 1)

            def squares(s, ready, used, junk, sums, done):
                wait(act, ready, s)
                wait(act, used, s + -1)
                for t in range(TB):
                    act.activation(junk[:, t, :], r_res[:, bass.ds(s.n * TB + t, 1), :].rearrange("p o d -> p (o d)"),
                                   ACT.Square, accum_out=sums[:, t:t + 1]).then_inc(S[done], 1)

            def copied(s, made, used_by, dst, src, done):
                wait(act, made, s)
                wait(act, *used_by)
                act.activation(dst, src, ACT.Copy).then_inc(S[done], 1)

            def body(i, on_):
                for j in range(SLOTS):
                    if on_(PROB):
                        for g in ((3 * (j // 2), 3 * (j // 2) + 1) if j % 2 == 0 else (3 * (j // 2) + 2,)):
                            exponentials(i + PROB, g)
                    if on_(EXPS):
                        hidden(i + EXPS, j)
                    if j == 0 and on_(PROJ):
                        s = i + PROJ
                        copied(s, "a1Tp", ("q_mm", s + -1), a1T[:, :], PS[:, MB, 0:T], "a1T_ready")
                    if j == 2 and on_(PROJ):
                        s = i + PROJ
                        wait(act, "laTp", s)
                        wait(act, "v_mm", s + -1)
                        act.activation(laT[:, :], PS[0:LAT, MB, 0:T], ACT.Identity, scale=lng[:, 0:1], bias=lnb[:, 0:1])\
                           .then_inc(S["laT_ready"], 1)
                    if j == 3 and on_(TAIL):
                        s = i + TAIL
                        copied(s, "onTp", ("wo_mm", s + -1), onT[:, :], PS[:, MB, 0:T], "onT_ready")
                    if j == 3 and on_(NORM):
                        squares(i + NORM, "h_ready2", "f_eps2", sqj, s1, "f_sq")
                    if j == 4 and on_(PROJ):
                        part(i + PROJ, 0, 0, rt, "rt_ready", "p0_ready")
                    if j == 4 and on_(TAIL):
                        squares(i + TAIL, "r_ready", "t_eps", sqk, s2, "t_sq")
                    if j == 5 and on_(PROJ):
                        part(i + PROJ, 1, 0, rt, "rt_ready", "p0_ready")
                        part(i + PROJ, 0, 1, rr, "rr1_ready", "p1_ready")
                    if j == 6 and on_(PROJ):
                        part(i + PROJ, 1, 1, rr, "rr1_ready", "p1_ready")
                    if j == 6 and on_(TAIL):
                        s = i + TAIL
                        copied(s, "a2Tp", ("z_ready", s + -2), a2T[s.par][:, :], PS[:, MB, 0:T], "a2T_ready")
                    if j in (2, 4, 6) and on_(PROB):
                        values_out(i + PROB, j // 2 - 1)
                    if j == 6 and on_(MAXI):
                        s = i + MAXI
                        wait(act, "nTp", s)
                        if not isinstance(s.n, int) or s.n > 0:
                            act.wait_ge(negmax_out, 16 * s.n)
                        act.activation(nT[:, :], PS[0:3 * MH, MB, 0:T // 2].bitcast(BF16), ACT.Copy)\
                           .then_inc(S["nT_ready"], 1)
                    if j == 7 and on_(TAIL):
                        s = i + TAIL
                        wait(act, "pickTp", s)
                        wait(act, "y_mm", s + -2)
                        act.activation(pickT[s.par][:, :], PS[0:NE, MB, 0:T], ACT.Copy).then_inc(S["pickT_ready"], 1)
                        act.activation(missT[s.par][:, :], PS[0:NE, MB, 0:T], ACT.Copy, scale=1.0, bias=-1.0)\
                           .then_inc(S["missT_ready"], 1)
                    if j == 7 and on_(PROB):
                        values_out(i + PROB, 3)
                    if j == 7 and on_(PROJ):
                        s = i + PROJ
                        wait(act, "v_mm", s)
                        wait(act, "pv_done", s + -2)
                        act.activation(v1[s.par][:, :, :, 0:MD], PS[:, MB, 0:T].rearrange("p (t h d) -> p t h d", t=TB, h=MH),
                                       ACT.Copy).then_inc(S["v_ready"], 1)
            turns(act, body)

        @block.vector
        def _(dve):
            dve.wait_ge(w_in, N_W)
            dve.tensor_scalar(wq2[:, :], wq2[:, :], n1w[:, 0:1], None, ALU.mult).then_inc(w_set, 1)
            dve.tensor_scalar(wdkv[:, :], wdkv[:, :], n1w[:, 0:1], None, ALU.mult).then_inc(w_set, 1)
            dve.tensor_scalar(gw[:, :], gw[:, :], n2w[:, 0:1], None, ALU.mult).then_inc(w_set, 1)
            dve.tensor_scalar(w1[:, :], w1[:, :], n2w[:, 0:1], None, ALU.mult).then_inc(w_set, 1)

            def norm_stats(s, tile_of, st, mv, stats, mean, used):
                wait(dve, used, s + -1)
                for t in range(TB):
                    dve.bn_stats(st[:, t, :], tile_of(t)).then_inc(S[stats], 1)
                for t in range(TB):
                    wait(dve, stats, s, t + 1)
                    apart(dve)
                    dve.bn_aggr(mv[:, t, :], st[:, t, :]).then_inc(S[mean], 1)

            def r_tile(s, t):
                return r_res[:, bass.ds(s.n * TB + t, 1), :].rearrange("p o d -> p (o d)")

            def x_tile(s, t):
                return x_res[:, bass.ds(s.n * TB + t, 1), :].rearrange("p o d -> p (o d)")

            def maximum(s, g):
                wait(dve, "n_ready", s + -1)
                wait(dve, "max_mm", s, g + 1)
                to, heads = (nm[:, 0, 4 * g:4 * g + 4], 4) if g < 4 else (nm[:, 1, 2 * g - 8:2 * g - 6], 2)
                dve.tensor_reduce(to, PS[:, XB, :].rearrange("p (h k) -> p h k", h=heads), AX.X, ALU.max, negate=True)\
                   .then_inc(S["max_ready"], 1)

            def normalised(s, t):
                ot = PS[:, WB, :].rearrange("p (h c) -> p h c", c=32)
                wait(dve, "OT_mm", s, t + 1)
                wait(dve, "on_ready", s + -1, t + 1)
                dve.reciprocal(rec[:, t, :], ot[:, :, MD]).then_inc(S["rec_ready"], 1)
                wait(dve, "rec_ready", s, t + 1)
                wait(dve, "onTp", s + -1)
                dve.tensor_tensor(on[:, t, :].rearrange("p (h d) -> p h d", d=MD), ot[:, :, 0:MD],
                                  rec[:, t, :].unsqueeze(2).broadcast_to([P, MH, MD]), ALU.mult).then_inc(S["on_ready"], 1)

            def rotate(s, x, made):
                wait(dve, made, s)
                wait(dve, "rt_ready", s + -1, x + 1)
                dve.tensor_tensor(rt1[:, x, :], PS[:, WB, 0:T], rope_cos[:, :], ALU.mult).then_inc(S["rt1_ready"], 1)
                dve.tensor_tensor(rt2[:, x, :], PS[:, WB, T:2 * T], rope_sin[:, :], ALU.mult).then_inc(S["rt2_ready"], 1)

            def rest_of(s, x):
                wait(dve, "p0_ready", s, x + 1)
                wait(dve, "p1_ready", s + -1, x + 1)
                dve.tensor_tensor(rr[:, x, :], rt[:, x, :], parts[:, 0, x, :], ALU.subtract).then_inc(S["rr1_ready"], 1)

            def last_part(s, x):
                wait(dve, "p1_ready", s, x + 1)
                if not isinstance(s.n, int) or s.n >= 1:
                    dve.wait_ge(parts_out[(s + -1).par], 32 * ((s + -1).half + 1))
                dve.tensor_tensor(parts[:, 2, x, :], rr[:, x, :], parts[:, 1, x, :], ALU.subtract)\
                   .then_inc(S["parts_ready"], 1)

            def body(i, on_):
                for j in range(SLOTS):
                    if j < 6 and on_(MAXI):
                        maximum(i + MAXI, 2 * j)
                    if j == 0 and on_(OUT):
                        s = i + OUT
                        wait(dve, "y_mm", s)
                        wait(dve, "yg_ready", s + -1)
                        dve.tensor_tensor(yr[:, :, :], PS[:, YB, 0:T].rearrange("p (t d) -> p t d", t=TB),
                                          r_res[:, bass.ts(s.n, TB), :], ALU.add).then_inc(S["yr_ready"], 1)
                    if j < 2 and on_(TAIL):
                        normalised(i + TAIL, j)
                    if j == 0 and on_(NORM):
                        s = i + NORM
                        norm_stats(s, lambda t: x_tile(s, t), ln_st, ln_mv, "f_stats", "f_mean", "f_xn")
                    if j == 1 and on_(NORM):
                        s = i + NORM
                        wait(dve, "f_rstd", s)
                        wait(dve, "f_scaled", s + -1)
                        for t in range(TB):
                            dve.tensor_scalar(xn[:, t, :], x_tile(s, t), ln_mv[:, t, 0:1], ln_rs[:, t:t + 1],
                                              ALU.subtract, ALU.mult).then_inc(S["f_xn"], 1)
                    lat = PS[:, MB, 0:TB * LAT].rearrange("p (t c) -> p t c", t=TB)
                    if j == 2 and on_(PROJ):
                        s = i + PROJ
                        wait(dve, "lat_mm", s)
                        norm_stats(s, lambda t: lat[:, t, :], la_st, la_mv, "la_stats", "la_mean", "la_ready")
                    if j == 3 and on_(PROJ):
                        rotate(i + PROJ, 0, "q_mm")
                    if j == 4 and on_(PROJ):
                        rotate(i + PROJ, 1, "k_mm")
                    if j == 5 and on_(PROJ):
                        rest_of(i + PROJ, 0)
                        rest_of(i + PROJ, 1)
                    if j < 6 and on_(MAXI):
                        maximum(i + MAXI, 2 * j + 1)
                    if j == 2 and on_(PROJ):
                        s = i + PROJ
                        wait(dve, "la_rstd", s)
                        wait(dve, "laTp", s + -1)
                        for t in range(TB):
                            dve.tensor_scalar(la[:, t, :], lat[:, t, :], la_mv[:, t, 0:1], la_rs[:, t:t + 1], ALU.subtract,
                                              ALU.mult).then_inc(S["la_ready"], 1)
                    if j == 4 and on_(TAIL):
                        s = i + TAIL
                        wait(dve, "wo_mm", s)
                        h = r_res[:, bass.ts(s.n, TB), :]
                        dve.tensor_tensor(h, h, PS[:, MB, 0:T].rearrange("p (t d) -> p t d", t=TB), ALU.add)\
                           .then_inc(S["r_ready"], 1)
                    if j == 6 and on_(MAXI):
                        s = i + MAXI
                        wait(dve, "max_ready", s)
                        wait(dve, "nTp", s + -1)
                        dve.tensor_copy(nparts[:, :, 0, :], nm[:, :, :]).then_inc(S["n_0"], 1)
                        wait(dve, "n_0", s)
                        dve.tensor_tensor(nr[:, :, :], nm[:, :, :], nparts[:, :, 0, :], ALU.subtract).then_inc(S["n_r1"], 1)
                        wait(dve, "n_r1", s)
                        dve.tensor_copy(nparts[:, :, 1, :], nr[:, :, :]).then_inc(S["n_1"], 1)
                        wait(dve, "n_1", s)
                        dve.tensor_tensor(nparts[:, :, 2, :], nr[:, :, :], nparts[:, :, 1, :], ALU.subtract)\
                           .then_inc(S["n_ready"], 1)
                    if j == 5 and on_(TAIL):
                        s = i + TAIL
                        wait(dve, "t_rstd", s)
                        wait(dve, "a2Tp", s + -1)
                        for t in range(TB):
                            dve.tensor_scalar(a2[:, t, :], r_tile(s, t), s2r[:, t:t + 1], None, ALU.mult)\
                               .then_inc(S["a2_ready"], 1)
                    if j == 6 and on_(PROJ):
                        last_part(i + PROJ, 0)
                        last_part(i + PROJ, 1)
                    if j == 6 and on_(NORM):
                        s = i + NORM
                        wait(dve, "f_rstd2", s)
                        wait(dve, "a1Tp", s + -1)
                        for t in range(TB):
                            dve.tensor_scalar(a1[:, t, :], r_tile(s, t), s1r[:, t:t + 1], None, ALU.mult)\
                               .then_inc(S["a1_ready"], 1)
                    if j == 7 and on_(TAIL):
                        s = i + TAIL
                        wait(dve, "lg_mm", s)
                        dve.tensor_tensor(lg[:, :, :], PS[:, MB, 0:TB * NE].rearrange("p (t e) -> p t e", t=TB), gb4[:, :, :],
                                          ALU.add).then_inc(S["lg_ready"], 1)
                        wait(dve, "lg_ready", s)
                        dve.tensor_reduce(lmax[:, :], lg[:, :, :], AX.X, ALU.max).then_inc(S["lmax_ready"], 1)
                        wait(dve, "lmax_ready", s)
                        dve.tensor_tensor(hit[:, :, :], lg[:, :, :], lmax[:, :].unsqueeze(2).broadcast_to([P, TB, NE]),
                                          ALU.is_ge).then_inc(S["hit_ready"], 1)
                        wait(dve, "hit_ready", s)
                        apart(dve)
                        dve.tensor_tensor_scan(hits[:, :, :].rearrange("p t e -> p (t e)"), cum_keep[:, :],
                                               hit[:, :, :].rearrange("p t e -> p (t e)"), 0.0, ALU.mult, ALU.add)\
                           .then_inc(S["hits_ready"], 1)
                        wait(dve, "hits_ready", s)
                        wait(dve, "pickTp", s + -1)
                        dve.scalar_tensor_tensor(out=pick[:, :, :], in0=hits[:, :, :], scalar=1.0, in1=hit[:, :, :],
                                                 op0=ALU.is_equal, op1=ALU.mult).then_inc(S["pick_ready"], 1)
            turns(dve, body)

        @block.tensor
        def _(pe):
            pe.wait_ge(w_in, N_W)
            pe.wait_ge(w_set, 4)
            pe.wait_ge(act_set, 3)

            def values_back(s, p):
                wait(pe, "h_ready", s, p + 1)
                if p == 0:
                    wait(pe, "yr_ready", s + -1)
                for m in range(2):
                    for t in range(TB):
                        mm = pe.matmul(PS[:, YB, t * D:(t + 1) * D], hs[:, p % 2, m, t * P:(t + 1) * P],
                                       w2[:, 2 * p + m, :], start=(p == 0 and m == 0 and t == 0), stop=False,
                                       skip_group_check=True)
                mm.then_inc(S["h_used"], 1)

            def hidden(s, p):
                if p == 0:
                    wait(pe, "missT_ready", s)
                wait(pe, "h_ready", s, p)
                for m in range(2):
                    pe.matmul(PS[:, ZB, m * T:(m + 1) * T], w1[:, (2 * p + m) * P:(2 * p + m + 1) * P], a2T[s.par][:, :],
                              start=(m == 0), stop=False, skip_group_check=True)
                pe.matmul(PS[:, ZB, :].rearrange("p (m t) -> p m t", m=2), off[:, 2 * p // HT, :],
                          missT[s.par][:, :].unsqueeze(1).broadcast_to([NE, 2, T]), start=False, stop=True,
                          skip_group_check=True).then_inc(S["z_ready"], 1)

            def chain_T(s, src, tiles, width, name):
                for t in range(tiles):
                    mm = pe.transpose(PS[0:width, MB, t * P:(t + 1) * P], src(t), ident[:, :])
                mm.then_inc(S[name], 1)

            def scores_for_exp(s, hg, x):
                q, k = qs[s.par], ks[s.par]
                R = KROWS + MROWS
                g = 3 * hg + x
                if g == 0:
                    pe.wait_ge(negmax_in, 16 * (s.n + 1))
                wait(pe, "prob_ready", s, g + 1 - 2)
                bank = PS[:, PB[g % 2], :]
                if x < 2:
                    for c in range(2):
                        mm = pe.matmul(bank[:, c * T:(c + 1) * T], k[0:R, 4 * hg + 2 * x + c, 0:P],
                                       q[0:R, 4 * hg + 2 * x + c, :], start=True, stop=True)
                else:
                    for c in range(4):
                        mm = pe.matmul(bank[:, c * P:(c + 1) * P], k[0:R, 4 * hg + c, P:2 * P],
                                       q[0:R, 4 * hg + c, P:2 * P], start=True, stop=True)
                mm.then_inc(S["prob_mm"], 1)

            def values(s, hg):
                if hg == 0:
                    wait(pe, "v_ready", s)
                wait(pe, "diag_ready", s, 2 * hg + 2)
                wait(pe, "prob_ready", s, 3 * hg + 3)
                wait(pe, "o_ready", s, hg + 1 - 2)
                for kt in range(TB):
                    for c in range(4):
                        if kt == 0:
                            o, pr = slice((hg % 2) * T, (hg % 2 + 1) * T), slice(c * T, (c + 1) * T)
                        else:
                            o, pr = slice((hg % 2) * T + P, (hg % 2 + 1) * T), slice(4 * T + c * P, 4 * T + (c + 1) * P)
                        mm = pe.matmul(PS[32 * c:32 * c + 32, OB, o], v1[s.par][:, kt, 4 * hg + c, :],
                                       pexp[:, hg % 2, pr], start=(kt == 0), stop=(kt == 1), skip_group_check=True)
                mm.then_inc(S["pv_done"], 1)

            def scores_for_max(s, g):
                q, k = qs[s.par], ks[s.par]
                if g == 0:
                    pe.wait_ge(stack_in[s.par], 144 * (s.half + 1))
                wait(pe, "max_ready", s, g)
                bank = PS[:, XB, :]
                if g < 4:
                    pe.matmul(bank.rearrange("p (h k) -> p h k", h=4), ident_b[:, :],
                              above[:, :].unsqueeze(1).broadcast_to([P, 4, P]), start=True, stop=False,
                              skip_group_check=True)
                    for c in range(4):
                        mm = pe.matmul(bank[:, c * P:(c + 1) * P], q[0:KROWS, 4 * g + c, 0:P],
                                       k[0:KROWS, 4 * g + c, 0:P], start=False, stop=True, skip_group_check=True)
                else:
                    pe.matmul(bank.rearrange("p (h k) -> p h k", h=2)[:, :, P:2 * P], ident_b[:, :],
                              above[:, :].unsqueeze(1).broadcast_to([P, 2, P]), start=True, stop=False,
                              skip_group_check=True)
                    for c in range(2):
                        h = 2 * (g - 4) + c
                        mm = pe.matmul(bank[:, c * T:(c + 1) * T], q[0:KROWS, h, P:2 * P],
                                       k[0:KROWS, h, :], start=False, stop=True, skip_group_check=True)
                mm.then_inc(S["max_mm"], 1)

            def reader_before(i, on_, *candidates):
                for name, lag in candidates:
                    if on_(lag):
                        return wait(pe, name, i + lag)

            def back_rows(s, t):
                wait(pe, "o_ready", s)
                for g in range(4):
                    mm = pe.transpose(PS[:, WB, g * P:(g + 1) * P], o_sb[:, g, t * P:(t + 1) * P], ident[:, :])
                mm.then_inc(S["OT_mm"], 1)

            def chains(i, on_, j):
                s, e = i + PROJ, i + TAIL
                if j == 0 and on_(TAIL):
                    reader_before(i, on_, ("rt2_ready", PROJ - 1), ("on_ready", TAIL - 1))
                    back_rows(e, 0)
                if j == 1 and on_(TAIL):
                    wait(pe, "on_ready", e, 1)
                    back_rows(e, 1)
                if j == 0 and on_(PROJ):
                    wait(pe, "a1_ready", s)
                    reader_before(i, on_, ("v_ready", PROJ - 1))
                    chain_T(s, lambda t: a1[:, t, :], TB, D, "a1Tp")
                if j == 1 and on_(PROJ):
                    wait(pe, "a1T_ready", s)
                    for t in range(TB):
                        mm = pe.matmul(PS[:, MB, t * LAT:(t + 1) * LAT], a1T[:, t * P:(t + 1) * P], wdkv[:, :],
                                       start=True, stop=True)
                    mm.then_inc(S["lat_mm"], 1)
                if j == 2 and on_(PROJ):
                    reader_before(i, on_, ("on_ready", TAIL), ("rt2_ready", PROJ - 1))
                    pe.matmul(PS[:, WB, 0:T], wq2[:, 0:P], a1T[:, :], start=True, stop=True)
                    pe.matmul(PS[:, WB, T:2 * T], wq2[:, P // 2:P // 2 + P], a1T[:, :], start=True, stop=True)\
                      .then_inc(S["q_mm"], 1)
                if j == 3 and on_(PROJ):
                    wait(pe, "laT_ready", s)
                    wait(pe, "rt2_ready", s, 1)
                    pe.matmul(PS[:, WB, 0:T], wuk2[:, 0:P], laT[:, :], start=True, stop=True)
                    pe.matmul(PS[:, WB, T:2 * T], wuk2[:, P // 2:P // 2 + P], laT[:, :], start=True, stop=True)\
                      .then_inc(S["k_mm"], 1)
                if j == 3 and on_(TAIL):
                    wait(pe, "on_ready", e)
                    reader_before(i, on_, ("laT_ready", PROJ), ("v_ready", PROJ - 1), ("missT_ready", TAIL - 1))
                    chain_T(e, lambda t: on[:, t, :], TB, P, "onTp")
                if j == 4 and on_(TAIL):
                    wait(pe, "onT_ready", e)
                    for t in range(TB):
                        mm = pe.matmul(PS[:, MB, t * D:(t + 1) * D], onT[:, t * P:(t + 1) * P], wo2[:, :],
                                       start=True, stop=True)
                    mm.then_inc(S["wo_mm"], 1)
                if j == 6 and on_(TAIL):
                    wait(pe, "a2_ready", e)
                    chain_T(e, lambda t: a2[:, t, :], TB, D, "a2Tp")
                if j == 7 and on_(TAIL):
                    wait(pe, "a2T_ready", e)
                    reader_before(i, on_, ("nT_ready", MAXI))
                    for t in range(TB):
                        mm = pe.matmul(PS[:, MB, t * NE:(t + 1) * NE], a2T[e.par][:, t * P:(t + 1) * P], gw[:, :],
                                       start=True, stop=True)
                    mm.then_inc(S["lg_mm"], 1)

            def chains_late(i, on_, j):
                s, e = i + PROJ, i + TAIL
                if j == 2 and on_(PROJ):
                    wait(pe, "la_ready", s)
                    apart(pe)
                    chain_T(s, lambda t: la[:, t, :], TB, LAT, "laTp")
                if j == 6 and on_(MAXI):
                    m = i + MAXI
                    wait(pe, "n_ready", m)
                    reader_before(i, on_, ("a2T_ready", TAIL), ("laT_ready", PROJ), ("v_ready", PROJ - 1))
                    apart(pe)
                    for t in range(TB):
                        mm = pe.transpose(PS[0:3 * MH, MB, t * P // 2:(t + 1) * P // 2].bitcast(BF16),
                                          nparts[:, t, :, :].rearrange("p a h -> p (a h)"), ident_b[:, :])
                    mm.then_inc(S["nTp"], 1)
                if j == 7 and on_(TAIL):
                    wait(pe, "pick_ready", e)
                    chain_T(e, lambda t: pick[:, t, :], TB, NE, "pickTp")

            def body(i, on_):
                for j in range(SLOTS):
                    if on_(PROB):
                        for x in ((0, 1) if j % 2 == 0 else (2,)):
                            scores_for_exp(i + PROB, j // 2, x)
                    if j == 7:
                        chains(i, on_, j)
                    if on_(EXPS):
                        hidden(i + EXPS, j)
                    if j < 6 and on_(MAXI):
                        scores_for_max(i + MAXI, 2 * j)
                    if j != 7:
                        chains(i, on_, j)
                    if on_(EXPS) and j > 0:
                        values_back(i + EXPS, j - 1)
                    if j < 6 and on_(MAXI):
                        scores_for_max(i + MAXI, 2 * j + 1)
                    if on_(PROB) and j % 2 == 0 and j > 0:
                        values(i + PROB, j // 2 - 1)
                    chains_late(i, on_, j)
                if on_(PROB):
                    values(i + PROB, 3)
                if on_(PROJ):
                    s = i + PROJ
                    reader_before(i, on_, ("missT_ready", TAIL), ("nT_ready", MAXI), ("laT_ready", PROJ))
                    for t in range(TB):
                        mm = pe.matmul(PS[:, MB, t * P:(t + 1) * P], laT[:, t * P:(t + 1) * P], wuv[:, :],
                                       start=True, stop=True)
                    mm.then_inc(S["v_mm"], 1)
                if on_(EXPS):
                    s = i + EXPS
                    values_back(s, 7)
                    for t in range(TB):
                        mm = pe.matmul(PS[:, YB, t * D:(t + 1) * D], pickT[s.par][:, t * P:(t + 1) * P], b2[:, :],
                                       start=False, stop=True, skip_group_check=True)
                    mm.then_inc(S["y_mm"], 1)
            turns(pe, body)


def build(nc, a, out):
    with ExitStack() as ctx:
        x_res = ctx.enter_context(nc.sbuf_tensor("x_res", [P, B * TB, D], F32))
        ident = ctx.enter_context(nc.sbuf_tensor("ident_sb", [P, P], F32))
        mhalf = ctx.enter_context(nc.sbuf_tensor("mhalf", [P, 16], F32))
        rowmod_dram = nc.dram_tensor("rowmod_dram", (B, 4, D), F32, kind="Internal").ap()
        consts_in = ctx.enter_context(nc.semaphore("consts_in"))
        linear_attention(nc, a, x_res, ident, mhalf, rowmod_dram, consts_in, None)
        feed_forward(nc, a, out, x_res, ident, mhalf, rowmod_dram, consts_in, None)


def kernel(**inputs):
    import numpy as _np
    import concourse.bacc as _bacc
    from concourse.bass_utils import run_bass_kernel_spmd as _run

    g = {k: _np.asarray(v) for k, v in inputs.items()}
    arrays = {
        "x": g["L0_attn_x"], "wq": g["L0_attn_Wq"], "wk": g["L0_attn_Wk"],
        "wvg": _np.concatenate([g["L0_attn_Wv"], g["L0_attn_Wg"]], axis=1),
        "w1t": g["L0_attn_gk_w1"].T, "w2": g["L0_attn_gk_w2"], "gk_b": g["L0_attn_gk_b2"].reshape(-1, 1),
        "gnorm": _np.concatenate([g["L0_attn_g_norm_w"]] * 2).reshape(-1, 1), "wo": g["L0_attn_Wo"],
        "cT": g["L0_c"].T, "wmod": g["L0_wmod"],
    }
    def by_feature(w):
        w = w.reshape(-1, MH, MD).transpose(0, 2, 1).reshape(-1, P)
        return _np.concatenate([w, w[:, :P // 2]], axis=1)

    arrays.update({
        "wq2": by_feature(g["L0_ffn_Wq"].T), "wuk2": by_feature(g["L0_ffn_Wuk"].T), "wdkv": g["L0_ffn_Wdkv"].T,
        "wuv": g["L0_ffn_Wuv"].T, "wo2": g["L0_ffn_Wo"].T, "n1w": g["L0_ffn_norm1_w"].reshape(-1, 1),
        "n2w": g["L0_ffn_norm2_w"].reshape(-1, 1), "lng": g["L0_ffn_ln_g"].reshape(-1, 1),
        "lnb": g["L0_ffn_ln_b"].reshape(-1, 1), "gw": g["L0_ffn_gate_w"].T, "gate_b": g["L0_ffn_gate_b"].reshape(1, -1),
        "w1": g["L0_ffn_W1"].transpose(2, 0, 1).reshape(D, NE * HID), "b1": g["L0_ffn_b1"].reshape(NE * HT, P).T,
        "w2e": g["L0_ffn_W2"].transpose(0, 2, 1).reshape(NE * HID, D), "b2": g["L0_ffn_b2"],
    })
    arrays.update(shape_constants())
    arrays = {f"in_{k}": _np.ascontiguousarray(v) for k, v in arrays.items()}
    nc = _bacc.Bacc("TRN2", target_bir_lowering=False, num_devices=1)
    aps = {k[3:]: nc.dram_tensor(k, v.shape, mybir.dt.from_np(v.dtype), kind="ExternalInput").ap()
           for k, v in arrays.items()}
    out = nc.dram_tensor("out", g["L0_attn_x"].shape, F32, kind="ExternalOutput").ap()
    build(nc, aps, out)
    r = _run(nc, [arrays], core_ids=[0])
    return r.results[0]["out"]
```

```python
from contextlib import ExitStack

import numpy as np

import concourse.bass as bass
from concourse import mybir

F32 = mybir.dt.float32
BF16 = mybir.dt.bfloat16
U32 = mybir.dt.uint32
I32 = mybir.dt.int32
ALU = mybir.AluOpType
ACT = mybir.ActivationFunctionType
AX = mybir.AxisListType

P = 128
D = 128
B = 32
T = 256
TB = T // P
EPS = 1e-5
EPS_RMS = 1e-6

GH, GK, GV, CH = 4, 32, 64, 64
DV = GH * GV
UB = 2
UT = UB * TB
UN = UB * T
UNITS = B // UB
NCH = T // CH
GATE_NORM = 16.0

MH, MD = 16, 8
LAT = 64
KROWS = 6 * MD
MROWS = 3

NE, HID = 4, 512
HT = HID // P
REGION = B * T + P
SORTED_TILES = B * TB + NE


def shape_constants():
    half = MD // 2
    pos = np.arange(T, dtype=np.float32)
    freq = (np.float32(1.0) / np.float32(10000.0) ** (np.arange(half, dtype=np.float32) / np.float32(half))).astype(np.float32)
    ang = (pos[None, :] * freq[:, None]).astype(np.float32)
    cos, sin = np.cos(ang).astype(np.float32), np.sin(ang).astype(np.float32)
    rope_cos = np.repeat(np.concatenate([cos, cos]), MH, axis=0)
    rope_sin = np.repeat(np.concatenate([-sin, sin]), MH, axis=0)
    ident = np.eye(P, dtype=np.float32)
    s, t = np.arange(P)[:, None], np.arange(P)[None, :]
    chunk_causal = ((s <= t) & (s // CH == t // CH)).astype(np.float32)
    above = np.where(t > s, -1e30, 0.0).astype(np.float32)
    scan_keep = np.tile((np.arange(UN) % CH != 0).astype(np.float32), (P, 1))
    head_of_row = (np.arange(P)[:, None] // GK == np.arange(GH)[None, :]).astype(np.float32)
    before = (s < t).astype(np.float32)
    region0 = np.tile((np.arange(NE) * REGION).astype(np.float32), (P, 1))
    multiples = np.tile((np.arange(B * TB) * P).astype(np.float32), (P, 1))
    numbers = np.tile(np.arange(SORTED_TILES).astype(np.float32), (P, 1))
    tile_no = np.concatenate([np.arange(P, dtype=np.float32)[:, None], numbers], axis=1)
    first_of_four = np.tile((np.arange(TB * NE) % NE != 0).astype(np.float32), (P, 1))
    return {"rope_cos": rope_cos, "rope_sin": rope_sin, "ident": ident, "chunk_causal": chunk_causal,
            "above": above, "scan_keep": scan_keep, "head_of_row": head_of_row, "first_of_four": first_of_four,
            "before": before, "region0": region0, "multiples": multiples, "tile_no": tile_no}


def linear_attention(nc, a, x_res, ident, mhalf, rowmod_dram, consts_in, later):
    with ExitStack() as ctx:
        def sb(name, shape, dt=F32):
            return ctx.enter_context(nc.sbuf_tensor(name, shape, dt))

        def sem(name):
            return ctx.enter_context(nc.semaphore(name))

        chunk_causal = sb("chunk_causal_sb", [P, P])
        scan_keep = sb("scan_keep_sb", [P, UN])
        head_of_row = sb("head_of_row_sb", [P, GH])
        wq = sb("wq", [D, P])
        wk = sb("wk", [D, P])
        wvg = sb("wvg", [D, 2 * DV])
        w1t = sb("w1t", [16, D])
        w2 = sb("w2", [16, P])
        w12 = sb("w12", [D, P])
        gk_b = sb("gk_b", [P, 1])
        wo = sb("wo", [P, 2, D])
        gnorm = sb("gnorm", [P, 1])
        cT = sb("cT", [D, B])
        cth = sb("cth", [D, B])
        csil = sb("csil", [D, B])
        wmod = sb("wmod", [D, 6 * D])
        shiftT = sb("shiftT", [D, B])
        scaleT = sb("scaleT", [D, B])
        rowmod = sb("rowmod", [B, 4, D])
        sgn = sb("sgn", [B, 2, D])

        ln1_st = sb("ln1_st", [P, UT, 6])
        ln1_mv = sb("ln1_mv", [P, UT, 2])
        ln1_ve = sb("ln1_ve", [P, UT])
        ln1_rs = sb("ln1_rs", [P, UT])
        xn = sb("xn", [P, UT, D])
        hT = sb("hT", [D, UN])
        g_a = sb("g_a", [P, UN])
        g_e = sb("g_e", [P, UN])
        g_l = sb("g_l", [P, UN])
        g_m = sb("g_m", [P, UN])
        g_g = sb("g_g", [P, UN])
        g_cum = sb("g_cum", [P, UN])
        eb = sb("eb", [P, UN])
        enb = sb("enb", [P, UN])
        qg = sb("qg", [P, UN])
        kg = sb("kg", [P, UN])
        kH = sb("kH", [P, UN])
        kHt = sb("kHt", [P, UT, P])
        v_sb = sb("v_sb", [P, UT, DV])
        tg = sb("tg", [P, UT, DV])
        sg = sb("sg", [P, UT, DV])
        qg_bd = sb("qg_bd", [P, UT, GH, P])
        att = sb("att", [P, UT, GH, P])
        state = sb("state", [P, UB, NCH - 1, GV])
        state_bd = sb("state_bd", [P, UB * (NCH - 1), GH, GV])
        sq = sb("sq", [P, UT * GH, GV])
        og = sb("og", [P, UT * GH, GV])
        og2 = sb("og2", [P, UT * GH, GV])
        ss = sb("ss", [P, UT * GH])
        ss_e = sb("ss_e", [P, UT * GH])
        rrms = sb("rrms", [P, UT * GH])
        oT = sb("oT", [P, UT, 2, P])
        ga_bc = sb("ga_bc", [P, UB, D])
        yg = sb("yg", [P, UB, TB, D])

        PS = ctx.enter_context(nc.psum_tensor("PS", [P, 8, 512], F32))

        x_head_in = sem("x_head_in")
        x_rest_in = sem("x_rest_in")
        tanh_c = sem("tanh_c")
        silu_c = sem("silu_c")
        setup_mm = sem("setup_mm")
        setup_v = sem("setup_v")
        setup_v2 = sem("setup_v2")
        mhalf_set = sem("mhalf_set")
        rowmod_out = sem("rowmod_out")
        own_step = sem("own_step")
        ga_in = sem("ga_in")
        S = {n: sem(n) for n in (
            "ln1_stats", "ln1_mean", "ln1_eps", "ln1_rstd", "xn_ready", "xnT_ready", "hT_ready", "z_ready",
            "g_abs", "g_exp", "g_ln", "g_min", "g_ready", "cum_ready", "eb_ready", "enb_ready",
            "q_ready", "k_ready", "vg_ready", "v_ready", "tanh_ready", "sg_ready", "qg_ready", "kg_ready",
            "kH_ready", "qbd_ready", "kHT_ready", "kHt_ready", "A_ready", "att_ready", "U_ready", "H_step", "H_ready", "bd_ready",
            "o_ready", "sq_ready", "og_ready", "ss_ready", "ss_eps", "rrms_ready", "og2_ready", "oTp_ready",
            "oT_ready", "y_ready", "yg_ready", "x1_ready")}
        PER = {"ln1_stats": UT, "ln1_mean": UT, "xn_ready": UT, "hT_ready": UB, "vg_ready": UT, "A_ready": UT,
               "att_ready": UT, "qbd_ready": GH, "H_step": 3}

        def wait(eng, name, n, k=None):
            per = PER.get(name, 1)
            k = per if k is None else k
            if isinstance(n, int) and n * per + k <= 0:
                return
            eng.wait_ge(S[name], n * per + k)

        def apart(eng):
            eng.sem_inc(own_step, 1)

        block = ctx.enter_context(nc.Block())

        CONST_LOADS = [
            (ident, "ident"), (chunk_causal, "chunk_causal"), (scan_keep, "scan_keep"), (head_of_row, "head_of_row"),
            (wq, "wq"), (wk, "wk"), (wvg, "wvg"), (w1t, "w1t"), (w2, "w2"), (gk_b, "gk_b"), (gnorm, "gnorm"),
            (cT, "cT"), (wmod, "wmod")]
        N_CONST = 16 * (len(CONST_LOADS) + 1)

        x_tiles = a["x"].rearrange("b (t p) d -> p (b t) d", p=P)

        @block.sync
        def _(sp):
            for dst, name in CONST_LOADS:
                sp.dma_start(dst[:, :], a[name]).then_inc(consts_in, 16)
            sp.dma_start(wo[:, :, :], a["wo"].rearrange("(e p) n -> p e n", p=P)).then_inc(consts_in, 16)
            sp.dma_start(x_res[:, 0:3 * UT, :], x_tiles[:, 0:3 * UT, :]).then_inc(x_head_in, 16)
            sp.dma_start(x_res[:, 3 * UT:, :], x_tiles[:, 3 * UT:, :]).then_inc(x_rest_in, 16)
            for dst, src in later["loads"]:
                sp.dma_start(dst, src).then_inc(later["w_in"], 16)
            sp.wait_ge(setup_v2, 4)
            sp.dma_start(rowmod_dram, rowmod[:, :, :]).then_inc(rowmod_out, 16)
            sp.wait_ge(rowmod_out, 16)

            def load_ga(u):
                wait(sp, "yg_ready", u - 1)
                sp.dma_start(ga_bc[:, :, :], rowmod_dram[bass.ts(u, UB), 0:1, :].rearrange("b o d -> o b d")
                             .broadcast_to([P, UB, D])).then_inc(ga_in, 16)
            load_ga(0)
            with sp.Fori(1, UNITS) as u:
                load_ga(u)

        @block.gpsimd
        def _(pool):
            pool.memset(mhalf[:, :], -0.5).then_inc(mhalf_set, 1)
            pool.wait_ge(mhalf_set, 1)

            def ln1_rstd(u):
                wait(pool, "ln1_mean", u)
                apart(pool)
                pool.tensor_scalar(ln1_ve[:, :], ln1_mv[:, :, 1], EPS, None, ALU.add).then_inc(S["ln1_eps"], 1)
                wait(pool, "ln1_eps", u)
                wait(pool, "xn_ready", u - 1)
                pool.tensor_tensor(ln1_rs[:, :], ln1_ve[:, :], mhalf[:, 0:UT], ALU.pow).then_inc(S["ln1_rstd"], 1)

            def output_rstd(u):
                wait(pool, "ss_ready", u)
                apart(pool)
                pool.tensor_scalar(ss_e[:, :], ss[:, :], 1.0 / GV, EPS, ALU.mult, ALU.add).then_inc(S["ss_eps"], 1)
                wait(pool, "ss_eps", u)
                wait(pool, "og2_ready", u - 1)
                pool.tensor_tensor(rrms[:, :], ss_e[:, :], mhalf[:, :], ALU.pow).then_inc(S["rrms_ready"], 1)

            def add_output(u):
                wait(pool, "yg_ready", u)
                xs = x_res[:, bass.ts(u, UT), :].rearrange("p (b t) d -> p b t d", b=UB)
                pool.tensor_tensor(xs, xs, yg[:, :, :, :], ALU.add).then_inc(S["x1_ready"], 1)

            def body(u, first=False, last=False, ends=False):
                if not first:
                    output_rstd(u - 1)
                if not last and not ends:
                    ln1_rstd(u + 2)
                if not first:
                    add_output(u - 1)

            ln1_rstd(0)
            ln1_rstd(1)
            body(0, first=True)
            wait(pool, "ln1_rstd", 2)
            for n, (where, value) in enumerate(later["fills"]):
                if n > 0:
                    pool.wait_ge(later["pool_set"], n)
                pool.memset(where, value).then_inc(later["pool_set"], 1)
            pool.wait_ge(later["pool_set"], later["fills_n"])
            body(1)
            with pool.Fori(2, UNITS - 2) as u:
                body(u)
            body(UNITS - 2, ends=True)
            body(UNITS - 1, last=True)
            output_rstd(UNITS - 1)
            add_output(UNITS - 1)

        @block.scalar
        def _(act):
            act.wait_ge(consts_in, N_CONST)
            act.activation(cth[:, :], cT[:, :], ACT.Tanh, scale=0.5).then_inc(tanh_c, 1)

            def modulate(u):
                wait(act, "xnT_ready", u)
                wait(act, "vg_ready", u - 1)
                for i in range(UB):
                    b = u * UB + i
                    act.activation(hT[:, i * T:(i + 1) * T], PS[:, 0, i * T:(i + 1) * T], ACT.Identity,
                                   scale=scaleT[:, bass.ds(b, 1)], bias=shiftT[:, bass.ds(b, 1)]).then_inc(S["hT_ready"], 1)

            def gate_logs(u):
                wait(act, "z_ready", u)
                wait(act, "g_ready", u - 1)
                act.activation(g_a[:, :], PS[:, 1, :], ACT.Abs, bias=gk_b[:, 0:1]).then_inc(S["g_abs"], 1)
                wait(act, "g_abs", u)
                act.activation(g_e[:, :], g_a[:, :], ACT.Exp, scale=-1.0).then_inc(S["g_exp"], 1)
                wait(act, "g_exp", u)
                act.activation(g_l[:, :], g_e[:, :], ACT.Ln, bias=1.0).then_inc(S["g_ln"], 1)

            def decays(u):
                wait(act, "cum_ready", u)
                wait(act, "bd_ready", u - 1)
                wait(act, "kH_ready", u - 1)
                act.activation(eb[:, :], g_cum[:, :], ACT.Exp, scale=1.0 / GATE_NORM).then_inc(S["eb_ready"], 1)
                act.activation(enb[:, :], g_cum[:, :], ACT.Exp, scale=-1.0 / GATE_NORM).then_inc(S["enb_ready"], 1)

            def output_T(u):
                wait(act, "oTp_ready", u)
                wait(act, "y_ready", u - 1)
                act.activation(oT[:, :, :, :].rearrange("p j e t -> p (j e t)"),
                               PS[:, 6:8, :].rearrange("p k n -> p (k n)"), ACT.Copy).then_inc(S["oT_ready"], 1)

            def body(u, first=False, last=False):
                decays(u)
                if not last:
                    modulate(u + 1)
                wait(act, "vg_ready", u)
                wait(act, "o_ready", u - 1)
                act.activation(v_sb[:, :, :], PS[:, 4:8, 0:DV], ACT.Copy).then_inc(S["v_ready"], 1)
                wait(act, "sg_ready", u - 1)
                act.activation(tg[:, :, :], PS[:, 4:8, DV:2 * DV], ACT.Tanh, scale=0.5).then_inc(S["tanh_ready"], 1)
                wait(act, "kHT_ready", u)
                act.activation(kHt[:, :, :], PS[:, 2, :].rearrange("p (j c) -> p j c", j=UT), ACT.Copy)\
                   .then_inc(S["kHt_ready"], 1)
                if not last:
                    gate_logs(u + 1)
                if not first:
                    output_T(u - 1)
                wait(act, "o_ready", u)
                wait(act, "ss_ready", u - 1)
                act.activation(sq[:, :, :], PS[:, 4:6, :].rearrange("p k (h v) -> p (k h) v", v=GV), ACT.Square)\
                   .then_inc(S["sq_ready"], 1)

            act.wait_ge(setup_v, 2)
            modulate(0)
            gate_logs(0)
            body(0, first=True)
            body(1)
            with act.Fori(2, UNITS - 1) as u:
                body(u)
            body(UNITS - 1, last=True)
            output_T(UNITS - 1)

        @block.vector
        def _(dve):
            dve.wait_ge(tanh_c, 1)
            dve.scalar_tensor_tensor(out=cth[:, :], in0=cth[:, :], scalar=1.0, in1=cT[:, :], op0=ALU.add, op1=ALU.mult)\
               .then_inc(silu_c, 1)
            dve.wait_ge(silu_c, 1)
            dve.tensor_scalar(csil[:, :], cth[:, :], 0.5, None, ALU.mult).then_inc(silu_c, 1)
            dve.wait_ge(setup_mm, 3)
            dve.tensor_copy(shiftT[:, :], PS[:, 0, 0:B]).then_inc(setup_v, 1)
            dve.tensor_scalar(scaleT[:, :], PS[:, 0, B:2 * B], 1.0, None, ALU.add).then_inc(setup_v, 1)
            dve.tensor_copy(w12[:, :], PS[:, 2, 0:P]).then_inc(setup_v, 1)
            rows = PS[0:B, 1, :].rearrange("b (k d) -> b k d", k=4)
            dve.tensor_copy(rowmod[:, 1, :], rows[:, 1, :]).then_inc(setup_v2, 1)
            dve.tensor_scalar(rowmod[:, 2, :], rows[:, 2, :], 1.0, None, ALU.add).then_inc(setup_v2, 1)
            for i, k in enumerate((0, 3)):
                dve.tensor_scalar(sgn[:, i, :], rows[:, k, :], 0.0, 2.0, ALU.is_ge, ALU.mult).then_inc(setup_v, 1)
                dve.tensor_scalar(rowmod[:, k, :], rows[:, k, :], -1.0, 0.25, ALU.mult, ALU.max).then_inc(setup_v, 1)
                dve.wait_ge(setup_v, 3 + 3 * i + 2)
                dve.tensor_tensor(rowmod[:, k, :], rows[:, k, :], rowmod[:, k, :], ALU.max).then_inc(setup_v, 1)
                dve.wait_ge(setup_v, 3 + 3 * i + 3)
                dve.scalar_tensor_tensor(out=rowmod[:, k, :], in0=sgn[:, i, :], scalar=-1.0, in1=rowmod[:, k, :],
                                         op0=ALU.add, op1=ALU.mult).then_inc(setup_v2, 1)
            dve.tensor_scalar(wo[:, :, :], wo[:, :, :], gnorm[:, 0:1], 0.5, ALU.mult, ALU.mult).then_inc(setup_v, 1)

            def ln1_stats(u):
                wait(dve, "xn_ready", u - 1)
                for j in range(UT):
                    dve.bn_stats(ln1_st[:, j, :], x_res[:, bass.ds(u * UT + j, 1), :].rearrange("p o d -> p (o d)"))\
                       .then_inc(S["ln1_stats"], 1)
                for j in range(UT):
                    wait(dve, "ln1_stats", u, j + 1)
                    apart(dve)
                    dve.bn_aggr(ln1_mv[:, j, :], ln1_st[:, j, :]).then_inc(S["ln1_mean"], 1)

            def ln1_apply(u):
                wait(dve, "ln1_rstd", u)
                wait(dve, "xnT_ready", u - 1)
                for j in range(UT):
                    dve.tensor_scalar(xn[:, j, :], x_res[:, bass.ds(u * UT + j, 1), :].rearrange("p o d -> p (o d)"),
                                      ln1_mv[:, j, 0:1], ln1_rs[:, j:j + 1], ALU.subtract, ALU.mult)\
                       .then_inc(S["xn_ready"], 1)

            def gate_min(u):
                wait(dve, "g_abs", u)
                dve.tensor_scalar(g_m[:, :], PS[:, 1, :], gk_b[:, 0:1], 0.0, ALU.add, ALU.min).then_inc(S["g_min"], 1)

            def gate_cumsum(u):
                wait(dve, "g_ln", u)
                wait(dve, "g_min", u)
                wait(dve, "cum_ready", u - 1)
                dve.tensor_tensor(g_g[:, :], g_m[:, :], g_l[:, :], ALU.subtract).then_inc(S["g_ready"], 1)
                wait(dve, "g_ready", u)
                wait(dve, "enb_ready", u - 1)
                wait(dve, "eb_ready", u - 1)
                dve.tensor_tensor_scan(g_cum[:, :], scan_keep[:, :], g_g[:, :], 0.0, ALU.mult, ALU.add)\
                   .then_inc(S["cum_ready"], 1)

            def normed_output(u):
                wait(dve, "rrms_ready", u)
                wait(dve, "og_ready", u)
                wait(dve, "oTp_ready", u - 1)
                dve.tensor_tensor(og2[:, :, :], og[:, :, :], rrms[:, :].unsqueeze(2).broadcast_to([P, UT * GH, GV]),
                                  ALU.mult).then_inc(S["og2_ready"], 1)

            def gated_output(u):
                wait(dve, "y_ready", u)
                wait(dve, "x1_ready", u - 1)
                dve.wait_ge(ga_in, (u + 1) * 16)
                dve.tensor_tensor(yg[:, :, :, :], PS[:, 1, :].rearrange("p (b t d) -> p b t d", b=UB, t=TB),
                                  ga_bc[:, :, :].unsqueeze(2).broadcast_to([P, UB, TB, D]), ALU.mult)\
                   .then_inc(S["yg_ready"], 1)

            def body(u, first=False, last=False, ends=False):
                wait(dve, "q_ready", u)
                wait(dve, "eb_ready", u)
                wait(dve, "o_ready", u - 1)
                dve.scalar_tensor_tensor(out=qg[:, :], in0=PS[:, 2, :], scalar=float(GK) ** -0.5, in1=eb[:, :],
                                         op0=ALU.mult, op1=ALU.mult).then_inc(S["qg_ready"], 1)
                wait(dve, "k_ready", u)
                wait(dve, "enb_ready", u)
                dve.tensor_tensor(kg[:, :], PS[:, 3, :], enb[:, :], ALU.mult).then_inc(S["kg_ready"], 1)
                wait(dve, "kg_ready", u)
                wait(dve, "kHT_ready", u - 1)
                ebl = eb[:, CH - 1:UN:CH].unsqueeze(2).broadcast_to([P, UN // CH, CH])
                dve.tensor_tensor(kH[:, :].rearrange("p (c s) -> p c s", s=CH),
                                  kg[:, :].rearrange("p (c s) -> p c s", s=CH), ebl, ALU.mult).then_inc(S["kH_ready"], 1)
                wait(dve, "qg_ready", u)
                wait(dve, "A_ready", u - 1)
                for h in range(GH):
                    dve.tensor_scalar(qg_bd[:, :, h, :], qg[:, :].rearrange("p (j t) -> p j t", j=UT),
                                      head_of_row[:, h:h + 1], None, ALU.mult).then_inc(S["qbd_ready"], 1)
                wait(dve, "tanh_ready", u)
                wait(dve, "og_ready", u - 1)
                dve.scalar_tensor_tensor(out=sg[:, :, :], in0=tg[:, :, :], scalar=1.0, in1=PS[:, 4:8, DV:2 * DV],
                                         op0=ALU.add, op1=ALU.mult).then_inc(S["sg_ready"], 1)
                if not last:
                    gate_min(u + 1)
                if not first:
                    normed_output(u - 1)
                for j in range(UT):
                    wait(dve, "A_ready", u, j + 1)
                    dve.tensor_tensor(att[:, j, :, :], PS[:, 4 + j, :].rearrange("p (h t) -> p h t", h=GH),
                                      chunk_causal[:, :].unsqueeze(1).broadcast_to([P, GH, P]), ALU.mult)\
                       .then_inc(S["att_ready"], 1)
                if not last and not ends:
                    ln1_stats(u + 2)
                wait(dve, "U_ready", u)
                even = PS[:, 0, 0:UB * 2 * GV].rearrange("p (b c v) -> p b c v", b=UB, c=2)
                odd = PS[:, 3, 0:UB * GV].rearrange("p (b v) -> p b v", b=UB)
                wait(dve, "bd_ready", u - 1)
                dve.tensor_copy(state[:, :, 0, :], even[:, :, 0, :]).then_inc(S["H_step"], 1)
                for c in (1, 2):
                    wait(dve, "H_step", u, 1 if c == 1 else 2)
                    for i in range(UB):
                        at = i * T + c * CH + CH - 1
                        ins = dve.scalar_tensor_tensor(out=state[:, i, c, :], in0=state[:, i, c - 1, :],
                                                       scalar=eb[:, at:at + 1],
                                                       in1=odd[:, i, :] if c == 1 else even[:, i, 1, :],
                                                       op0=ALU.mult, op1=ALU.add)
                        if i == UB - 1:
                            ins.then_inc(S["H_step"], 1)
                wait(dve, "H_step", u)
                dve.tensor_tensor(state_bd[:, :, :, :],
                                  state[:, :, :, :].rearrange("p b c v -> p (b c) v").unsqueeze(2)
                                  .broadcast_to([P, UB * (NCH - 1), GH, GV]),
                                  head_of_row[:, :].unsqueeze(1).unsqueeze(3)
                                  .broadcast_to([P, UB * (NCH - 1), GH, GV]), ALU.mult).then_inc(S["bd_ready"], 1)
                if not last:
                    gate_cumsum(u + 1)
                if not last and not ends:
                    ln1_apply(u + 2)
                if not first:
                    gated_output(u - 1)
                wait(dve, "sq_ready", u)
                wait(dve, "og2_ready", u - 1)
                dve.tensor_tensor(og[:, :, :], PS[:, 4:6, :].rearrange("p k (h v) -> p (k h) v", v=GV),
                                  sg[:, :, :].rearrange("p j (h v) -> p (j h) v", v=GV), ALU.mult).then_inc(S["og_ready"], 1)
                wait(dve, "rrms_ready", u - 1)
                dve.tensor_reduce(ss[:, :], sq[:, :, :], AX.X, ALU.add).then_inc(S["ss_ready"], 1)

            dve.wait_ge(x_head_in, 16)
            ln1_stats(0)
            ln1_apply(0)
            gate_min(0)
            gate_cumsum(0)
            ln1_stats(1)
            ln1_apply(1)
            body(0, first=True)
            dve.wait_ge(x_rest_in, 16)
            body(1)
            with dve.Fori(2, UNITS - 2) as u:
                body(u)
            body(UNITS - 2, ends=True)
            body(UNITS - 1, last=True)
            normed_output(UNITS - 1)
            gated_output(UNITS - 1)

        @block.tensor
        def _(pe):
            pe.wait_ge(consts_in, N_CONST)
            pe.wait_ge(silu_c, 2)
            for k in range(2):
                pe.matmul(PS[:, 0, k * B:(k + 1) * B], wmod[:, k * D:(k + 1) * D], csil[:, :], start=(k == 0),
                          stop=True, skip_group_check=True)
            mm = pe.matmul(PS[0:B, 1, :], csil[:, :], wmod[:, 2 * D:6 * D], start=True, stop=True)
            mm.then_inc(setup_mm, 2)
            pe.matmul(PS[:, 2, 0:P], w1t[:, :], w2[:, :], start=True, stop=True).then_inc(setup_mm, 1)

            def normed_T(u):
                wait(pe, "xn_ready", u)
                wait(pe, "H_step", u - 2)
                wait(pe, "hT_ready", u - 1)
                for j in range(UT):
                    mm = pe.transpose(PS[:, 0, j * P:(j + 1) * P], xn[:, j, :], ident[:, :])
                mm.then_inc(S["xnT_ready"], 1)

            def gate_z(u):
                wait(pe, "hT_ready", u)
                wait(pe, "yg_ready", u - 3)
                wait(pe, "g_min", u - 1)
                pe.matmul(PS[:, 1, :], w12[:, :], hT[:, :], start=True, stop=True).then_inc(S["z_ready"], 1)

            def output_T(u):
                wait(pe, "og2_ready", u)
                wait(pe, "oT_ready", u - 1)
                for j in range(UT):
                    for e in range(2):
                        k = j * 2 + e
                        mm = pe.transpose(PS[:, 6 + k // 4, (k % 4) * P:(k % 4 + 1) * P],
                                          og2[:, j * GH + e * 2:j * GH + e * 2 + 2, :].rearrange("p h v -> p (h v)"),
                                          ident[:, :])
                mm.then_inc(S["oTp_ready"], 1)

            def output(u, last=False):
                wait(pe, "oT_ready", u)
                wait(pe, "yg_ready", u - 1)
                if not last:
                    wait(pe, "g_min", u + 2)
                for j in range(UT):
                    for e in range(2):
                        mm = pe.matmul(PS[:, 1, j * D:(j + 1) * D], oT[:, j, e, :], wo[:, e, :],
                                       start=(e == 0), stop=(e == 1))
                mm.then_inc(S["y_ready"], 1)

            def body(u, first=False, last=False):
                wait(pe, "kHt_ready", u - 1)
                pe.matmul(PS[:, 2, :], wq[:, :], hT[:, :], start=True, stop=True).then_inc(S["q_ready"], 1)
                wait(pe, "H_step", u - 1)
                pe.matmul(PS[:, 3, :], wk[:, :], hT[:, :], start=True, stop=True).then_inc(S["k_ready"], 1)
                wait(pe, "og_ready", u - 1)
                wait(pe, "oT_ready", u - 2)
                for j in range(UT):
                    pe.matmul(PS[:, 4 + j, :], hT[:, j * P:(j + 1) * P], wvg[:, :], start=True, stop=True)\
                      .then_inc(S["vg_ready"], 1)
                if not last:
                    normed_T(u + 1)
                    gate_z(u + 1)
                wait(pe, "kH_ready", u)
                wait(pe, "qg_ready", u)
                for j in range(UT):
                    mm = pe.transpose(PS[:, 2, j * P:(j + 1) * P], kH[:, j * P:(j + 1) * P], ident[:, :])
                mm.then_inc(S["kHT_ready"], 1)
                wait(pe, "v_ready", u)
                wait(pe, "sg_ready", u)
                wait(pe, "qbd_ready", u)
                for j in range(UT):
                    pe.matmul(PS[:, 4 + j, :], kg[:, j * P:(j + 1) * P], qg_bd[:, j, :, :].rearrange("p h t -> p (h t)"),
                              start=True, stop=True).then_inc(S["A_ready"], 1)
                wait(pe, "kHt_ready", u)
                apart(pe)
                for i in range(UB):
                    for c in range(NCH - 1):
                        j, half = i * TB + c // 2, c % 2
                        col = (i * 2 + c // 2) * GV if half == 0 else i * GV
                        rows = slice(half * CH, (half + 1) * CH)
                        for h in range(GH):
                            mm = pe.matmul(PS[h * GK:(h + 1) * GK, 3 * half, col:col + GV],
                                           kHt[rows, j, h * GK:(h + 1) * GK], v_sb[rows, j, h * GV:(h + 1) * GV],
                                           start=True, stop=True, skip_group_check=True)
                mm.then_inc(S["U_ready"], 1)
                wait(pe, "att_ready", u)
                if not first:
                    output_T(u - 1)
                for j in range(UT):
                    for h in range(GH):
                        pe.matmul(PS[:, 4 + j // 2, (j % 2) * DV + h * GV:(j % 2) * DV + (h + 1) * GV],
                                  att[:, j, h, :], v_sb[:, j, h * GV:(h + 1) * GV],
                                  start=(j % 2 == 0 and h == 0), stop=False, skip_group_check=True)
                if not first:
                    output(u - 1, last)
                wait(pe, "bd_ready", u)
                for i in range(UB):
                    for c in range(1, NCH):
                        j, half = i * TB + c // 2, c % 2
                        mm = pe.matmul(PS[half * CH:(half + 1) * CH, 4 + j // 2, (j % 2) * DV:(j % 2 + 1) * DV],
                                       qg[:, i * T + c * CH:i * T + (c + 1) * CH], state_bd[:, i * (NCH - 1) + c - 1, :, :],
                                       start=False, stop=True, skip_group_check=True)
                mm.then_inc(S["o_ready"], 1)

            pe.wait_ge(setup_v, 10)
            normed_T(0)
            gate_z(0)
            body(0, first=True)
            body(1)
            with pe.Fori(2, UNITS - 1) as u:
                body(u)
            body(UNITS - 1, last=True)
            output_T(UNITS - 1)
            output(UNITS - 1, last=True)


class Step:

    def __init__(self, k, c, turn, depth):
        self.k, self.c, self.turn, self.depth = k, c, turn, depth
        self.n = turn * k + c

    def __add__(self, d):
        return Step(self.k, self.c + d, self.turn, self.depth)

    @property
    def par(self):
        return self.c % self.depth

    @property
    def uses(self):
        return self.turn // self.depth * self.k + self.c // self.depth


def turns(eng, body, first, loop0, loop1, last, count, turn, depth):
    for i in range(first, loop0):
        body(Step(0, i, turn, depth), lambda lag, i=i: 0 <= i + lag < count)
    with eng.Fori(0, (loop1 - loop0) // turn) as k:
        for r in range(turn):
            body(Step(k, loop0 + r, turn, depth), lambda lag: True)
    for i in range(loop1, last + 1):
        body(Step(0, i, turn, depth), lambda lag, i=i: 0 <= i + lag < count)


BATCH_TURNS = (-4, 3, 27, B + 1, B, 3, 3)
TILE_TURNS = (-3, 4, SORTED_TILES - 4, SORTED_TILES + 1, SORTED_TILES, 4, 2)
OUT_TURNS = (-2, 2, B // 2 - 2, B // 2, B // 2, 2, 2)


def feed_forward_constants(nc, ctx, a):
    def sb(name, shape, dt=F32):
        return ctx.enter_context(nc.sbuf_tensor(name, shape, dt))

    rope_cos = sb("rope_cos_sb", [P, T])
    rope_sin = sb("rope_sin_sb", [P, T])
    above_f = sb("above_f", [P, P])
    above = sb("above_sb", [P, P], BF16)
    ident_b = sb("ident_b", [P, P], BF16)
    cum_keep = sb("cum_keep", [P, TB * NE])
    wq2 = sb("wq2", [D, P + P // 2])
    wuk2 = sb("wuk2", [LAT, P + P // 2])
    wdkv = sb("wdkv", [D, LAT])
    wuv = sb("wuv", [LAT, P])
    wo2 = sb("wo2", [P, D])
    n1w = sb("n1w", [D, 1])
    n2w = sb("n2w", [D, 1])
    lng = sb("lng", [LAT, 1])
    lnb = sb("lnb", [LAT, 1])
    gw = sb("gw", [D, NE])
    gb4 = sb("gb4", [P, TB, NE])
    w1 = sb("w1", [D, NE * HID])
    w2 = sb("w2e", [P, NE * HT, D])
    before_f = sb("before_f", [P, P])
    before = sb("before_sb", [P, P], BF16)
    region0 = sb("region0", [P, NE])
    multiples = sb("multiples", [P, B * TB])
    tile_no = sb("tile_no_sb", [P, 1 + SORTED_TILES])
    bias3 = sb("bias3", [96, NE * (HID + D)], BF16)
    one3 = sb("one3", [96, P], BF16)
    ones = sb("ones_sb", [P, P], BF16)
    filler = sb("filler", [P, D + 2 * NE])
    token = sb("token", [P, B * TB])
    v1 = [sb(f"v1_{n}", [P, TB, MH, 32]) for n in range(3)]
    ks = [sb(f"ks{n}", [64, MH, T], BF16) for n in range(3)]
    keep1 = sb("keep1", [P, NE])
    rows_of = sb("rows_of", [P, NE])
    b20 = sb("b20", [P, NE * (HID + D) // P])

    LOADS = [(rope_cos, "rope_cos"), (rope_sin, "rope_sin"), (above_f, "above"), (wq2, "wq2"), (wuk2, "wuk2"),
             (cum_keep, "first_of_four"), (wdkv, "wdkv"), (wuv, "wuv"), (wo2, "wo2"), (n1w, "n1w"), (n2w, "n2w"),
             (lng, "lng"), (lnb, "lnb"), (gw, "gw"), (w1, "w1"), (before_f, "before"), (region0, "region0"),
             (multiples, "multiples"), (tile_no, "tile_no")]
    loads = [(dst[:, :], a[name]) for dst, name in LOADS]
    loads.append((gb4[:, :, :], a["gate_b"].unsqueeze(0).broadcast_to([P, TB, NE])))
    loads.append((w2[:, :, :], a["w2e"].rearrange("(h p) n -> p h n", p=P)))
    loads.append((b20[:, :], a["bias"].rearrange("o (p c) -> (o p) c", p=P)))
    fills = [(ks[n][32:64, :, :], 1.0) for n in range(3)]
    fills += [(v1[n][:, :, :, :], 0.0) for n in range(3)] + [(v1[n][:, :, :, MD:MD + 1], 1.0) for n in range(3)]
    fills += [(one3[:, :], 0.0)] + [(one3[r:r + 1, :], 1.0) for r in (0, 32, 64)]
    fills += [(ones[:, :], 1.0), (filler[:, :], 0.0), (keep1[:, :], 1.0), (rows_of[:, :], 0.0), (bias3[:, :], 0.0)]
    return {"rope_cos": rope_cos, "rope_sin": rope_sin, "above_f": above_f, "above": above, "ident_b": ident_b, "cum_keep": cum_keep,
            "wq2": wq2, "wuk2": wuk2, "wdkv": wdkv, "wuv": wuv, "wo2": wo2, "n1w": n1w,
            "n2w": n2w, "lng": lng, "lnb": lnb, "gw": gw, "gb4": gb4, "w1": w1,
            "w2": w2, "before_f": before_f, "before": before, "region0": region0, "multiples": multiples, "tile_no": tile_no,
            "bias3": bias3, "one3": one3, "ones": ones, "filler": filler, "token": token, "v1": v1, "ks": ks,
            "keep1": keep1, "rows_of": rows_of, "b20": b20,
            "names": ("rope_cos", "rope_sin", "above_f", "above", "ident_b", "cum_keep", "wq2", "wuk2",
                      "wdkv", "wuv", "wo2", "n1w", "n2w", "lng", "lnb", "gw",
                      "gb4", "w1", "w2", "before_f", "before", "region0", "multiples", "tile_no",
                      "bias3", "one3", "ones", "filler", "token", "v1", "ks", "keep1", "rows_of",
                      "b20"),
            "loads": loads, "fills": fills, "fills_n": len(fills), "loads_n": 16 * len(loads),
            "w_in": ctx.enter_context(nc.semaphore("w_in")), "pool_set": ctx.enter_context(nc.semaphore("pool_set"))}


def feed_forward(nc, out, x_res, ident, mhalf, rowmod_dram, constants):
    NORM, PROJ, STACK, MAXI, PROB, TAIL, ROUTE = 4, 3, 2, 1, 0, -1, -2
    SLOTS = 8
    MAXIMA = ((0, 1, 2), (3, 4, 5), (6, 7), (8, 9), (10, 11), (), (), ())
    with ExitStack() as ctx:
        def sb(name, shape, dt=F32):
            return ctx.enter_context(nc.sbuf_tensor(name, shape, dt))

        all_sems = []

        def sem(name):
            all_sems.append(ctx.enter_context(nc.semaphore(name)))
            return all_sems[-1]

        r_res = sb("r_res", [P, B * TB, D])
        (rope_cos, rope_sin, above_f, above, ident_b, cum_keep, wq2, wuk2,
         wdkv, wuv, wo2, n1w, n2w, lng, lnb, gw,
         gb4, w1, w2, before_f, before, region0, multiples, tile_no,
         bias3, one3, ones, filler, token, v1, ks, keep1, rows_of,
         b20) = (
            constants[name] for name in constants["names"])
        w_in, pool_set, FILLS, N_W = (constants[name] for name in ("w_in", "pool_set", "fills_n", "loads_n"))
        b_rem = sb("b_rem", [P, NE * (HID + D) // P])
        b_parts = sb("b_parts", [P, 3, NE * (HID + D) // P], BF16)

        ln_st = sb("ln_st", [P, TB, 6])
        ln_mv = sb("ln_mv", [P, TB, 2])
        ln_ve = sb("ln_ve", [P, TB])
        ln_rs = sb("ln_rs", [P, TB])
        xn = sb("xn2", [P, TB, D])
        xc = sb("xc2", [P, TB, D])
        mod_bc = sb("mod_bc", [P, 2, D])
        sqj = sb("sqj", [P, TB, D])
        s1 = sb("s1", [P, TB])
        s1e = sb("s1e", [P, TB])
        s1r = sb("s1r", [P, TB])
        a1 = sb("a1", [P, TB, D])
        a1T = sb("a1T", [D, T])
        la_st = sb("la_st", [P, TB, 6])
        la_mv = sb("la_mv", [P, TB, 2])
        la_ve = sb("la_ve", [P, TB])
        la_rs = sb("la_rs", [P, TB])
        la = sb("la", [P, TB, LAT])
        laT = sb("laT", [LAT, T])
        rt1 = sb("rt1", [P, 2, T])
        rt2 = sb("rt2", [P, 2, T])
        rt = sb("rt", [P, 2, T])
        rr = sb("rr", [P, 2, T])
        parts = sb("parts", [P, 3, 2, T], BF16)
        qs = [sb(f"qs{n}", [64, MH, T], BF16) for n in range(3)]
        nm = sb("nm", [P, TB, MH])
        nr = sb("nr", [P, TB, MH])
        nparts = sb("nparts", [P, TB, 3, MH], BF16)
        nT = sb("nT", [3 * MH, T], BF16)
        pexp = sb("pexp", [P, 2, 1536])
        o_sb = sb("o_sb", [P, 4, T])
        rec = sb("rec", [P, TB, MH])
        on = sb("on", [P, TB, MH * MD])
        onT = sb("onT", [P, T])
        sqk = sb("sqk", [P, TB, D])
        s2 = sb("s2", [P, TB])
        s2e = sb("s2e", [P, TB])
        s2r = sb("s2r", [P, TB])
        a2 = [sb(f"a2_{n}", [P, TB, D + 1]) for n in range(3)]
        a2T = sb("a2T", [D, T])
        lg = sb("lg", [P, TB, NE])
        lmax = sb("lmax", [P, TB])
        hit = sb("hit", [P, TB, NE])
        hits = sb("hits", [P, TB, NE])
        pick = sb("pick", [P, TB, NE], BF16)
        nextrow = sb("nextrow", [P, NE])
        place = sb("place", [P, TB, NE])
        placed = sb("placed", [P, TB, NE])
        rowf = sb("rowf", [P, TB])
        row_at = sb("row_at", [P, TB], U32)
        pad_f = sb("pad_f", [P, NE])
        pad_at = sb("pad_at", [P, NE], U32)
        past = sb("past", [P, NE, B * TB])
        tiles_of = sb("tiles_of", [P, NE])
        tile0 = sb("tile0", [P, NE])
        region_of = sb("region_of", [P, SORTED_TILES, NE])
        tiles_before = sb("tiles_before", [P, SORTED_TILES, NE])
        tile_f = sb("tile_f", [P, 5, SORTED_TILES])
        table = sb("table", [P, 2, SORTED_TILES], I32)
        w1_now = [pexp[:, 0, n * HID:(n + 1) * HID] for n in range(2)]
        w2_now = [o_sb[:, 2 * n:2 * n + 2, :].rearrange("p a (b d) -> p (a b) d", d=D) for n in range(2)]
        b1_now = [parts[0:96, n, :, :].rearrange("p x t -> p (x t)") for n in range(2)]
        b2_now = [parts[0:96, 2, n, 0:D] for n in range(2)]
        hidT = [pexp[:, 1, n * HID:(n + 1) * HID].rearrange("p (m t) -> p m t", m=HT) for n in range(2)]
        xs = [pexp[:, x, 2 * HID + n * (D + 1):2 * HID + (n + 1) * (D + 1)] for x, n in ((0, 0), (1, 0), (1, 1), (1, 2))]
        xsT = [pexp[:, 0, 2 * HID + (2 + n) * D:2 * HID + (3 + n) * D] for n in range(2)]
        ys = [rt2[:, n // 2, n % 2 * D:(n % 2 + 1) * D] for n in range(4)]
        gat = [o_sb[:, 2 * n:2 * n + 2, :].rearrange("p b (t d) -> p b t d", t=TB) for n in range(2)]
        gate = [rt1[:, n, :].rearrange("p (b d) -> p b d", b=2) for n in range(2)]
        fin1, fin2, res = ([pexp[:, n, x * 2 * T:(x + 1) * 2 * T].rearrange("p (b t d) -> p b t d", b=2, t=TB)
                            for n in range(2)] for x in range(3))
        to = [sb(f"to{n}", [P, 1], U32) for n in range(4)]

        PS = ctx.enter_context(nc.psum_tensor("PS2", [P, 8, 512], F32))
        PB, XB, OB, WB, RB, MB = (0, 1), (2, 5), 3, 4, 6, 7
        XT, HB, YB = (0, 1), (2, 3), (6, 7)

        parts_dram = nc.dram_tensor("parts_dram", (B, 2, 3 * MD, MH, T), BF16, kind="Internal").ap()
        negmax_dram = nc.dram_tensor("negmax_dram", (B, 3, MH, T), BF16, kind="Internal").ap()

        bias_dram = nc.dram_tensor("bias_dram", (3, NE * (HID + D)), BF16, kind="Internal").ap()
        rows_dram = nc.dram_tensor("rows_dram", (NE * REGION + NE * P, D + 1), F32, kind="Internal").ap()
        y_dram = nc.dram_tensor("y_dram", (B * T + 2 * NE * P, D), F32, kind="Internal").ap()

        w_set = sem("w_set")
        act_set = sem("act_set")
        mod_in = sem("mod_in")
        gb_in = [sem("gb_in0"), sem("gb_in1")]
        rows_out = sem("rows_out")
        pads_out = sem("pads_out")
        bias_in = sem("bias_in")
        bias_out = sem("bias_out")
        bias_set = sem("bias_set")
        spare_out = sem("spare_out")
        plan = sem("plan")
        tile_in = [sem(f"tile_in{n}") for n in range(4)]
        y_out = [sem(f"y_out{n}") for n in range(4)]
        gat_in = [sem("gat_in0"), sem("gat_in1")]
        parts_out = [sem(f"parts_out{n}") for n in range(3)]
        stack_in = [sem(f"stack_in{n}") for n in range(3)]
        negmax_out = sem("negmax_out")
        negmax_in = sem("negmax_in")
        res_out = [sem("res_out0"), sem("res_out1")]
        own = sem("own2")
        PER = {"f_stats": TB, "f_mean": TB, "f_xn": TB, "f_sq": TB, "a1_ready": TB, "la_stats": TB, "la_mean": TB,
               "la_ready": TB, "max_mm": 12, "max_ready": 12, "prob_mm": 12, "prob_ready": 12, "diag_ready": 8,
               "pv_done": 4, "o_ready": 4, "OT_mm": TB, "rec_ready": TB, "on_ready": TB, "rt1_ready": 2, "rt2_ready": 2,
               "rt_ready": 2, "p0_ready": 2, "rr1_ready": 2, "p1_ready": 2, "parts_ready": 2, "t_sq": TB, "a2_ready": TB,
               "hidden_set": 2, "output_set": 2}
        NAMES = ("f_stats f_mean f_eps f_rstd f_xn f_scaled h_ready2 f_sq f_eps2 f_rstd2 a1_ready a1Tp a1T_ready lat_mm "
                 "la_stats la_mean la_eps la_rstd la_ready laTp laT_ready q_mm k_mm rt1_ready rt2_ready rt_ready p0_ready rr1_ready "
                 "p1_ready parts_ready v_mm v_ready max_mm max_ready n_0 n_r1 n_1 n_ready nTp nT_ready prob_mm prob_ready "
                 "diag_ready pv_done o_ready OT_mm rec_ready on_ready onTp onT_ready wo_mm r_ready t_sq t_eps t_rstd "
                 "number_ready a2_ready a2Tp a2T_ready lg_mm lg_ready lmax_ready hit_ready hits_ready pick_ready "
                 "place_mm place_ready nextrow_ready placed_ready rowf_ready row_at_ready "
                 "xsTp xsT_ready hidden_set output_set hidT_mm hidT_ready y_mm ys_ready to_ready fin1_ready fin2_ready res_ready").split()
        S = {n: sem("ff_" + n) for n in NAMES}

        def wait(eng, name, s, k=None):
            per = PER.get(name, 1)
            k = per if k is None else k
            if isinstance(s.n, int) and s.n * per + k <= 0:
                return
            eng.wait_ge(S[name], s.n * per + k)

        def apart(eng):
            eng.sem_inc(own, 1)

        with nc.Block() as clearing:
            @clearing.gpsimd
            def _(pool):
                numbers = sorted(x.num for x in all_sems)
                ends = [n for n in numbers if n + 1 not in numbers]
                starts = [n for n in numbers if n - 1 not in numbers]
                for start, end in zip(starts, ends):
                    pool.sem_clear(range(start, end + 1))

        block = ctx.enter_context(nc.Block())
        PLANNED = 15
        LOAD, ROWS, HIDDEN, SECOND, OUTPUT, BACK = 3, 1, 0, -1, -2, -2
        GATHER = 2

        def row(cell, engine, most):
            return nc.values_load(cell, engines=(engine,), min_val=0, max_val=most)

        @block.sync
        def _(sp):
            sp.wait_ge(pool_set, FILLS)
            sp.wait_ge(w_set, 6)
            for x in range(NE):
                sp.dma_start(rows_dram[NE * REGION + x * P:NE * REGION + (x + 1) * P, :],
                             filler[:, NE + x:NE + x + D + 1]).then_inc(spare_out, 16)

            def place_biases():
                sp.wait_ge(bias_set, 5)
                sp.dma_start(bias_dram.rearrange("a (p c) -> p a c", p=P), b_parts[:, :, :]).then_inc(bias_out, 16)
                sp.wait_ge(bias_out, 16)
                for n in range(3):
                    sp.dma_start(bias3[32 * n:32 * n + 1, :], bias_dram[n:n + 1, :]).then_inc(bias_in, 16)

            def body(i, on_):
                if on_(NORM):
                    s = i + NORM
                    wait(sp, "h_ready2", s + -1)
                    sp.dma_start(mod_bc[:, :, :], rowmod_dram[bass.ds(s.n, 1), 1:3, :].broadcast_to([P, 2, D]))\
                      .then_inc(mod_in, 16)
                if on_(STACK):
                    s = i + STACK
                    sp.wait_ge(parts_out[s.par], 32 * (s.uses + 1))
                    wait(sp, "prob_mm", s + -3)
                    sin = stack_in[s.par]
                    src = parts_dram[bass.ds(s.n, 1)].rearrange("o a r h t -> (o a) r (h t)")
                    q, k = src[0], src[1]
                    qd, kd = (x[:, :, :].rearrange("r h t -> r (h t)") for x in (qs[s.par], ks[s.par]))
                    sp.dma_start(qd[0:24, :], q[0:24, :]).then_inc(sin, 16)
                    sp.dma_start(qd[24:40, :], q[0:16, :]).then_inc(sin, 16)
                    sp.dma_start(qd[40:48, :], q[0:8, :]).then_inc(sin, 16)
                    for row, part in ((0, 0), (8, 0), (16, 0), (24, 1), (32, 1), (40, 2)):
                        sp.dma_start(kd[row:row + 8, :], k[part * 8:part * 8 + 8, :]).then_inc(sin, 16)
                if on_(MAXI):
                    s = i + MAXI
                    wait(sp, "nT_ready", s)
                    dst = negmax_dram[bass.ds(s.n, 1)]
                    sp.dma_start(dst.rearrange("o a h t -> (o a h) t"), nT[:, :]).then_inc(negmax_out, 16)
                    sp.wait_ge(negmax_out, 16 * (s.n + 1))
                    wait(sp, "prob_mm", s + -3)
                    sp.dma_start(qs[s.par][KROWS:KROWS + 3, :, :].rearrange("r h t -> r (h t)"),
                                 dst.rearrange("o a h t -> (o a) (h t)")).then_inc(negmax_in, 16)
                if on_(PROJ):
                    s = i + PROJ
                    for x in range(2):
                        wait(sp, "parts_ready", s, x + 1)
                        sp.dma_start(parts_dram[bass.ds(s.n, 1), x].rearrange("o (a d) h t -> (o d h) a t", a=3),
                                     parts[:, :, x, :]).then_inc(parts_out[s.par], 16)
            def body_and_biases(i, on_):
                body(i, on_)
                if isinstance(i.n, int) and i.n == BATCH_TURNS[0]:
                    place_biases()
            turns(sp, body_and_biases, *BATCH_TURNS)

            def tile_body(i, on_):
                if on_(LOAD):
                    n = i + LOAD
                    wait(sp, "xsTp", n + -4)
                    wait(sp, "to_ready", n + -4)
                    at_row = row(table[0:1, 0, bass.ds(n.n, 1)], mybir.EngineType.SP, NE * REGION + (NE - 1) * P)
                    sp.dma_start(xs[n.c % 4][:, :], rows_dram[bass.ds(at_row, P), :]).then_inc(tile_in[n.c % 4], 16)
            sp.wait_ge(plan, PLANNED)
            sp.wait_ge(rows_out, 16 * B * TB)
            sp.wait_ge(pads_out, 16 * NE)
            sp.wait_ge(spare_out, 16 * NE)
            turns(sp, tile_body, *TILE_TURNS)

            def out_body(i, on_):
                if on_(GATHER):
                    s = i + GATHER
                    wait(sp, "fin1_ready", s + -2)
                    sp.dma_start(gat[s.par].rearrange("p b t d -> p (b t) d"),
                                 y_dram[bass.ds(s.n * 2 * T, 2 * T), :].rearrange("(t p) d -> p t d", p=P))\
                      .then_inc(gat_in[s.par], 16)
                    wait(sp, "fin2_ready", s + -2)
                    sp.dma_start(gate[s.par], rowmod_dram[bass.ds(s.n * 2, 2), 3, :].unsqueeze(0).broadcast_to([P, 2, D]))\
                      .then_inc(gb_in[s.par], 16)
                if on_(0):
                    wait(sp, "res_ready", i)
                    sp.dma_start(out[bass.ds(i.n * 2, 2)].rearrange("b (t p) d -> p (b t) d", p=P),
                                 res[i.par].rearrange("p b t d -> p (b t) d")).then_inc(res_out[i.par], 16)
            for n in range(4):
                sp.wait_ge(y_out[n], 16 * (SORTED_TILES // 4))
            turns(sp, out_body, *OUT_TURNS)
            for n in range(2):
                sp.wait_ge(res_out[n], 16 * (B // 4))

        @block.gpsimd
        def _(pool):
            def rstd(s, src, ve, rs, eps, scale, got, stepped, done, used):
                wait(pool, got, s)
                apart(pool)
                pool.tensor_scalar(ve[:, :], src, scale, eps, ALU.mult, ALU.add).then_inc(S[stepped], 1)
                wait(pool, used, s + -1)
                wait(pool, stepped, s)
                pool.tensor_tensor(rs[:, :], ve[:, :], mhalf[:, 0:TB], ALU.pow).then_inc(S[done], 1)

            def keys_after_queries(s, hg, x):
                wait(pool, "prob_ready", s, 3 * hg + 2 + x)
                apart(pool)
                buf = pexp[:, hg % 2, 1024 * x:1024 + 512 * x].rearrange("p (h q) -> p h q", h=4)[:, :, 0:P]
                pool.affine_select(out=buf, in_=buf, compare_op=ALU.is_ge, fill=0.0, base=0,
                                   pattern=[[0, 4], [1, P]], channel_multiplier=-1).then_inc(S["diag_ready"], 1)

            def rotated(s, x):
                wait(pool, "rt1_ready", s, x + 1)
                wait(pool, "rt2_ready", s, x + 1)
                wait(pool, "rr1_ready", s + -1, x + 1)
                wait(pool, "p0_ready", s + -1, x + 1)
                pool.tensor_tensor(rt[:, x, :], rt1[:, x, :], rt2[:, x, :], ALU.add).then_inc(S["rt_ready"], 1)

            def body(i, on_):
                for j in range(SLOTS):
                    if on_(PROB):
                        keys_after_queries(i + PROB, j // 2, j % 2)
                    if j == 0 and on_(NORM):
                        s = i + NORM
                        rstd(s, ln_mv[:, :, 1], ln_ve, ln_rs, EPS, 1.0, "f_mean", "f_eps", "f_rstd", "f_xn")
                    if j == 2 and on_(PROJ):
                        s = i + PROJ
                        rstd(s, la_mv[:, :, 1], la_ve, la_rs, EPS, 1.0, "la_mean", "la_eps", "la_rstd", "la_ready")
                    if j == 3 and on_(NORM):
                        s = i + NORM
                        pool.wait_ge(mod_in, 16 * (s.n + 1))
                        wait(pool, "f_xn", s)
                        pool.tensor_tensor(xc[:, :, :], xn[:, :, :], mod_bc[:, 1:2, :].broadcast_to([P, TB, D]), ALU.mult)\
                            .then_inc(S["f_scaled"], 1)
                        wait(pool, "f_scaled", s)
                        pool.tensor_tensor(r_res[:, bass.ts(s.n, TB), :], xc[:, :, :],
                                           mod_bc[:, 0:1, :].broadcast_to([P, TB, D]), ALU.add).then_inc(S["h_ready2"], 1)
                    if j == 3 and on_(PROJ):
                        rotated(i + PROJ, 0)
                    if j == 4 and on_(PROJ):
                        rotated(i + PROJ, 1)
                    if j == 5 and on_(TAIL):
                        s = i + TAIL
                        rstd(s, s2[:, :], s2e, s2r, EPS_RMS, 1.0 / D, "t_sq", "t_eps", "t_rstd", "a2_ready")
                    if j == 5 and on_(NORM):
                        s = i + NORM
                        rstd(s, s1[:, :], s1e, s1r, EPS_RMS, 1.0 / D, "f_sq", "f_eps2", "f_rstd2", "a1_ready")
                    if j == 7 and on_(ROUTE):
                        s = i + ROUTE
                        wait(pool, "row_at_ready", s)
                        wait(pool, "number_ready", s)
                        apart(pool)
                        for t in range(TB):
                            pool.indirect_dma_start(rows_dram[:, :], bass.IndirectOffsetOnAxis(row_at[:, t:t + 1], 0),
                                                    a2[s.par][:, t, :], None).then_inc(rows_out, 16)
            turns(pool, body, *BATCH_TURNS)

            pool.wait_ge(plan, 2)
            for e in range(NE):
                pool.indirect_dma_start(rows_dram[:, :], bass.IndirectOffsetOnAxis(pad_at[:, e:e + 1], 0),
                                        filler[:, e:e + D + 1], None).then_inc(pads_out, 16)

            def tile_body(i, on_):
                if on_(BACK):
                    n = i + BACK
                    wait(pool, "to_ready", n)
                    wait(pool, "ys_ready", n)
                    apart(pool)
                    pool.indirect_dma_start(y_dram[:, :], bass.IndirectOffsetOnAxis(to[n.c % 4][:, 0:1], 0),
                                            ys[n.c % 4][:, :], None).then_inc(y_out[n.c % 4], 16)
            turns(pool, tile_body, *TILE_TURNS)

        @block.scalar
        def _(act):
            act.wait_ge(w_in, N_W)
            act.activation(above[:, :], above_f[:, :], ACT.Copy).then_inc(act_set, 1)
            act.activation(before[:, :], before_f[:, :], ACT.Copy).then_inc(act_set, 1)
            act.activation(ident_b[:, :], ident[:, :], ACT.Copy).then_inc(act_set, 1)
            act.wait_ge(pool_set, FILLS)
            act.wait_ge(w_set, 4)

            def exponentials(s, g):
                hg, x = g // 3, g % 3
                wait(act, "prob_mm", s, g + 1)
                wait(act, "pv_done", s, hg + 1 - 2)
                act.activation(pexp[:, hg % 2, x * 512:(x + 1) * 512], PS[:, PB[g % 2], :], ACT.Exp,
                               scale=float(MD) ** -0.5).then_inc(S["prob_ready"], 1)

            def values_out(s, hg):
                wait(act, "pv_done", s, hg + 1)
                wait(act, "OT_mm", s + -1)
                act.activation(o_sb[:, hg, :], PS[:, OB, (hg % 2) * T:(hg % 2 + 1) * T], ACT.Copy)\
                   .then_inc(S["o_ready"], 1)

            def part(s, x, a, src, source_ready, done):
                wait(act, source_ready, s, x + 1)
                if not isinstance(s.n, int) or s.n >= 1:
                    act.wait_ge(parts_out[(s + -1).par], 32 * ((s + -1).uses + 1))
                act.activation(parts[:, a, x, :], src[:, x, :], ACT.Copy).then_inc(S[done], 1)

            def squares(s, ready, used, junk, sums, done):
                wait(act, ready, s)
                wait(act, used, s + -1)
                for t in range(TB):
                    act.activation(junk[:, t, :], r_res[:, bass.ds(s.n * TB + t, 1), :].rearrange("p o d -> p (o d)"),
                                   ACT.Square, accum_out=sums[:, t:t + 1]).then_inc(S[done], 1)

            def copied(s, made, used_by, dst, src, done):
                wait(act, made, s)
                wait(act, *used_by)
                act.activation(dst, src, ACT.Copy).then_inc(S[done], 1)

            def body(i, on_):
                for j in range(SLOTS):
                    if on_(PROB):
                        for g in ((3 * (j // 2), 3 * (j // 2) + 1) if j % 2 == 0 else (3 * (j // 2) + 2,)):
                            exponentials(i + PROB, g)
                    if j == 0 and on_(PROJ):
                        s = i + PROJ
                        copied(s, "a1Tp", ("q_mm", s + -1), a1T[:, :], PS[:, MB, 0:T], "a1T_ready")
                    if j == 2 and on_(PROJ):
                        s = i + PROJ
                        wait(act, "laTp", s)
                        wait(act, "v_mm", s + -1)
                        act.activation(laT[:, :], PS[0:LAT, MB, 0:T], ACT.Identity, scale=lng[:, 0:1], bias=lnb[:, 0:1])\
                           .then_inc(S["laT_ready"], 1)
                    if j == 3 and on_(TAIL):
                        s = i + TAIL
                        copied(s, "onTp", ("wo_mm", s + -1), onT[:, :], PS[:, MB, 0:T], "onT_ready")
                    if j == 4 and on_(NORM):
                        squares(i + NORM, "h_ready2", "f_eps2", sqj, s1, "f_sq")
                    if j == 4 and on_(PROJ):
                        part(i + PROJ, 0, 0, rt, "rt_ready", "p0_ready")
                    if j == 5 and on_(TAIL):
                        squares(i + TAIL, "r_ready", "t_eps", sqk, s2, "t_sq")
                    if j == 5 and on_(PROJ):
                        part(i + PROJ, 1, 0, rt, "rt_ready", "p0_ready")
                        part(i + PROJ, 0, 1, rr, "rr1_ready", "p1_ready")
                    if j == 6 and on_(PROJ):
                        part(i + PROJ, 1, 1, rr, "rr1_ready", "p1_ready")
                    if j == 5 and on_(MAXI):
                        s = i + MAXI
                        wait(act, "nTp", s)
                        if not isinstance(s.n, int) or s.n > 0:
                            act.wait_ge(negmax_out, 16 * s.n)
                        act.activation(nT[:, :], PS[0:3 * MH, MB, 0:T // 2].bitcast(BF16), ACT.Copy)\
                           .then_inc(S["nT_ready"], 1)
                    if j in (2, 4, 6) and on_(PROB):
                        values_out(i + PROB, j // 2 - 1)
                    if j == 7 and on_(TAIL):
                        s = i + TAIL
                        copied(s, "a2Tp", ("lg_mm", s + -1), a2T[:, :], PS[:, MB, 0:T], "a2T_ready")
                    if j == 7 and on_(PROB):
                        values_out(i + PROB, 3)
                    if j == 7 and on_(PROJ):
                        s = i + PROJ
                        wait(act, "v_mm", s)
                        wait(act, "pv_done", s + -3)
                        act.activation(v1[s.par][:, :, :, 0:MD], PS[:, RB, T:2 * T].rearrange("p (t h d) -> p t h d", t=TB, h=MH),
                                       ACT.Copy).then_inc(S["v_ready"], 1)
            turns(act, body, *BATCH_TURNS)

            def tile_body(i, on_):
                if on_(ROWS):
                    n = i + ROWS
                    wait(act, "xsTp", n)
                    wait(act, "hidT_mm", n + -2)
                    act.activation(xsT[n.par][:, :], PS[:, XT[n.par], 0:P], ACT.Copy).then_inc(S["xsT_ready"], 1)
                if on_(BACK):
                    n = i + BACK
                    wait(act, "y_mm", n)
                    if not isinstance(n.n, int) or n.n >= 4:
                        act.wait_ge(y_out[n.c % 4], 16 * (n.k + n.c // 4))
                    act.activation(ys[n.c % 4][:, :], PS[:, YB[n.par], 0:D], ACT.Copy).then_inc(S["ys_ready"], 1)
                if on_(HIDDEN):
                    n = i + HIDDEN
                    wait(act, "hidT_mm", n)
                    wait(act, "y_mm", n + -2)
                    act.activation(hidT[n.par][:, :, :].rearrange("p m t -> p (m t)"), PS[:, HB[n.par], :], ACT.Relu)\
                       .then_inc(S["hidT_ready"], 1)
            turns(act, tile_body, *TILE_TURNS)

        @block.vector
        def _(dve):
            dve.wait_ge(w_in, N_W)
            dve.wait_ge(pool_set, FILLS)
            dve.tensor_scalar(wq2[:, :], wq2[:, :], n1w[:, 0:1], None, ALU.mult).then_inc(w_set, 1)
            dve.tensor_scalar(wdkv[:, :], wdkv[:, :], n1w[:, 0:1], None, ALU.mult).then_inc(w_set, 1)
            dve.tensor_scalar(gw[:, :], gw[:, :], n2w[:, 0:1], None, ALU.mult).then_inc(w_set, 1)
            dve.tensor_scalar(w1[:, :], w1[:, :], n2w[:, 0:1], None, ALU.mult).then_inc(w_set, 1)
            dve.tensor_scalar(token[:, :], multiples[:, :], tile_no[:, 0:1], None, ALU.add).then_inc(w_set, 1)
            dve.tensor_scalar(filler[:, D:D + 2 * NE], multiples[:, 0:2 * NE], tile_no[:, 0:1], float(B * T), ALU.add,
                              ALU.add).then_inc(w_set, 1)

            def norm_stats(s, tile_of, st, mv, stats, mean, used):
                wait(dve, used, s + -1)
                for t in range(TB):
                    dve.bn_stats(st[:, t, :], tile_of(t)).then_inc(S[stats], 1)
                for t in range(TB):
                    wait(dve, stats, s, t + 1)
                    apart(dve)
                    dve.bn_aggr(mv[:, t, :], st[:, t, :]).then_inc(S[mean], 1)

            def r_tile(s, t):
                return r_res[:, bass.ds(s.n * TB + t, 1), :].rearrange("p o d -> p (o d)")

            def x_tile(s, t):
                return x_res[:, bass.ds(s.n * TB + t, 1), :].rearrange("p o d -> p (o d)")

            def maximum(s, g):
                wait(dve, "n_ready", s + -1)
                wait(dve, "max_mm", s, g + 1)
                to, heads = (nm[:, 0, 4 * g:4 * g + 4], 4) if g < 4 else (nm[:, 1, 2 * g - 8:2 * g - 6], 2)
                dve.tensor_reduce(to, PS[:, XB[g % 2], :].rearrange("p (h k) -> p h k", h=heads), AX.X, ALU.max, negate=True)\
                   .then_inc(S["max_ready"], 1)

            def normalised(s, t):
                ot = PS[:, WB, :].rearrange("p (h c) -> p h c", c=32)
                wait(dve, "OT_mm", s, t + 1)
                wait(dve, "on_ready", s + -1, t + 1)
                dve.reciprocal(rec[:, t, :], ot[:, :, MD]).then_inc(S["rec_ready"], 1)
                wait(dve, "rec_ready", s, t + 1)
                wait(dve, "onTp", s + -1)
                dve.tensor_tensor(on[:, t, :].rearrange("p (h d) -> p h d", d=MD), ot[:, :, 0:MD],
                                  rec[:, t, :].unsqueeze(2).broadcast_to([P, MH, MD]), ALU.mult).then_inc(S["on_ready"], 1)

            def rotate(s, x, made):
                wait(dve, made, s)
                wait(dve, "rt_ready", s + -1, x + 1)
                dve.tensor_tensor(rt1[:, x, :], PS[:, WB, 0:T], rope_cos[:, :], ALU.mult).then_inc(S["rt1_ready"], 1)
                dve.tensor_tensor(rt2[:, x, :], PS[:, WB, T:2 * T], rope_sin[:, :], ALU.mult).then_inc(S["rt2_ready"], 1)

            def rest_of(s, x):
                wait(dve, "p0_ready", s, x + 1)
                wait(dve, "p1_ready", s + -1, x + 1)
                dve.tensor_tensor(rr[:, x, :], rt[:, x, :], parts[:, 0, x, :], ALU.subtract).then_inc(S["rr1_ready"], 1)

            def last_part(s, x):
                wait(dve, "p1_ready", s, x + 1)
                if not isinstance(s.n, int) or s.n >= 1:
                    dve.wait_ge(parts_out[(s + -1).par], 32 * ((s + -1).uses + 1))
                dve.tensor_tensor(parts[:, 2, x, :], rr[:, x, :], parts[:, 1, x, :], ALU.subtract)\
                   .then_inc(S["parts_ready"], 1)

            def body(i, on_):
                for j in range(SLOTS):
                    if j == 3 and on_(PROJ):
                        rotate(i + PROJ, 0, "q_mm")
                    lat = PS[:, MB, 0:TB * LAT].rearrange("p (t c) -> p t c", t=TB)
                    if j == 2 and on_(PROJ):
                        s = i + PROJ
                        wait(dve, "lat_mm", s)
                        norm_stats(s, lambda t: lat[:, t, :], la_st, la_mv, "la_stats", "la_mean", "la_ready")
                    for g in MAXIMA[j][:1] if on_(MAXI) else ():
                        maximum(i + MAXI, g)
                    if j == 0 and on_(ROUTE):
                        s = i + ROUTE
                        wait(dve, "lg_mm", s)
                        dve.tensor_tensor(lg[:, :, :], PS[:, MB, 0:TB * NE].rearrange("p (t e) -> p t e", t=TB), gb4[:, :, :],
                                          ALU.add).then_inc(S["lg_ready"], 1)
                        wait(dve, "lg_ready", s)
                        dve.tensor_reduce(lmax[:, :], lg[:, :, :], AX.X, ALU.max).then_inc(S["lmax_ready"], 1)
                        wait(dve, "lmax_ready", s)
                        dve.tensor_tensor(hit[:, :, :], lg[:, :, :], lmax[:, :].unsqueeze(2).broadcast_to([P, TB, NE]),
                                          ALU.is_ge).then_inc(S["hit_ready"], 1)
                        wait(dve, "hit_ready", s)
                        apart(dve)
                        dve.tensor_tensor_scan(hits[:, :, :].rearrange("p t e -> p (t e)"), cum_keep[:, :],
                                               hit[:, :, :].rearrange("p t e -> p (t e)"), 0.0, ALU.mult, ALU.add)\
                           .then_inc(S["hits_ready"], 1)
                        wait(dve, "hits_ready", s)
                        wait(dve, "place_mm", s + -1)
                        dve.scalar_tensor_tensor(out=pick[:, :, :], in0=hits[:, :, :], scalar=1.0, in1=hit[:, :, :],
                                                 op0=ALU.is_equal, op1=ALU.mult).then_inc(S["pick_ready"], 1)

                    if j < 2 and on_(TAIL):
                        normalised(i + TAIL, j)
                    for g in MAXIMA[j][1:2] if on_(MAXI) else ():
                        maximum(i + MAXI, g)
                    if j == 0 and on_(NORM):
                        s = i + NORM
                        norm_stats(s, lambda t: x_tile(s, t), ln_st, ln_mv, "f_stats", "f_mean", "f_xn")
                    if j == 1 and on_(NORM):
                        s = i + NORM
                        wait(dve, "f_rstd", s)
                        wait(dve, "f_scaled", s + -1)
                        for t in range(TB):
                            dve.tensor_scalar(xn[:, t, :], x_tile(s, t), ln_mv[:, t, 0:1], ln_rs[:, t:t + 1],
                                              ALU.subtract, ALU.mult).then_inc(S["f_xn"], 1)
                    if j == 4 and on_(ROUTE):
                        s = i + ROUTE
                        wait(dve, "place_mm", s)
                        wait(dve, "nextrow_ready", s + -1)
                        counts = PS[:, RB, 0:3 * NE].rearrange("p (t e) -> p t e", e=NE)
                        dve.tensor_tensor(place[:, :, :], counts[:, 0:TB, :],
                                          nextrow[:, :].unsqueeze(1).broadcast_to([P, TB, NE]), ALU.add)\
                           .then_inc(S["place_ready"], 1)
                        wait(dve, "place_ready", s)
                        dve.tensor_tensor(nextrow[:, :], nextrow[:, :], counts[:, TB, :], ALU.add)\
                           .then_inc(S["nextrow_ready"], 1)
                        dve.tensor_tensor(placed[:, :, :], place[:, :, :], pick[:, :, :], ALU.mult)\
                           .then_inc(S["placed_ready"], 1)
                        wait(dve, "placed_ready", s)
                        dve.tensor_reduce(rowf[:, :], placed[:, :, :], AX.X, ALU.add).then_inc(S["rowf_ready"], 1)
                        wait(dve, "rowf_ready", s)
                        if not isinstance(s.n, int) or s.n > 0:
                            dve.wait_ge(rows_out, 16 * TB * s.n)
                        dve.tensor_copy(row_at[:, :], rowf[:, :]).then_inc(S["row_at_ready"], 1)
                    if j == 4 and on_(PROJ):
                        rotate(i + PROJ, 1, "k_mm")
                    if j == 5 and on_(MAXI):
                        s = i + MAXI
                        wait(dve, "max_ready", s)
                        wait(dve, "nTp", s + -1)
                        dve.tensor_copy(nparts[:, :, 0, :], nm[:, :, :]).then_inc(S["n_0"], 1)
                        wait(dve, "n_0", s)
                        dve.tensor_tensor(nr[:, :, :], nm[:, :, :], nparts[:, :, 0, :], ALU.subtract).then_inc(S["n_r1"], 1)
                        wait(dve, "n_r1", s)
                        dve.tensor_copy(nparts[:, :, 1, :], nr[:, :, :]).then_inc(S["n_1"], 1)
                        wait(dve, "n_1", s)
                        dve.tensor_tensor(nparts[:, :, 2, :], nr[:, :, :], nparts[:, :, 1, :], ALU.subtract)\
                           .then_inc(S["n_ready"], 1)
                    if j == 5 and on_(PROJ):
                        rest_of(i + PROJ, 0)
                        rest_of(i + PROJ, 1)
                    for g in MAXIMA[j][2:] if on_(MAXI) else ():
                        maximum(i + MAXI, g)
                    if j == 2 and on_(PROJ):
                        s = i + PROJ
                        wait(dve, "la_rstd", s)
                        wait(dve, "laTp", s + -1)
                        for t in range(TB):
                            dve.tensor_scalar(la[:, t, :], lat[:, t, :], la_mv[:, t, 0:1], la_rs[:, t:t + 1], ALU.subtract,
                                              ALU.mult).then_inc(S["la_ready"], 1)
                    if j == 4 and on_(TAIL):
                        s = i + TAIL
                        wait(dve, "wo_mm", s)
                        h = r_res[:, bass.ts(s.n, TB), :]
                        dve.tensor_tensor(h, h, PS[:, MB, 0:T].rearrange("p (t d) -> p t d", t=TB), ALU.add)\
                           .then_inc(S["r_ready"], 1)
                    if j == 6 and on_(TAIL):
                        s = i + TAIL
                        wait(dve, "t_rstd", s)
                        wait(dve, "a2Tp", s + -1)
                        if not isinstance(s.n, int) or s.n > 2:
                            dve.wait_ge(rows_out, 16 * TB * (s.n + -2))
                        dve.tensor_copy(a2[s.par][:, :, D], token[:, bass.ts(s.n, TB)]).then_inc(S["number_ready"], 1)
                        for t in range(TB):
                            dve.tensor_scalar(a2[s.par][:, t, 0:D], r_tile(s, t), s2r[:, t:t + 1], None, ALU.mult)\
                               .then_inc(S["a2_ready"], 1)
                    if j == 6 and on_(PROJ):
                        last_part(i + PROJ, 0)
                        last_part(i + PROJ, 1)
                    if j == 6 and on_(NORM):
                        s = i + NORM
                        wait(dve, "f_rstd2", s)
                        wait(dve, "a1Tp", s + -1)
                        for t in range(TB):
                            dve.tensor_scalar(a1[:, t, :], r_tile(s, t), s1r[:, t:t + 1], None, ALU.mult)\
                               .then_inc(S["a1_ready"], 1)

            def split_biases():
                dve.tensor_copy(b_parts[:, 0, :], b20[:, :]).then_inc(bias_set, 1)
                dve.wait_ge(bias_set, 1)
                dve.tensor_tensor(b_rem[:, :], b20[:, :], b_parts[:, 0, :], ALU.subtract).then_inc(bias_set, 1)
                dve.wait_ge(bias_set, 2)
                dve.tensor_copy(b_parts[:, 1, :], b_rem[:, :]).then_inc(bias_set, 1)
                dve.wait_ge(bias_set, 3)
                dve.tensor_tensor(b_rem[:, :], b_rem[:, :], b_parts[:, 1, :], ALU.subtract).then_inc(bias_set, 1)
                dve.wait_ge(bias_set, 4)
                dve.tensor_copy(b_parts[:, 2, :], b_rem[:, :]).then_inc(bias_set, 1)

            dve.tensor_copy(nextrow[:, :], region0[:, :]).then_inc(w_set, 1)
            dve.wait_ge(w_set, 7)

            def body_and_biases(i, on_):
                body(i, on_)
                if isinstance(i.n, int) and i.n == BATCH_TURNS[0]:
                    split_biases()
            turns(dve, body_and_biases, *BATCH_TURNS)

            steps = [0]

            def done(instruction):
                instruction.then_inc(plan, 1)
                steps[0] += 1
                dve.wait_ge(plan, steps[0])

            wait(dve, "nextrow_ready", Step(0, B - 1, 1, 1))
            done(dve.tensor_scalar(pad_f[:, :], nextrow[:, :], tile_no[:, 0:1], None, ALU.add))
            done(dve.tensor_copy(pad_at[:, :], pad_f[:, :]))
            done(dve.tensor_tensor(rows_of[:, :], nextrow[:, :], region0[:, :], ALU.subtract))
            done(dve.tensor_tensor(past[:, :, :], rows_of[:, :].unsqueeze(2).broadcast_to([P, NE, B * TB]),
                                   multiples[:, :].unsqueeze(1).broadcast_to([P, NE, B * TB]), ALU.is_gt))
            done(dve.tensor_reduce(tiles_of[:, :], past[:, :, :], AX.X, ALU.add))
            done(dve.tensor_tensor_scan(tile0[:, :], keep1[:, :], tiles_of[:, :], 0.0, ALU.mult, ALU.add))
            over = [P, SORTED_TILES, NE]
            number = tile_no[:, 1:SORTED_TILES + 1]
            done(dve.tensor_tensor(region_of[:, :, :], number.unsqueeze(2).broadcast_to(over),
                                   tile0[:, :].unsqueeze(1).broadcast_to(over), ALU.is_ge))
            done(dve.tensor_reduce(tile_f[:, 0, :], region_of[:, :, :], AX.X, ALU.add))
            done(dve.tensor_tensor(tiles_before[:, :, :], region_of[:, :, :],
                                   tiles_of[:, :].unsqueeze(1).broadcast_to(over), ALU.mult))
            done(dve.tensor_reduce(tile_f[:, 1, :], tiles_before[:, :, :], AX.X, ALU.add))
            done(dve.tensor_tensor(tile_f[:, 2, :], number, tile_f[:, 1, :], ALU.subtract))
            done(dve.tensor_scalar(tile_f[:, 3, :], tile_f[:, 2, :], float(P), None, ALU.mult))
            done(dve.scalar_tensor_tensor(out=tile_f[:, 4, :], in0=tile_f[:, 0, :], scalar=float(REGION),
                                          in1=tile_f[:, 3, :], op0=ALU.mult, op1=ALU.add))
            done(dve.tensor_scalar(table[:, 0, :], tile_f[:, 4, :], float(NE * REGION + (NE - 1) * P), None, ALU.min))
            done(dve.tensor_scalar(table[:, 1, :], tile_f[:, 0, :], float(NE - 1), None, ALU.min))

            def tile_body(i, on_):
                if on_(ROWS):
                    n = i + ROWS
                    e_hid = row(table[0:1, 1, bass.ds(n.n, 1)], mybir.EngineType.DVE, NE - 1)
                    wait(dve, "hidT_mm", n + -2)
                    dve.tensor_copy(w1_now[n.par][:, :], w1[:, bass.ds(e_hid * HID, HID)]).then_inc(S["hidden_set"], 1)
                    dve.tensor_copy(b1_now[n.par][:, :], bias3[:, bass.ds(e_hid * HID, HID)]).then_inc(S["hidden_set"], 1)
                if on_(HIDDEN):
                    n = i + HIDDEN
                    dve.wait_ge(tile_in[n.c % 4], 16 * (n.k + n.c // 4 + 1))
                    if not isinstance(n.n, int) or n.n >= 4:
                        dve.wait_ge(y_out[n.c % 4], 16 * (n.k + n.c // 4))
                    dve.tensor_copy(to[n.c % 4][:, :], xs[n.c % 4][:, D:D + 1]).then_inc(S["to_ready"], 1)
                if on_(SECOND):
                    n = i + SECOND
                    e_out = row(table[0:1, 1, bass.ds(n.n, 1)], mybir.EngineType.DVE, NE - 1)
                    wait(dve, "y_mm", n + -2)
                    dve.tensor_copy(w2_now[n.par][:, :, :], w2[:, bass.ds(e_out * HT, HT), :]).then_inc(S["output_set"], 1)
                    dve.tensor_copy(b2_now[n.par][:, :], bias3[:, bass.ds(e_out * D + NE * HID, D)])\
                       .then_inc(S["output_set"], 1)
            dve.wait_ge(bias_in, 48)
            dve.wait_ge(plan, PLANNED)
            turns(dve, tile_body, *TILE_TURNS)

            def out_body(i, on_):
                if on_(0):
                    s = i
                    old_r, old_x = (x[:, bass.ts(s.n, 2 * TB), :].rearrange("p (b t) d -> p b t d", b=2)
                                    for x in (r_res, x_res))
                    dve.wait_ge(gat_in[s.par], 16 * (s.uses + 1))
                    dve.tensor_tensor(fin1[s.par], gat[s.par], old_r, ALU.add).then_inc(S["fin1_ready"], 1)
                    dve.wait_ge(gb_in[s.par], 16 * (s.uses + 1))
                    wait(dve, "fin1_ready", s)
                    dve.tensor_tensor(fin2[s.par], fin1[s.par], gate[s.par].unsqueeze(2).broadcast_to([P, 2, TB, D]),
                                      ALU.mult).then_inc(S["fin2_ready"], 1)
                    if not isinstance(s.n, int) or s.n >= 2:
                        dve.wait_ge(res_out[s.par], 16 * s.uses)
                    wait(dve, "fin2_ready", s)
                    dve.tensor_tensor(res[s.par], fin2[s.par], old_x, ALU.add).then_inc(S["res_ready"], 1)
            turns(dve, out_body, *OUT_TURNS)

        @block.tensor
        def _(pe):
            pe.wait_ge(w_in, N_W)
            pe.wait_ge(w_set, 4)
            pe.wait_ge(act_set, 3)
            pe.wait_ge(pool_set, FILLS)

            def chain_T(s, src, tiles, width, name):
                for t in range(tiles):
                    mm = pe.transpose(PS[0:width, MB, t * P:(t + 1) * P], src(t), ident[:, :])
                mm.then_inc(S[name], 1)

            def scores_for_exp(s, hg, x):
                q, k = qs[s.par], ks[s.par]
                R = KROWS + MROWS
                g = 3 * hg + x
                if g == 0:
                    pe.wait_ge(negmax_in, 16 * (s.n + 1))
                wait(pe, "prob_ready", s, g + 1 - 2)
                bank = PS[:, PB[g % 2], :]
                if x < 2:
                    for c in range(2):
                        mm = pe.matmul(bank[:, c * T:(c + 1) * T], k[0:R, 4 * hg + 2 * x + c, 0:P],
                                       q[0:R, 4 * hg + 2 * x + c, :], start=True, stop=True)
                else:
                    for c in range(4):
                        mm = pe.matmul(bank[:, c * P:(c + 1) * P], k[0:R, 4 * hg + c, P:2 * P],
                                       q[0:R, 4 * hg + c, P:2 * P], start=True, stop=True)
                mm.then_inc(S["prob_mm"], 1)

            def values(s, hg):
                if hg == 0:
                    wait(pe, "v_ready", s)
                wait(pe, "diag_ready", s, 2 * hg + 2)
                wait(pe, "prob_ready", s, 3 * hg + 3)
                wait(pe, "o_ready", s, hg + 1 - 2)
                for kt in range(TB):
                    for c in range(4):
                        if kt == 0:
                            o, pr = slice((hg % 2) * T, (hg % 2 + 1) * T), slice(c * T, (c + 1) * T)
                        else:
                            o, pr = slice((hg % 2) * T + P, (hg % 2 + 1) * T), slice(4 * T + c * P, 4 * T + (c + 1) * P)
                        mm = pe.matmul(PS[32 * c:32 * c + 32, OB, o], v1[s.par][:, kt, 4 * hg + c, :],
                                       pexp[:, hg % 2, pr], start=(kt == 0), stop=(kt == 1), skip_group_check=True)
                mm.then_inc(S["pv_done"], 1)

            def scores_for_max(s, g):
                q, k = qs[s.par], ks[s.par]
                if g == 0:
                    pe.wait_ge(stack_in[s.par], 144 * (s.uses + 1))
                wait(pe, "max_ready", s, g + 1 - 2)
                bank = PS[:, XB[g % 2], :]
                if g < 4:
                    pe.matmul(bank.rearrange("p (h k) -> p h k", h=4), ident_b[:, :],
                              above[:, :].unsqueeze(1).broadcast_to([P, 4, P]), start=True, stop=False,
                              skip_group_check=True)
                    for c in range(4):
                        mm = pe.matmul(bank[:, c * P:(c + 1) * P], q[0:KROWS, 4 * g + c, 0:P],
                                       k[0:KROWS, 4 * g + c, 0:P], start=False, stop=True, skip_group_check=True)
                else:
                    pe.matmul(bank.rearrange("p (h k) -> p h k", h=2)[:, :, P:2 * P], ident_b[:, :],
                              above[:, :].unsqueeze(1).broadcast_to([P, 2, P]), start=True, stop=False,
                              skip_group_check=True)
                    for c in range(2):
                        h = 2 * (g - 4) + c
                        mm = pe.matmul(bank[:, c * T:(c + 1) * T], q[0:KROWS, h, P:2 * P],
                                       k[0:KROWS, h, :], start=False, stop=True, skip_group_check=True)
                mm.then_inc(S["max_mm"], 1)

            def reader_before(i, on_, *candidates):
                for name, lag in candidates:
                    if on_(lag):
                        return wait(pe, name, i + lag)

            def back_rows(s, t):
                wait(pe, "o_ready", s)
                for g in range(4):
                    mm = pe.transpose(PS[:, WB, g * P:(g + 1) * P], o_sb[:, g, t * P:(t + 1) * P], ident[:, :])
                mm.then_inc(S["OT_mm"], 1)

            def chains(i, on_, j):
                s, e = i + PROJ, i + TAIL
                if j == 0 and on_(TAIL):
                    reader_before(i, on_, ("rt2_ready", PROJ - 1), ("on_ready", TAIL - 1))
                    back_rows(e, 0)
                if j == 1 and on_(TAIL):
                    wait(pe, "on_ready", e, 1)
                    back_rows(e, 1)
                if j == 0 and on_(PROJ):
                    wait(pe, "a1_ready", s)
                    reader_before(i, on_, ("lg_ready", TAIL - 1), ("nT_ready", MAXI - 1), ("laT_ready", PROJ - 1))
                    chain_T(s, lambda t: a1[:, t, :], TB, D, "a1Tp")
                if j == 1 and on_(PROJ):
                    wait(pe, "a1T_ready", s)
                    for t in range(TB):
                        mm = pe.matmul(PS[:, MB, t * LAT:(t + 1) * LAT], a1T[:, t * P:(t + 1) * P], wdkv[:, :],
                                       start=True, stop=True)
                    mm.then_inc(S["lat_mm"], 1)
                if j == 2 and on_(PROJ):
                    reader_before(i, on_, ("on_ready", TAIL), ("rt2_ready", PROJ - 1))
                    pe.matmul(PS[:, WB, 0:T], wq2[:, 0:P], a1T[:, :], start=True, stop=True)
                    pe.matmul(PS[:, WB, T:2 * T], wq2[:, P // 2:P // 2 + P], a1T[:, :], start=True, stop=True)\
                      .then_inc(S["q_mm"], 1)
                if j == 3 and on_(TAIL):
                    wait(pe, "on_ready", e)
                    reader_before(i, on_, ("laT_ready", PROJ), ("lg_ready", TAIL - 1), ("nT_ready", MAXI - 1))
                    chain_T(e, lambda t: on[:, t, :], TB, P, "onTp")
                if j == 4 and on_(TAIL):
                    wait(pe, "onT_ready", e)
                    for t in range(TB):
                        mm = pe.matmul(PS[:, MB, t * D:(t + 1) * D], onT[:, t * P:(t + 1) * P], wo2[:, :],
                                       start=True, stop=True)
                    mm.then_inc(S["wo_mm"], 1)
                if j == 7 and on_(TAIL):
                    wait(pe, "a2_ready", e)
                    reader_before(i, on_, ("nT_ready", MAXI))
                    chain_T(e, lambda t: a2[e.par][:, t, 0:D], TB, D, "a2Tp")

            def chains_late(i, on_, j):
                s, e = i + PROJ, i + TAIL
                if j == 2 and on_(PROJ):
                    wait(pe, "la_ready", s)
                    apart(pe)
                    chain_T(s, lambda t: la[:, t, :], TB, LAT, "laTp")
                if j == 3 and on_(PROJ):
                    wait(pe, "laT_ready", s)
                    wait(pe, "rt2_ready", s, 1)
                    pe.matmul(PS[:, WB, 0:T], wuk2[:, 0:P], laT[:, :], start=True, stop=True)
                    pe.matmul(PS[:, WB, T:2 * T], wuk2[:, P // 2:P // 2 + P], laT[:, :], start=True, stop=True)\
                      .then_inc(S["k_mm"], 1)
                if j == 6 and on_(PROJ):
                    wait(pe, "v_ready", s + -1)
                    wait(pe, "nextrow_ready", i + ROUTE) if on_(ROUTE) else None
                    for t in range(TB):
                        mm = pe.matmul(PS[:, RB, T + t * P:T + (t + 1) * P], laT[:, t * P:(t + 1) * P], wuv[:, :],
                                       start=True, stop=True)
                    mm.then_inc(S["v_mm"], 1)
                if j == 5 and on_(MAXI):
                    m = i + MAXI
                    wait(pe, "n_ready", m)
                    reader_before(i, on_, ("r_ready", TAIL), ("laT_ready", PROJ), ("nT_ready", MAXI - 1))
                    apart(pe)
                    for t in range(TB):
                        mm = pe.transpose(PS[0:3 * MH, MB, t * P // 2:(t + 1) * P // 2].bitcast(BF16),
                                          nparts[:, t, :, :].rearrange("p a h -> p (a h)"), ident_b[:, :])
                    mm.then_inc(S["nTp"], 1)
                if j == 2 and on_(ROUTE):
                    m = i + ROUTE
                    wait(pe, "pick_ready", m)
                    wait(pe, "nextrow_ready", m + -1)
                    reader_before(i, on_, ("v_ready", PROJ - 1))
                    both = pick[:, :, :].rearrange("p t e -> p (t e)")
                    pe.matmul(PS[:, RB, 0:2 * NE], before[:, :], both, start=True, stop=False)
                    pe.matmul(PS[:, RB, NE:2 * NE], ones[:, :], pick[:, 0, :], start=False, stop=True)
                    pe.matmul(PS[:, RB, 2 * NE:3 * NE], ones[:, :], pick[:, 0, :], start=True, stop=False)
                    pe.matmul(PS[:, RB, 2 * NE:3 * NE], ones[:, :], pick[:, 1, :], start=False, stop=True)\
                      .then_inc(S["place_mm"], 1)

            def body(i, on_):
                for j in range(SLOTS):
                    if on_(PROB):
                        for x in ((0, 1) if j % 2 == 0 else (2,)):
                            scores_for_exp(i + PROB, j // 2, x)
                    for g in MAXIMA[j][:2] if on_(MAXI) else ():
                        scores_for_max(i + MAXI, g)
                    chains(i, on_, j)
                    for g in MAXIMA[j][2:] if on_(MAXI) else ():
                        scores_for_max(i + MAXI, g)
                    if on_(PROB) and j % 2 == 0 and j > 0:
                        values(i + PROB, j // 2 - 1)
                    chains_late(i, on_, j)
                if on_(PROB):
                    values(i + PROB, 3)
                if on_(TAIL):
                    e = i + TAIL
                    wait(pe, "a2T_ready", e)
                    for t in range(TB):
                        mm = pe.matmul(PS[:, MB, t * NE:(t + 1) * NE], a2T[:, t * P:(t + 1) * P], gw[:, :],
                                       start=True, stop=True)
                    mm.then_inc(S["lg_mm"], 1)
            turns(pe, body, *BATCH_TURNS)

            def tile_body(i, on_):
                if on_(ROWS):
                    n = i + ROWS
                    pe.wait_ge(tile_in[n.c % 4], 16 * (n.k + n.c // 4 + 1))
                    wait(pe, "xsT_ready", n + -2)
                    apart(pe)
                    pe.transpose(PS[:, XT[n.par], 0:P], xs[n.c % 4][:, 0:D], ident[:, :]).then_inc(S["xsTp"], 1)
                if on_(OUTPUT):
                    n = i + OUTPUT
                    wait(pe, "hidT_ready", n)
                    wait(pe, "output_set", n)
                    wait(pe, "ys_ready", n + -2)
                    apart(pe)
                    bank = PS[:, YB[n.par], 0:D]
                    pe.matmul(bank, one3[:, :], b2_now[n.par][:, :], start=True, stop=False)
                    for m in range(HT):
                        mm = pe.matmul(bank, hidT[n.par][:, m, :], w2_now[n.par][:, m, :], start=False, stop=(m == HT - 1))
                    mm.then_inc(S["y_mm"], 1)
                if on_(HIDDEN):
                    n = i + HIDDEN
                    wait(pe, "xsT_ready", n)
                    wait(pe, "hidden_set", n)
                    wait(pe, "hidT_ready", n + -2)
                    apart(pe)
                    for m in range(HT):
                        pe.matmul(PS[:, HB[n.par], m * P:(m + 1) * P], b1_now[n.par][:, m * P:(m + 1) * P], one3[:, :],
                                  start=(m == 0), stop=False, skip_group_check=True)
                    for m in range(HT):
                        mm = pe.matmul(PS[:, HB[n.par], m * P:(m + 1) * P], w1_now[n.par][:, m * P:(m + 1) * P],
                                       xsT[n.par][:, :], start=False, stop=True, skip_group_check=True)
                    mm.then_inc(S["hidT_mm"], 1)
            turns(pe, tile_body, *TILE_TURNS)


def build(nc, a, out):
    with ExitStack() as ctx:
        x_res = ctx.enter_context(nc.sbuf_tensor("x_res", [P, B * TB, D], F32))
        ident = ctx.enter_context(nc.sbuf_tensor("ident_sb", [P, P], F32))
        mhalf = ctx.enter_context(nc.sbuf_tensor("mhalf", [P, 16], F32))
        rowmod_dram = nc.dram_tensor("rowmod_dram", (B, 4, D), F32, kind="Internal").ap()
        consts_in = ctx.enter_context(nc.semaphore("consts_in"))
        later = feed_forward_constants(nc, ctx, a)
        linear_attention(nc, a, x_res, ident, mhalf, rowmod_dram, consts_in, later)
        feed_forward(nc, out, x_res, ident, mhalf, rowmod_dram, later)


def kernel(**inputs):
    import numpy as _np
    import concourse.bacc as _bacc
    from concourse.bass_utils import run_bass_kernel_spmd as _run

    g = {k: _np.asarray(v) for k, v in inputs.items()}
    arrays = {
        "x": g["L0_attn_x"], "wq": g["L0_attn_Wq"], "wk": g["L0_attn_Wk"],
        "wvg": _np.concatenate([g["L0_attn_Wv"], g["L0_attn_Wg"]], axis=1),
        "w1t": g["L0_attn_gk_w1"].T, "w2": g["L0_attn_gk_w2"], "gk_b": g["L0_attn_gk_b2"].reshape(-1, 1),
        "gnorm": _np.concatenate([g["L0_attn_g_norm_w"]] * 2).reshape(-1, 1), "wo": g["L0_attn_Wo"],
        "cT": g["L0_c"].T, "wmod": g["L0_wmod"],
    }
    def by_feature(w):
        w = w.reshape(-1, MH, MD).transpose(0, 2, 1).reshape(-1, P)
        return _np.concatenate([w, w[:, :P // 2]], axis=1)

    arrays.update({
        "wq2": by_feature(g["L0_ffn_Wq"].T), "wuk2": by_feature(g["L0_ffn_Wuk"].T), "wdkv": g["L0_ffn_Wdkv"].T,
        "wuv": g["L0_ffn_Wuv"].T, "wo2": g["L0_ffn_Wo"].T, "n1w": g["L0_ffn_norm1_w"].reshape(-1, 1),
        "n2w": g["L0_ffn_norm2_w"].reshape(-1, 1), "lng": g["L0_ffn_ln_g"].reshape(-1, 1),
        "lnb": g["L0_ffn_ln_b"].reshape(-1, 1), "gw": g["L0_ffn_gate_w"].T, "gate_b": g["L0_ffn_gate_b"].reshape(1, -1),
        "w1": g["L0_ffn_W1"].transpose(2, 0, 1).reshape(D, NE * HID),
        "bias": _np.concatenate([g["L0_ffn_b1"].reshape(1, -1), g["L0_ffn_b2"].reshape(1, -1)], axis=1),
        "w2e": g["L0_ffn_W2"].transpose(0, 2, 1).reshape(NE * HID, D),
    })
    arrays.update(shape_constants())
    arrays = {f"in_{k}": _np.ascontiguousarray(v) for k, v in arrays.items()}
    nc = _bacc.Bacc("TRN2", target_bir_lowering=False, num_devices=1)
    aps = {k[3:]: nc.dram_tensor(k, v.shape, mybir.dt.from_np(v.dtype), kind="ExternalInput").ap()
           for k, v in arrays.items()}
    out = nc.dram_tensor("out", g["L0_attn_x"].shape, F32, kind="ExternalOutput").ap()
    build(nc, aps, out)
    r = _run(nc, [arrays], core_ids=[0])
    return r.results[0]["out"]
```
